# Optimizing a Trainium2 kernel written in Bass

```python
import numpy as np
import jax
import jax.numpy as jnp

def _softmax(x, axis=-1):
    return jax.nn.softmax(x, axis=axis)

def _gelu(x):
    return jax.nn.gelu(x, approximate=True)

def _silu(x):
    return jax.nn.silu(x)

def _sigmoid(x):
    return jax.nn.sigmoid(x)

def _layernorm(x, axis=-1, eps=1e-05):
    m = jnp.mean(x, axis=axis, keepdims=True)
    v = jnp.var(x, axis=axis, keepdims=True)
    return (x - m) / jnp.sqrt(v + eps)

def _scatter_add(tgt, idx, src, axis=0):
    return tgt.at[idx].add(src)

def _segment_sum(src, seg, n):
    return jax.ops.segment_sum(src, seg, n)
kernel_name = 'mk_gnn_ffn_d2_gnn_r32_aa6036'

def setup_inputs(seed: int=0):
    np.random.seed(seed)
    _w = jnp.asarray

    def _rec_inputs():
        import jax
        import jax.numpy as jnp
        _gk = jax.random.key(seed)
        x = -0.0003713 + 1 * jax.random.normal(jax.random.fold_in(_gk, 1), (3125, 256), jnp.float32)
        src = jax.random.randint(jax.random.fold_in(_gk, 2), (50000,), 0, 3125, jnp.int32)
        dst = jax.random.randint(jax.random.fold_in(_gk, 3), (50000,), 0, 3125, jnp.int32)
        _o = jnp.argsort(dst, stable=True)
        src = src[_o]
        dst = dst[_o]
        edge_weight = jax.random.uniform(jax.random.fold_in(_gk, 12), (50000,), jnp.float32, 0.0, 0.999996)
        return (x, src, dst, edge_weight)
    x, src, dst, edge_weight = _rec_inputs()

    def _L0_gnn_setup():
        import jax, jax.numpy as jnp
        import numpy as np
        N, E, L, C, D = (50000, 12500, 3, 4, 64)
        IN_DIM = C * D
        key = jax.random.key(seed)
        ks = jax.random.split(key, 10)
        return {'features': jax.random.normal(ks[0], (N, IN_DIM), dtype=jnp.float32), 'src': jax.random.randint(ks[1], (E,), 0, N, dtype=jnp.int32), 'dst': jax.random.randint(ks[2], (E,), 0, N, dtype=jnp.int32), 'edge_w': jax.random.uniform(ks[3], (E,), dtype=jnp.float32), 'fc_w': jax.random.normal(ks[4], (L, IN_DIM, IN_DIM), dtype=jnp.float32) * 0.05, 'fc_b': jax.random.normal(ks[5], (L, IN_DIM), dtype=jnp.float32) * 0.05, 'ch_w': jax.random.normal(ks[6], (L, C, D, D), dtype=jnp.float32) * 0.1, 'ch_b': jax.random.normal(ks[7], (L, C, D), dtype=jnp.float32) * 0.1, 'mlp_w': jax.random.normal(ks[8], (IN_DIM, L * IN_DIM), dtype=jnp.float32) * 0.05, 'mlp_b': jax.random.normal(ks[9], (IN_DIM,), dtype=jnp.float32) * 0.05}
    _L0_gnn_all = _L0_gnn_setup()
    _L0_gnn_in = {k: v for k, v in _L0_gnn_all.items() if k in ('fc_w', 'fc_b', 'ch_w', 'ch_b', 'mlp_w', 'mlp_b')}
    del _L0_gnn_all

    def _L0_ffn_setup():
        import jax, jax.numpy as jnp
        import numpy as np
        E = 8
        K = 2
        D = 256
        H = 512
        DOUT = 256
        EPS = 1e-05
        key = jax.random.key(seed)
        ks = jax.random.split(key, 9)
        s = 0.02
        return {'x': jax.random.normal(ks[0], (4, 256, D), jnp.float32), 'gamma': 1.0 + 0.05 * jax.random.normal(ks[1], (D,), jnp.float32), 'beta': 0.05 * jax.random.normal(ks[2], (D,), jnp.float32), 'Wr': 0.01 * jax.random.normal(ks[3], (D, E), jnp.float32), 'br': jnp.zeros((E,), jnp.float32), 'W1': s * jax.random.normal(ks[4], (E, D, H), jnp.float32), 'b1': s * jax.random.normal(ks[5], (E, H), jnp.float32), 'W2': s * jax.random.normal(ks[6], (E, H, DOUT), jnp.float32), 'b2': s * jax.random.normal(ks[7], (E, DOUT), jnp.float32)}
    _L0_ffn_all = _L0_ffn_setup()
    _L0_ffn_in = {k: v for k, v in _L0_ffn_all.items() if k in ('gamma', 'beta', 'Wr', 'br', 'W1', 'b1', 'W2', 'b2')}
    del _L0_ffn_all

    def _L1_gnn_setup():
        import jax, jax.numpy as jnp
        import numpy as np
        V = 50000
        E = 18750
        D = 256
        K = 20
        OUT = 256

        def layer_norm(x, g, b, eps=1e-05):
            mu = jnp.mean(x, axis=-1, keepdims=True)
            var = jnp.var(x, axis=-1, keepdims=True)
            return (x - mu) * jax.lax.rsqrt(var + eps) * g + b
        key = jax.random.key(seed)
        ks = jax.random.split(key, 12)

        def rn(k, shape, s=0.05):
            return jax.random.normal(k, shape, dtype=jnp.float32) * s
        return dict(node_feats=jax.random.normal(ks[0], (V, D), dtype=jnp.float32), src=jax.random.randint(ks[1], (E,), 0, V), dst=jax.random.randint(ks[2], (E,), 0, V), Wp=rn(ks[3], (D, K)), bp=jnp.zeros((K,), jnp.float32), gp=jnp.ones((K,), jnp.float32), betap=jnp.zeros((K,), jnp.float32), Wk=rn(ks[4], (K * K, OUT)), bk=jnp.zeros((OUT,), jnp.float32), gk=jnp.ones((OUT,), jnp.float32), betak=jnp.zeros((OUT,), jnp.float32), We=rn(ks[5], (2 * D, 1)), be=jnp.zeros((1,), jnp.float32), Wn=rn(ks[6], (D, D)), bn=jnp.zeros((D,), jnp.float32), W_ih=rn(ks[7], (3 * D, D)), W_hh=rn(ks[8], (3 * D, D)), b_ih=jnp.zeros((3 * D,), jnp.float32), b_hh=jnp.zeros((3 * D,), jnp.float32), g_ln=jnp.ones((D,), jnp.float32), beta_ln=jnp.zeros((D,), jnp.float32), Wc=rn(ks[9], (D + OUT, D)), bc=jnp.zeros((D,), jnp.float32), gc=jnp.ones((D,), jnp.float32), betac=jnp.zeros((D,), jnp.float32))
    _L1_gnn_all = _L1_gnn_setup()
    _L1_gnn_in = {k: v for k, v in _L1_gnn_all.items() if k in ('Wp', 'bp', 'gp', 'betap', 'Wk', 'bk', 'gk', 'betak', 'We', 'be', 'Wn', 'bn', 'W_ih', 'W_hh', 'b_ih', 'b_hh', 'g_ln', 'beta_ln', 'Wc', 'bc', 'gc', 'betac')}
    del _L1_gnn_all

    def _L1_ffn_setup():
        import jax, jax.numpy as jnp
        import numpy as np
        B, S, D = (8, 128, 256)
        H = 4 * D
        CAPACITY = 0.5
        key = jax.random.key(seed)
        ks = jax.random.split(key, 6)
        x = jax.random.normal(ks[0], (B, S, D), dtype=jnp.float32)
        attention_mask = jnp.zeros((B, 1, 1, S), dtype=jnp.float32)
        wr = jax.random.normal(ks[1], (D, 1), dtype=jnp.float32) * 0.02
        br = jnp.zeros((1,), dtype=jnp.float32)
        w1 = jax.random.normal(ks[2], (D, H), dtype=jnp.float32) * 0.02
        b1 = jnp.zeros((H,), dtype=jnp.float32)
        w2 = jax.random.normal(ks[3], (H, D), dtype=jnp.float32) * 0.02
        b2 = jnp.zeros((D,), dtype=jnp.float32)
        return {'x': x, 'attention_mask': attention_mask, 'wr': wr, 'br': br, 'w1': w1, 'b1': b1, 'w2': w2, 'b2': b2}
    _L1_ffn_all = _L1_ffn_setup()
    _L1_ffn_in = {k: v for k, v in _L1_ffn_all.items() if k in ('attention_mask', 'wr', 'br', 'w1', 'b1', 'w2', 'b2')}
    del _L1_ffn_all
    return {'x': x, 'src': src, 'dst': dst, 'edge_weight': edge_weight, 'L0_gnn_fc_w': _L0_gnn_in['fc_w'], 'L0_gnn_fc_b': _L0_gnn_in['fc_b'], 'L0_gnn_ch_w': _L0_gnn_in['ch_w'], 'L0_gnn_ch_b': _L0_gnn_in['ch_b'], 'L0_gnn_mlp_w': _L0_gnn_in['mlp_w'], 'L0_gnn_mlp_b': _L0_gnn_in['mlp_b'], 'L0_ffn_gamma': _L0_ffn_in['gamma'], 'L0_ffn_beta': _L0_ffn_in['beta'], 'L0_ffn_Wr': _L0_ffn_in['Wr'], 'L0_ffn_br': _L0_ffn_in['br'], 'L0_ffn_W1': _L0_ffn_in['W1'], 'L0_ffn_b1': _L0_ffn_in['b1'], 'L0_ffn_W2': _L0_ffn_in['W2'], 'L0_ffn_b2': _L0_ffn_in['b2'], 'L1_gnn_Wp': _L1_gnn_in['Wp'], 'L1_gnn_bp': _L1_gnn_in['bp'], 'L1_gnn_gp': _L1_gnn_in['gp'], 'L1_gnn_betap': _L1_gnn_in['betap'], 'L1_gnn_Wk': _L1_gnn_in['Wk'], 'L1_gnn_bk': _L1_gnn_in['bk'], 'L1_gnn_gk': _L1_gnn_in['gk'], 'L1_gnn_betak': _L1_gnn_in['betak'], 'L1_gnn_We': _L1_gnn_in['We'], 'L1_gnn_be': _L1_gnn_in['be'], 'L1_gnn_Wn': _L1_gnn_in['Wn'], 'L1_gnn_bn': _L1_gnn_in['bn'], 'L1_gnn_W_ih': _L1_gnn_in['W_ih'], 'L1_gnn_W_hh': _L1_gnn_in['W_hh'], 'L1_gnn_b_ih': _L1_gnn_in['b_ih'], 'L1_gnn_b_hh': _L1_gnn_in['b_hh'], 'L1_gnn_g_ln': _L1_gnn_in['g_ln'], 'L1_gnn_beta_ln': _L1_gnn_in['beta_ln'], 'L1_gnn_Wc': _L1_gnn_in['Wc'], 'L1_gnn_bc': _L1_gnn_in['bc'], 'L1_gnn_gc': _L1_gnn_in['gc'], 'L1_gnn_betac': _L1_gnn_in['betac'], 'L1_ffn_attention_mask': _L1_ffn_in['attention_mask'], 'L1_ffn_wr': _L1_ffn_in['wr'], 'L1_ffn_br': _L1_ffn_in['br'], 'L1_ffn_w1': _L1_ffn_in['w1'], 'L1_ffn_b1': _L1_ffn_in['b1'], 'L1_ffn_w2': _L1_ffn_in['w2'], 'L1_ffn_b2': _L1_ffn_in['b2']}

def reference(x, src, dst, edge_weight, L0_gnn_fc_w, L0_gnn_fc_b, L0_gnn_ch_w, L0_gnn_ch_b, L0_gnn_mlp_w, L0_gnn_mlp_b, L0_ffn_gamma, L0_ffn_beta, L0_ffn_Wr, L0_ffn_br, L0_ffn_W1, L0_ffn_b1, L0_ffn_W2, L0_ffn_b2, L1_gnn_Wp, L1_gnn_bp, L1_gnn_gp, L1_gnn_betap, L1_gnn_Wk, L1_gnn_bk, L1_gnn_gk, L1_gnn_betak, L1_gnn_We, L1_gnn_be, L1_gnn_Wn, L1_gnn_bn, L1_gnn_W_ih, L1_gnn_W_hh, L1_gnn_b_ih, L1_gnn_b_hh, L1_gnn_g_ln, L1_gnn_beta_ln, L1_gnn_Wc, L1_gnn_bc, L1_gnn_gc, L1_gnn_betac, L1_ffn_attention_mask, L1_ffn_wr, L1_ffn_br, L1_ffn_w1, L1_ffn_b1, L1_ffn_w2, L1_ffn_b2):
    import jax
    import jax.numpy as jnp

    def _L0_gnn_ref(features, src, dst, edge_w, fc_w, fc_b, ch_w, ch_b, mlp_w, mlp_b):
        import jax, jax.numpy as jnp
        import numpy as np
        N, E, L, C, D = (50000, 12500, 3, 4, 64)
        IN_DIM = C * D
        n = features.shape[0]
        ones = jnp.ones_like(edge_w)
        deg_out = jnp.maximum(jax.ops.segment_sum(ones, src, num_segments=n), 1.0)
        deg_in = jnp.maximum(jax.ops.segment_sum(ones, dst, num_segments=n), 1.0)
        norm_out = (deg_out ** (-0.5))[:, None, None]
        norm_in = (deg_in ** (-0.5))[:, None, None]
        x = features
        outs = []
        for l in range(L):
            h = x @ fc_w[l].T + fc_b[l]
            f = h.reshape(n, C, D) * norm_out
            f = jnp.einsum('ncd,cde->nce', f, ch_w[l])
            m = f[src] * edge_w[:, None, None]
            agg = jax.ops.segment_sum(m, dst, num_segments=n)
            r = agg * norm_in + ch_b[l]
            r = jax.nn.relu(r)
            x = r.reshape(n, C * D)
            outs.append(x)
        hcat = jnp.concatenate(outs, axis=-1)
        return hcat @ mlp_w.T + mlp_b

    def _L0_ffn_ref(x, gamma, beta, Wr, br, W1, b1, W2, b2):
        import jax, jax.numpy as jnp
        import numpy as np
        E = 8
        K = 2
        D = 256
        H = 512
        DOUT = 256
        EPS = 1e-05
        mu = jnp.mean(x, axis=-1, keepdims=True)
        var = jnp.mean(jnp.square(x - mu), axis=-1, keepdims=True)
        xn = (x - mu) * jax.lax.rsqrt(var + EPS) * gamma + beta
        logits = jnp.einsum('bsd,de->bse', xn, Wr) + br
        top_vals, top_idx = jax.lax.top_k(logits, K)
        w = jax.nn.softmax(top_vals, axis=-1)
        w_full = jnp.einsum('bsk,bske->bse', w, jax.nn.one_hot(top_idx, E, dtype=w.dtype))
        y = jnp.zeros(x.shape[:-1] + (DOUT,), x.dtype)
        for e in range(E):
            h = jax.nn.gelu(jnp.einsum('bsd,dh->bsh', xn, W1[e]) + b1[e], approximate=False)
            y_e = jnp.einsum('bsh,hd->bsd', h, W2[e]) + b2[e]
            y = y + y_e * w_full[..., e, None]
        return y

    def _L1_gnn_ref(node_feats, src, dst, Wp, bp, gp, betap, Wk, bk, gk, betak, We, be, Wn, bn, W_ih, W_hh, b_ih, b_hh, g_ln, beta_ln, Wc, bc, gc, betac):
        import jax, jax.numpy as jnp
        import numpy as np
        V = 50000
        E = 18750
        D = 256
        K = 20
        OUT = 256

        def layer_norm(x, g, b, eps=1e-05):
            mu = jnp.mean(x, axis=-1, keepdims=True)
            var = jnp.var(x, axis=-1, keepdims=True)
            return (x - mu) * jax.lax.rsqrt(var + eps) * g + b
        Vn = node_feats.shape[0]
        En = src.shape[0]
        npj = jax.nn.relu(layer_norm(node_feats @ Wp + bp, gp, betap))
        kron = jnp.einsum('ea,ek->eak', npj[src], npj[dst]).reshape(En, -1)
        kron = jax.nn.relu(layer_norm(kron @ Wk + bk, gk, betak))
        kron_feat = jax.ops.segment_sum(kron, dst, num_segments=Vn)
        he = jnp.concatenate([node_feats[dst], node_feats[src]], axis=1)
        logits = jax.nn.relu(he @ We + be)
        m = jax.ops.segment_max(logits, dst, num_segments=Vn)
        ex = jnp.exp(logits - m[dst])
        denom = jax.ops.segment_sum(ex, dst, num_segments=Vn)
        a = ex / denom[dst]
        hv = node_feats @ Wn + bn
        context = jax.nn.relu(jax.ops.segment_sum(hv[src] * a, dst, num_segments=Vn))
        gi = context @ W_ih.T + b_ih
        gh = node_feats @ W_hh.T + b_hh
        i_r, i_z, i_n = jnp.split(gi, 3, axis=1)
        h_r, h_z, h_n = jnp.split(gh, 3, axis=1)
        r = jax.nn.sigmoid(i_r + h_r)
        z = jax.nn.sigmoid(i_z + h_z)
        n = jnp.tanh(i_n + r * h_n)
        h = (1.0 - z) * n + z * node_feats
        gru_out = layer_norm(jax.nn.relu(h), g_ln, beta_ln)
        cat = jnp.concatenate([gru_out, kron_feat], axis=1)
        return jax.nn.relu(layer_norm(cat @ Wc + bc, gc, betac))

    def _L1_ffn_ref(x, attention_mask, wr, br, w1, b1, w2, b2):
        import jax, jax.numpy as jnp
        import numpy as np
        B, S, D = (8, 128, 256)
        H = 4 * D
        CAPACITY = 0.5
        b, s, d = x.shape
        weights = (jnp.einsum('bsd,do->bso', x, wr) + br)[..., 0]
        k = max(1, int(CAPACITY * s))
        kk = k - 1 if k > 1 else 1
        _, idx = jax.lax.top_k(weights, k)
        sel_idx = idx[:, :kk]
        sel = jnp.take_along_axis(x, sel_idx[:, :, None], axis=1)
        h = jax.nn.gelu(jnp.einsum('bkd,dh->bkh', sel, w1) + b1)
        y = jnp.einsum('bkh,hd->bkd', h, w2) + b2
        w_sel = jnp.take_along_axis(weights, sel_idx, axis=1)
        y = y * w_sel[..., None]
        batch_idx = jnp.arange(b)[:, None]
        processed = jnp.zeros_like(x).at[batch_idx, sel_idx].set(y)
        return processed + x
    x = x + _L0_gnn_ref(_layernorm(x, axis=-1), src, dst, edge_weight, L0_gnn_fc_w, L0_gnn_fc_b, L0_gnn_ch_w, L0_gnn_ch_b, L0_gnn_mlp_w, L0_gnn_mlp_b)
    x = x + _L0_ffn_ref(_layernorm(x, axis=-1)[None], L0_ffn_gamma, L0_ffn_beta, L0_ffn_Wr, L0_ffn_br, L0_ffn_W1, L0_ffn_b1, L0_ffn_W2, L0_ffn_b2)[0]
    x = x + _L1_gnn_ref(_layernorm(x, axis=-1), src, dst, L1_gnn_Wp, L1_gnn_bp, L1_gnn_gp, L1_gnn_betap, L1_gnn_Wk, L1_gnn_bk, L1_gnn_gk, L1_gnn_betak, L1_gnn_We, L1_gnn_be, L1_gnn_Wn, L1_gnn_bn, L1_gnn_W_ih, L1_gnn_W_hh, L1_gnn_b_ih, L1_gnn_b_hh, L1_gnn_g_ln, L1_gnn_beta_ln, L1_gnn_Wc, L1_gnn_bc, L1_gnn_gc, L1_gnn_betac)
    x = x + _L1_ffn_ref(_layernorm(x, axis=-1)[None], L1_ffn_attention_mask, L1_ffn_wr, L1_ffn_br, L1_ffn_w1, L1_ffn_b1, L1_ffn_w2, L1_ffn_b2)[0]
    return x

_drawn_inputs = setup_inputs


def setup_inputs(seed=0):
    import zlib

    import numpy as np

    out = dict(_drawn_inputs(seed))
    spreads = {'L0_ffn_br': (0.0, 0.1),
     'L1_gnn_bp': (0.0, 0.1),
     'L1_gnn_gp': (1.0, 0.2),
     'L1_gnn_betap': (0.0, 0.1),
     'L1_gnn_bk': (0.0, 0.1),
     'L1_gnn_gk': (1.0, 0.2),
     'L1_gnn_betak': (0.0, 0.1),
     'L1_gnn_bn': (0.0, 0.8),
     'L1_gnn_b_ih': (0.0, 0.8),
     'L1_gnn_b_hh': (0.0, 0.8),
     'L1_gnn_g_ln': (1.0, 0.6),
     'L1_gnn_beta_ln': (0.0, 0.8),
     'L1_gnn_bc': (0.0, 0.8),
     'L1_gnn_gc': (1.0, 0.2),
     'L1_gnn_betac': (0.0, 0.1),
     'L1_ffn_b1': (0.0, 0.8),
     'L1_ffn_b2': (0.0, 0.8)}
    factors = {'L0_ffn_gamma': 6.011,
     'L0_ffn_beta': 4.79,
     'L0_ffn_b1': 8.0,
     'L0_ffn_b2': 4.269,
     'L1_gnn_We': 8.0,
     'L1_gnn_Wn': 5.166,
     'L1_gnn_W_ih': 4.366,
     'L1_ffn_wr': 4.461,
     'L1_ffn_w1': 6.567,
     'L1_ffn_w2': 6.167}
    for name, (base, spread) in spreads.items():
        noise = np.random.default_rng([zlib.crc32(name.encode()), seed]).standard_normal(out[name].shape)
        drawn = base * np.exp(spread * noise) if base else spread * noise
        out[name] = jnp.asarray(drawn.astype(out[name].dtype))
    for name, factor in factors.items():
        out[name] = (out[name] * factor).astype(out[name].dtype)
    return out
```

```python
from contextlib import ExitStack

import concourse.bass as bass
import numpy as np
from concourse import mybir

F32 = mybir.dt.float32
BF16 = mybir.dt.bfloat16
I32 = mybir.dt.int32
ALU = mybir.AluOpType
ACT = mybir.ActivationFunctionType
AX = mybir.AxisListType

P = 128
N, D, E = 3125, 256, 50000
KC = D // P
NT = -(-N // P)
NP = NT * P
ET = 392
EP = ET * P
IG = 4
NI = 416
IP = NI // IG
L = 3
C, DH = 4, 64
NE, H = 8, 512
KD = 20
KCH = 101
EPS = 1e-5
U = 8
UT = 4
assert NI >= ET + NT - 1 and NI % U == 0 and NI == IG * IP


USED = []


def clear_semaphores(nc):
    nc.clear_and_free_semaphores(list(USED))
    USED.clear()
    nc.all_engine_barrier()


class Phase:

    def __init__(self, nc, name):
        self.nc, self.name = nc, name

    def __enter__(self):
        self.stack = ExitStack()
        return self

    def __exit__(self, *exc):
        return self.stack.__exit__(*exc)

    def sb(self, name, shape, dt=F32):
        return self.stack.enter_context(self.nc.sbuf_tensor(f"{self.name}_{name}", shape, dt))

    def ps(self, name, shape=(P, 512)):
        return self.stack.enter_context(self.nc.psum_tensor(f"{self.name}_{name}", list(shape), F32))

    def sem(self, name):
        handle = self.nc.alloc_semaphore(f"{self.name}_{name}")
        USED.append(handle)
        return handle

    def block(self):
        return self.stack.enter_context(self.nc.Block())


def wait(eng, sem, value):
    if not (isinstance(value, int) and value <= 0):
        eng.wait_ge(sem, value)


class Steps:

    def __init__(self, eng, sem):
        self.eng, self.sem, self.n = eng, sem, 0

    def __call__(self, instruction):
        self.n += 1
        instruction.then_inc(self.sem, 1)
        return self

    def done(self):
        self.eng.wait_ge(self.sem, self.n)


def pipeline(eng, stages, count, unroll):
    last = max(lag for _, lag in stages)
    peeled, blocks = 1 + -(-last // unroll), count // unroll

    def tick(block, u):
        for body, lag in stages:
            over, slot = divmod(u - lag, unroll)
            if not isinstance(block, int):
                body(block * unroll + (u - lag), block + over if over else block, slot)
            elif 0 <= (block + over) * unroll + slot < count:
                body((block + over) * unroll + slot, block + over, slot)

    looped = blocks > peeled
    for n in range(peeled * unroll if looped else count + last):
        tick(n // unroll, n % unroll)
    if not looped:
        return
    with eng.Fori(peeled, blocks) as b:
        for u in range(unroll):
            tick(b, u)
    for n in range(blocks * unroll, count + last):
        tick(n // unroll, n % unroll)


def each(eng, body, count, unroll):
    pipeline(eng, [(body, 0)], count, unroll)


def at(i):
    return bass.ds(i, 1)


def tile_of(t, i, width=None):
    return t[:, at(i), 0:width or t.shape[2]].rearrange("p a d -> p (a d)")


def stat(mean_rstd, t, n):
    return mean_rstd[:, at(t), n:n + 1].rearrange("p a b -> p (a b)")


def bcast(vector, rows):
    return vector.rearrange("(a n) -> a n", a=1).to_broadcast((rows, vector.shape[0]))


def constants(nc, top):
    k = {}
    k["ident"] = top.sb("ident", [P, P])
    k["iota"] = top.sb("iota", [P, P])
    k["ones"] = top.sb("ones", [P, P])
    k["eps"] = top.sb("eps", [P, 1])
    with Phase(nc, "const") as ph:
        made, ready = ph.sem("made"), ph.sem("ready")
        block = ph.block()

        @block.gpsimd
        def _(pool):
            pool.memset(k["ident"][:, :], 0.0).then_inc(made, 1)
            pool.memset(k["ones"][:, :], 1.0).then_inc(ready, 1)
            pool.memset(k["eps"][:, :], EPS).then_inc(ready, 1)
            pool.iota(k["iota"][:, :], pattern=[[1, P]], base=0, channel_multiplier=0,
                      allow_small_or_imprecise_dtypes=True).then_inc(ready, 1)
            pool.wait_ge(made, 1)
            pool.affine_select(out=k["ident"][:, :], in_=k["ident"][:, :], compare_op=ALU.not_equal, fill=1.0,
                               base=0, pattern=[[-1, P]], channel_multiplier=1).then_inc(ready, 1)
            pool.wait_ge(ready, 4)
    return k


def order_edges(nc, t, k, edges):
    with Phase(nc, "order") as ph:
        cols = EP // P
        dst_i = ph.sb("dst_i", [P, cols], I32)
        dst_f = ph.sb("dst_f", [P, cols])
        nxt_i = ph.sb("nxt_i", [P, cols], I32)
        nxt_f = ph.sb("nxt_f", [P, cols])
        src_i = ph.sb("src_i", [P, cols], I32)
        wgt = ph.sb("wgt", [P, cols])
        fall = ph.sb("fall", [P, cols])
        falls = ph.sb("falls", [P, 1])
        unordered = ph.sb("unordered", [P, 1], I32)
        bin_i = ph.sb("bin_i", [P, cols], I32)
        bin_f = ph.sb("bin_f", [P, cols])
        mask = ph.sb("mask", [P, cols])
        rank = ph.sb("rank", [P, cols])
        none = ph.sb("none", [P, cols])
        place = ph.sb("place", [P, cols])
        place_i = ph.sb("place_i", [P, cols], I32)
        count = ph.sb("count", [P, NT])
        total = ph.sb("total", [P, NT])
        start = ph.sb("start", [P, NT])
        zero = ph.sb("zero", [P, NT])
        below = ph.sb("below", [P, P])
        slot = ph.sb("slot", [P, 1], I32)
        one_s = ph.sb("one_s", [P, 1], I32)
        one_d = ph.sb("one_d", [P, 1], I32)
        one_w = ph.sb("one_w", [P, 1])
        tot_ps = ph.ps("tot_ps")
        pre_ps = ph.ps("pre_ps")
        flag_ps = ph.ps("flag_ps")

        loaded, own, pool_own = ph.sem("loaded"), ph.sem("own"), ph.sem("pool_own")
        below_ready, falls_ready, flag_sum = ph.sem("below_ready"), ph.sem("falls_ready"), ph.sem("flag_sum")
        flag_ready, counts_ready, prefix = ph.sem("flag_ready"), ph.sem("counts_ready"), ph.sem("prefix")
        place_ready, slot_ready = ph.sem("place_ready"), ph.sem("slot_ready")
        copied, stored, issued = ph.sem("copied"), ph.sem("stored"), ph.sem("issued")
        block = ph.block()

        rows = lambda a: a.rearrange("(p c) -> p c", p=P)

        @block.sync
        def _(sp):
            sp.dma_start(dst_i[:, :], rows(t["dst"])).then_inc(loaded, 16)
            sp.dma_start(nxt_i[0:P - 1, :], t["dst"][1:1 + (P - 1) * cols].rearrange("(p c) -> p c", c=cols)
                         ).then_inc(loaded, 16)
            sp.dma_start(nxt_i[P - 1:P, 0:cols - 1],
                         t["dst"][1 + (P - 1) * cols:EP].rearrange("(a c) -> a c", a=1)).then_inc(loaded, 16)
            sp.dma_start(nxt_i[P - 1:P, cols - 1:cols],
                         t["dst"][EP - 1:EP].rearrange("(a c) -> a c", a=1)).then_inc(loaded, 16)
            sp.dma_start(src_i[:, :], rows(t["src"])).then_inc(loaded, 16)
            sp.dma_start(wgt[:, :], rows(t["weight"])).then_inc(loaded, 16)
            sp.wait_ge(flag_ready, 1)
            flag = sp.value_load(unordered[0:1, 0:1], min_val=0, max_val=EP)
            with sp.If(flag < 1):
                sp.dma_start(rows(edges["src"]), rows(t["src"])).then_inc(copied, 16)
                sp.dma_start(rows(edges["dst"]), rows(t["dst"])).then_inc(copied, 16)
                sp.dma_start(rows(edges["weight"]), rows(t["weight"])).then_inc(copied, 16)
                sp.wait_ge(copied, 48)
            with sp.Else():
                sp.nop()

        @block.vector
        def _(dve):
            step = Steps(dve, own)
            step(dve.memset(none[:, :], 0.0))
            step(dve.memset(place[:, :], 0.0))
            step(dve.memset(zero[:, :], 0.0))
            dve.wait_ge(loaded, 96)
            step(dve.tensor_copy(dst_f[:, :], dst_i[:, :]))
            step(dve.tensor_copy(nxt_f[:, :], nxt_i[:, :]))
            step(dve.tensor_scalar(bin_i[:, :], dst_i[:, :], 7, None, ALU.arith_shift_right))
            step.done()
            step(dve.tensor_tensor(fall[:, :], nxt_f[:, :], dst_f[:, :], ALU.is_lt))
            step(dve.tensor_copy(bin_f[:, :], bin_i[:, :]))
            step.done()
            dve.tensor_reduce(falls[:, :], fall[:, :], AX.X, ALU.add).then_inc(falls_ready, 1)
            for b in range(NT):
                step(dve.tensor_scalar(mask[:, :], bin_f[:, :], float(b), None, ALU.is_equal))
                step.done()
                step(dve.tensor_reduce(count[:, b:b + 1], mask[:, :], AX.X, ALU.add))
                step.done()
            dve.sem_inc(counts_ready, 1)
            dve.wait_ge(prefix, 2)
            step(dve.tensor_copy(total[:, :], tot_ps[:, 0:NT]))
            step.done()
            step(dve.tensor_tensor_scan(start[:, :], total[:, :], zero[:, :], 0.0, ALU.add, ALU.add))
            step.done()
            step(dve.tensor_tensor(start[:, :], start[:, :], total[:, :], ALU.subtract))
            step.done()
            step(dve.tensor_tensor(start[:, :], start[:, :], pre_ps[:, 0:NT], ALU.add))
            dve.wait_ge(flag_sum, 1)
            dve.tensor_copy(unordered[:, :], flag_ps[:, 0:1]).then_inc(flag_ready, 1)
            step.done()
            dve.wait_ge(flag_ready, 1)
            flag = dve.value_load(unordered[0:1, 0:1], min_val=0, max_val=EP)
            with dve.If(flag < 1):
                dve.nop()
            with dve.Else():
                for b in range(NT):
                    step(dve.tensor_scalar(mask[:, :], bin_f[:, :], float(b), None, ALU.is_equal))
                    step.done()
                    step(dve.tensor_tensor_scan(rank[:, :], mask[:, :], none[:, :], 0.0, ALU.add, ALU.add))
                    step.done()
                    step(dve.tensor_scalar(rank[:, :], rank[:, :], start[:, b:b + 1], -1.0, ALU.add, ALU.add))
                    step.done()
                    step(dve.tensor_tensor(rank[:, :], rank[:, :], mask[:, :], ALU.mult))
                    step.done()
                    step(dve.tensor_tensor(place[:, :], place[:, :], rank[:, :], ALU.add))
                    step.done()
                dve.tensor_copy(place_i[:, :], place[:, :]).then_inc(place_ready, 1)

        @block.tensor
        def _(pe):
            pe.wait_ge(falls_ready, 1)
            pe.matmul(flag_ps[:, 0:1], k["ones"][:, :], falls[:, :], start=True, stop=True).then_inc(flag_sum, 1)
            pe.wait_ge(counts_ready, 1)
            pe.wait_ge(below_ready, 1)
            pe.matmul(tot_ps[:, 0:NT], k["ones"][:, :], count[:, :], start=True, stop=True).then_inc(prefix, 1)
            pe.matmul(pre_ps[:, 0:NT], below[:, :], count[:, :], start=True, stop=True).then_inc(prefix, 1)

        @block.gpsimd
        def _(pool):
            pool.affine_select(out=below[:, :], in_=k["ones"][:, :], compare_op=ALU.is_ge, fill=0.0,
                               base=-1, pattern=[[1, P]], channel_multiplier=-1).then_inc(below_ready, 1)
            pool.wait_ge(flag_ready, 1)
            flag = pool.value_load(unordered[0:1, 0:1], min_val=0, max_val=EP)
            with pool.If(flag < 1):
                pool.nop()
            with pool.Else():
                pool.wait_ge(place_ready, 1)
                pool.wait_ge(loaded, 96)
                with pool.Fori(0, cols) as c:
                    pool.tensor_copy(slot[:, :], place_i[:, at(c)]).then_inc(slot_ready, 1)
                    pool.tensor_copy(one_s[:, :], src_i[:, at(c)]).then_inc(slot_ready, 1)
                    pool.tensor_copy(one_d[:, :], dst_i[:, at(c)]).then_inc(slot_ready, 1)
                    pool.tensor_copy(one_w[:, :], wgt[:, at(c)]).then_inc(slot_ready, 1)
                    pool.wait_ge(slot_ready, (c + 1) * 4)
                    pool.sem_inc(issued, 1)
                    for name, one in (("src", one_s), ("dst", one_d), ("weight", one_w)):
                        pool.indirect_dma_start(
                            out=edges[name].rearrange("(e a) -> e a", a=1),
                            out_offset=bass.IndirectOffsetOnAxis(ap=slot[:, :], axis=0),
                            in_=one[:, :], in_offset=None).then_inc(stored, 16)
                    pool.wait_ge(stored, (c + 1) * 48)


def degrees_and_items(nc, t, k, edges, g, tile_row):
    with Phase(nc, "items") as ph:
        cols = EP // P
        B = 14
        assert cols % B == 0
        raw = {n: ph.sb(f"{n}_raw", [P, cols], I32) for n in ("src", "dst")}
        part_i = ph.sb("part_i", [P, cols], I32)
        lo = {n: ph.sb(f"{n}_lo", [P, cols]) for n in ("src", "dst")}
        hi = {n: ph.sb(f"{n}_hi", [P, cols]) for n in ("src", "dst")}
        hot_lo = ph.sb("hot_lo", [P, 2, B, P], BF16)
        hot_hi = ph.sb("hot_hi", [P, 2, B, NT], BF16)
        deg = {n: ph.sb(f"{n}_deg", [P, NT]) for n in ("src", "dst")}
        root = {n: ph.sb(f"{n}_root", [P, NT]) for n in ("src", "dst")}
        deg_ps = {n: ph.ps(f"{n}_deg_ps") for n in ("src", "dst")}
        cnt_ps = ph.ps("cnt_ps")
        v = {n: ph.sb(n, [P, NT]) for n in ("cnt", "end", "zero", "some", "shift", "first", "span", "cum", "firstf",
                                            "lastf", "iota25")}
        vi = {n: ph.sb(n, [P, NT], I32) for n in ("starti", "endi")}
        w = {n: ph.sb(n, [P, IG, NT]) for n in ("past", "hot", "pick")}
        it = {n: ph.sb(n, [P, IG]) for n in ("idx", "tile", "tclamp", "etile", "valid", "off")}
        it_i = ph.sb("it_i", [P, IG], I32)
        tl_i = ph.sb("tl_i", [P, IG], I32)
        rec = {n: ph.sb(f"rec_{n}", [P, IG, P], d) for n, d in (("src", I32), ("dst", I32), ("w", F32))}
        recf = {n: ph.sb(f"recf_{n}", [P, IG, P]) for n in ("src", "dst")}
        tp = [ph.ps(f"tp{j}", (P, 512)) for j in range(4)]

        s = {n: ph.sem(n) for n in ("loaded", "own", "hot", "used", "deg", "root", "cnt", "idx", "gathered", "recf",
                                    "turned", "table", "row_out", "row_in", "rooted", "const", "rowmade")}
        block = ph.block()
        names = ("src", "dst")

        @block.sync
        def _(sp):
            sp.dma_start(raw["src"][:, :], edges["src"].rearrange("(p c) -> p c", p=P)).then_inc(s["loaded"], 16)
            sp.dma_start(raw["dst"][:, :], edges["dst"].rearrange("(p c) -> p c", p=P)).then_inc(s["loaded"], 16)
            sp.wait_ge(s["rowmade"], 1)
            with nc.allow_non_contiguous_dma(reason="416 words, once"):
                sp.dma_start(tile_row.rearrange("(g p) -> p g", p=IP), tl_i[0:IP, :]).then_inc(s["row_out"], 16)
            sp.wait_ge(s["row_out"], 16)
            sp.dma_start(g["item_tile"][:, :], tile_row.rearrange("(a n) -> a n", a=1)).then_inc(s["row_in"], 16)
            sp.wait_ge(s["row_in"], 16)

        @block.vector
        def _(dve):
            step = Steps(dve, s["own"])
            dve.wait_ge(s["loaded"], 32)
            for n in names:
                step(dve.tensor_scalar(part_i[:, :], raw[n][:, :], P - 1, None, ALU.bitwise_and))
                step.done()
                step(dve.tensor_copy(lo[n][:, :], part_i[:, :]))
                step.done()
                step(dve.tensor_scalar(part_i[:, :], raw[n][:, :], 7, None, ALU.arith_shift_right))
                step.done()
                step(dve.tensor_copy(hi[n][:, :], part_i[:, :]))
                step.done()
            blocks = cols // B

            def one_hots(n, first):
                def body(j, b, u):
                    wait(dve, s["used"], first + j - 1)
                    col = bass.ds(j * B, B)
                    dve.tensor_tensor(hot_lo[:, u, :, :], lo[n][:, col].unsqueeze(2).to_broadcast((P, B, P)),
                                      k["iota"][:, :].unsqueeze(1).to_broadcast((P, B, P)),
                                      ALU.is_equal).then_inc(s["hot"], 1)
                    dve.tensor_tensor(hot_hi[:, u, :, :], hi[n][:, col].unsqueeze(2).to_broadcast((P, B, NT)),
                                      k["iota"][:, 0:NT].unsqueeze(1).to_broadcast((P, B, NT)),
                                      ALU.is_equal).then_inc(s["hot"], 1)
                each(dve, body, blocks, 2)
            one_hots("dst", 0)
            one_hots("src", blocks)
            for j, n in enumerate(("dst", "src")):
                dve.wait_ge(s["deg"], j + 1)
                step(dve.tensor_copy(deg[n][:, :], deg_ps[n][:, 0:NT]))
                step.done()
                if n == "dst":
                    dve.sem_inc(s["idx"], 1)
            for n in names:
                step(dve.tensor_scalar(root[n][:, :], deg[n][:, :], 1.0, None, ALU.max))
            step.done()
            dve.sem_inc(s["root"], 1)
            dve.wait_ge(s["rooted"], 2)
            step(dve.reciprocal(g["norm_out"][:, :], root["src"][:, :]))
            step(dve.reciprocal(g["norm_in"][:, :], root["dst"][:, :]))
            dve.wait_ge(s["cnt"], 1)
            dve.wait_ge(s["const"], 1)
            step(dve.tensor_copy(v["cnt"][:, :], cnt_ps[:, 0:NT]))
            step(dve.memset(v["zero"][:, :], 0.0))
            step.done()
            step(dve.tensor_tensor_scan(v["end"][:, :], v["cnt"][:, :], v["zero"][:, :], 0.0, ALU.add, ALU.add))
            step(dve.tensor_scalar(v["some"][:, :], v["cnt"][:, :], 0.0, None, ALU.is_gt))
            step.done()
            step(dve.tensor_tensor(v["first"][:, :], v["end"][:, :], v["cnt"][:, :], ALU.subtract))
            step(dve.tensor_scalar(v["shift"][:, :], v["end"][:, :], -1.0, 0.0, ALU.add, ALU.max))
            step.done()
            step(dve.tensor_copy(vi["starti"][:, :], v["first"][:, :]))
            step(dve.tensor_copy(vi["endi"][:, :], v["shift"][:, :]))
            step.done()
            for n in ("starti", "endi"):
                step(dve.tensor_scalar(vi[n][:, :], vi[n][:, :], 7, None, ALU.arith_shift_right))
            step.done()
            step(dve.tensor_copy(v["firstf"][:, :], vi["starti"][:, :]))
            step(dve.tensor_copy(v["lastf"][:, :], vi["endi"][:, :]))
            step.done()
            step(dve.tensor_tensor(v["span"][:, :], v["lastf"][:, :], v["firstf"][:, :], ALU.subtract))
            step.done()
            step(dve.scalar_tensor_tensor(out=v["span"][:, :], in0=v["span"][:, :], scalar=1.0,
                                          in1=v["some"][:, :], op0=ALU.add, op1=ALU.mult))
            step.done()
            step(dve.tensor_tensor_scan(v["cum"][:, :], v["span"][:, :], v["zero"][:, :], 0.0, ALU.add, ALU.add))
            step.done()
            step(dve.tensor_tensor(v["shift"][:, :], v["span"][:, :], v["cum"][:, :], ALU.subtract))
            step.done()
            step(dve.tensor_tensor(v["shift"][:, :], v["shift"][:, :], v["firstf"][:, :], ALU.add))
            step.done()
            wide = (P, IG, NT)
            step(dve.tensor_tensor(w["past"][:, :, :], v["cum"][:, :].unsqueeze(1).to_broadcast(wide),
                                   it["idx"][:, :].unsqueeze(2).to_broadcast(wide), ALU.is_le))
            step.done()
            step(dve.tensor_reduce(it["tile"][:, :], w["past"][:, :, :], AX.X, ALU.add))
            step.done()
            step(dve.tensor_tensor(w["hot"][:, :, :], v["iota25"][:, :].unsqueeze(1).to_broadcast(wide),
                                   it["tile"][:, :].unsqueeze(2).to_broadcast(wide), ALU.is_equal))
            step(dve.tensor_scalar(it["valid"][:, :], it["tile"][:, :], float(NT), None, ALU.is_lt))
            step(dve.tensor_scalar(it["tclamp"][:, :], it["tile"][:, :], float(NT - 1), None, ALU.min))
            step.done()
            step(dve.tensor_tensor(w["pick"][:, :, :], w["hot"][:, :, :],
                                   v["shift"][:, :].unsqueeze(1).to_broadcast(wide), ALU.mult))
            step(dve.tensor_copy(tl_i[:, :], it["tclamp"][:, :]))
            step.done()
            dve.sem_inc(s["rowmade"], 1)
            step(dve.tensor_reduce(it["etile"][:, :], w["pick"][:, :, :], AX.X, ALU.add))
            step.done()
            step(dve.tensor_tensor(it["etile"][:, :], it["etile"][:, :], it["idx"][:, :], ALU.add))
            step.done()
            step(dve.tensor_scalar(it["etile"][:, :], it["etile"][:, :], 0.0, float(ET - 1), ALU.max, ALU.min))
            step.done()
            step(dve.tensor_copy(it_i[:, :], it["etile"][:, :]))
            step(dve.tensor_scalar(it["off"][:, :], it["valid"][:, :], -1.0e6, 1.0e6, ALU.mult, ALU.add))
            step.done()
            dve.sem_inc(s["idx"], 1)
            step(dve.scalar_tensor_tensor(out=it["off"][:, :], in0=it["tclamp"][:, :], scalar=float(P),
                                          in1=it["off"][:, :], op0=ALU.mult, op1=ALU.add))
            step.done()
            dve.wait_ge(s["gathered"], 16 * 3 * IG)
            for j in range(IG):
                step(dve.tensor_copy(recf["src"][0:IP, j, :], rec["src"][0:IP, j, :]))
                step(dve.tensor_copy(recf["dst"][0:IP, j, :], rec["dst"][0:IP, j, :]))
                step.done()
                step(dve.tensor_scalar(recf["dst"][0:IP, j, :], recf["dst"][0:IP, j, :], it["off"][0:IP, j:j + 1],
                                       None, ALU.subtract))
                step.done()
            dve.sem_inc(s["recf"], 1)
            for n, table in enumerate(("item_src", "item_dst", "item_w")):
                dve.wait_ge(s["turned"], n + 1)
                dve.tensor_copy(g[table][:, :], tp[n][:, 0:NI]).then_inc(s["table"], 1)
            dve.wait_ge(s["table"], 3)
            step.done()

        @block.scalar
        def _(act):
            act.wait_ge(s["root"], 1)
            for n in names:
                act.activation(root[n][:, :], root[n][:, :], ACT.Sqrt).then_inc(s["rooted"], 1)

        @block.tensor
        def _(pe):
            blocks = cols // B
            for first, n in ((0, "dst"), (blocks, "src")):
                def body(j, b, u, n=n, first=first):
                    wait(pe, s["hot"], (first + j + 1) * 2)
                    for c in range(B):
                        mm = pe.matmul(deg_ps[n][:, 0:NT], hot_lo[:, u, c, :], hot_hi[:, u, c, :],
                                       start=(isinstance(j, int) and j == 0 and c == 0),
                                       stop=(isinstance(j, int) and j == blocks - 1 and c == B - 1),
                                       skip_group_check=True)
                    mm.then_inc(s["used"], 1)
                each(pe, body, blocks, 2)
                pe.wait_ge(s["used"], first + blocks)
                pe.sem_inc(s["deg"], 1)
            pe.wait_ge(s["idx"], 1)
            pe.matmul(cnt_ps[:, 0:NT], k["ones"][:, :], deg["dst"][:, :], start=True, stop=True).then_inc(s["cnt"], 1)
            pe.wait_ge(s["recf"], 1)
            for n, r in enumerate((recf["src"], recf["dst"], rec["w"])):
                for j in range(IG):
                    tr = pe.transpose(tp[n][:, j * IP:(j + 1) * IP], r[0:IP, j, :], k["ident"][0:IP, 0:IP])
                tr.then_inc(s["turned"], 1)

        @block.gpsimd
        def _(pool):
            pool.iota(v["iota25"][:, :], pattern=[[1, NT]], base=0, channel_multiplier=0,
                      allow_small_or_imprecise_dtypes=True)
            pool.iota(it["idx"][:, :], pattern=[[IP, IG]], base=0, channel_multiplier=1,
                      allow_small_or_imprecise_dtypes=True).then_inc(s["const"], 1)
            pool.wait_ge(s["idx"], 2)
            for j in range(IG):
                for n, e, dt in (("src", "src", I32), ("dst", "dst", I32), ("w", "weight", F32)):
                    pool.indirect_dma_start(
                        out=rec[n][0:IP, j, :], out_offset=None,
                        in_=edges[e].rearrange("(r c) -> r c", c=P),
                        in_offset=bass.IndirectOffsetOnAxis(ap=it_i[0:IP, j:j + 1], axis=0)
                    ).then_inc(s["gathered"], 16)


def aggregate(nc, name, k, g, table, width, acc, weights, factors=None):
    with Phase(nc, name) as ph:
        col = ph.sb("col", [P, U], I32)
        rows = ph.sb("rows", [P, U, width])
        hot = ph.sb("hot", [P, U, P])
        out = [ph.ps(f"out{u}") for u in range(U)]
        col_ready, issued, hot_ready, summed, added, zeroed = (
            ph.sem(n) for n in ("col_ready", "issued", "hot_ready", "summed", "added", "zeroed"))
        here = [ph.sem(f"here{u}") for u in range(U)]
        block = ph.block()

        @block.scalar
        def _(act):
            def body(i, b, u):
                wait(act, here[u], b * 16)
                act.activation(col[:, u:u + 1], g["item_src"][:, at(i)], ACT.Copy).then_inc(col_ready, 1)
            each(act, body, NI, U)

        @block.gpsimd
        def _(pool):
            def body(i, b, u):
                wait(pool, col_ready, i + 1)
                wait(pool, summed, i + 1 - U)
                pool.sem_inc(issued, 1)
                pool.indirect_dma_start(
                    out=rows[:, u, :], out_offset=None, in_=table,
                    in_offset=bass.IndirectOffsetOnAxis(ap=col[:, u:u + 1], axis=0)).then_inc(here[u], 16)
            each(pool, body, NI, U)

        @block.vector
        def _(dve):
            dve.memset(acc[:, :, :], 0.0).then_inc(zeroed, 1)
            dve.wait_ge(zeroed, 1)

            def body(i, b, u):
                wait(dve, summed, i + 1 - U)
                dve.tensor_scalar(hot[:, u, :], k["iota"][:, :], g["item_dst"][:, at(i)], weights[:, at(i)],
                                  ALU.is_equal, ALU.mult).then_inc(hot_ready, 1)

            def add(i, b, u):
                tile = dve.value_load(g["item_tile"][0:1, at(i)], min_val=0, max_val=NT - 1)
                dst = tile_of(acc, tile)
                wait(dve, added, i)
                dve.wait_ge(summed, i + 1)
                if factors is None:
                    dve.tensor_tensor(dst, out[u][:, 0:width], dst, ALU.add).then_inc(added, 1)
                else:
                    dve.scalar_tensor_tensor(out=dst, in0=out[u][:, 0:width], scalar=factors[:, at(i)], in1=dst,
                                             op0=ALU.mult, op1=ALU.add).then_inc(added, 1)
            pipeline(dve, [(body, 0), (add, U // 2)], NI, U)
            dve.wait_ge(added, NI)

        @block.tensor
        def _(pe):
            def body(i, b, u):
                wait(pe, hot_ready, i + 1)
                wait(pe, added, i + 1 - U)
                wait(pe, here[u], (b + 1) * 16)
                pe.matmul(out[u][:, 0:width], hot[:, u, :], rows[:, u, :], start=True, stop=True
                          ).then_inc(summed, 1)
            each(pe, body, NI, U)


def layer_stats(nc, name, k, src, mean_rstd, width=D):
    with Phase(nc, name) as ph:
        stats = ph.sb("stats", [P, NT, 6])
        counted, taken, rooted, done = (ph.sem(n) for n in ("counted", "taken", "rooted", "done"))
        block = ph.block()

        @block.vector
        def _(dve):
            for t in range(NT):
                dve.bn_stats(stats[:, t, :], src[:, t, 0:width]).then_inc(counted, 1)
            for t in range(NT):
                dve.wait_ge(counted, t + 1)
                dve.bn_aggr(mean_rstd[:, t, :], stats[:, t, :]).then_inc(taken, 1)
            dve.wait_ge(rooted, 1)
            dve.reciprocal(mean_rstd[:, :, 1], mean_rstd[:, :, 1]).then_inc(done, 1)
            dve.wait_ge(done, 1)

        @block.scalar
        def _(act):
            act.wait_ge(taken, NT)
            act.activation(mean_rstd[:, :, 1], mean_rstd[:, :, 1], ACT.Sqrt, bias=k["eps"][:, 0:1]
                           ).then_inc(rooted, 1)


def first_gnn_weights(nc, t, k, mix, bias, channel_bias, mlp_bias):
    with Phase(nc, "w0") as ph:
        fc = ph.sb("fc", [P, L, KC, D])
        diag = ph.sb("diag", [P, L, KC, D])
        fcb = ph.sb("fcb", [P, L, KC])
        fcb_wide = ph.sb("fcb_wide", [P, L, KC, P])
        mix_ps = [ph.ps(f"mix_ps{j}") for j in range(KC)]
        bias_ps = ph.ps("bias_ps")
        zeroed, loaded, diag_in, wide, made, read, bmade, bread = (
            ph.sem(n) for n in ("zeroed", "loaded", "diag_in", "wide", "made", "read", "bmade", "bread"))
        block = ph.block()

        @block.sync
        def _(sp):
            for l in range(L):
                sp.dma_start(fc[:, l, :, :], t["fc_w"][l].rearrange("(c p) n -> p c n", p=P)).then_inc(loaded, 16)
                sp.dma_start(mix[:, l + 1, :, D:2 * D],
                             t["mlp_wT"][l * D:(l + 1) * D, :].rearrange("(c p) n -> p c n", p=P)
                             ).then_inc(loaded, 16)
                sp.dma_start(channel_bias[:, l, :], bcast(t["ch_b"][l].rearrange("c d -> (c d)"), P)
                             ).then_inc(loaded, 16)
            with nc.allow_non_contiguous_dma(reason="768 words, once"):
                sp.dma_start(fcb[:, :, :], t["fc_b"].rearrange("l (c p) -> p l c", p=P)).then_inc(loaded, 16)
            sp.dma_start(mlp_bias[:, :], bcast(t["mlp_b"], P)).then_inc(loaded, 16)
            sp.wait_ge(zeroed, 1)
            for l in range(L):
                for c in range(C):
                    p0 = (c * DH) % P
                    sp.dma_start(diag[p0:p0 + DH, l, c * DH // P, c * DH:(c + 1) * DH], t["ch_w"][l, c]
                                 ).then_inc(diag_in, 16)
            sp.wait_ge(loaded, 16 * (3 * L + 2))

        @block.gpsimd
        def _(pool):
            pool.memset(diag[:, :, :, :], 0.0).then_inc(zeroed, 1)

        @block.vector
        def _(dve):
            dve.wait_ge(loaded, 16 * (3 * L + 2))
            for l in range(L):
                for c in range(KC):
                    dve.tensor_scalar(fcb_wide[:, l, c, :], k["ones"][:, :], fcb[:, l, c:c + 1], None, ALU.mult
                                      ).then_inc(wide, 1)
            for l in range(L):
                for m in range(KC):
                    dve.wait_ge(made, l * KC + m + 1)
                    dve.tensor_copy(mix[:, l, m, 0:D], mix_ps[m][:, 0:D]).then_inc(read, 1)
                dve.wait_ge(bmade, l + 1)
                dve.tensor_copy(bias[:, l, :], bias_ps[:, 0:D]).then_inc(bread, 1)
            dve.wait_ge(read, L * KC)
            dve.wait_ge(bread, L)

        @block.tensor
        def _(pe):
            pe.wait_ge(loaded, 16 * (3 * L + 2))
            pe.wait_ge(diag_in, 16 * L * C)
            pe.wait_ge(wide, L * KC)
            for l in range(L):
                for m in range(KC):
                    wait(pe, read, (l - 1) * KC + m + 1)
                    for c in range(KC):
                        mm = pe.matmul(mix_ps[m][:, 0:D], fc[:, l, c, m * P:(m + 1) * P], diag[:, l, c, :],
                                       start=(c == 0), stop=(c == KC - 1))
                    mm.then_inc(made, 1)
                wait(pe, bread, l)
                for c in range(KC):
                    mm = pe.matmul(bias_ps[:, 0:D], fcb_wide[:, l, c, :], diag[:, l, c, :],
                                   start=(c == 0), stop=(c == KC - 1))
                mm.then_inc(bmade, 1)


def first_gnn_nodes(nc, l, k, g, x, acc, mix, bias, channel_bias, mlp_bias, table):
    lo, hi = (0 if l < L else D), (D if l == 0 else 2 * D)
    with Phase(nc, f"n{l}") as ph:
        sums = ph.sb("sums", [P, UT, D])
        node = ph.sb("node", [P, UT, D])
        turned = ph.sb("turned", [P, UT, KC, P])
        feat = ph.sb("feat", [P, UT, D])
        row = ph.sb("row", [P, UT, D])
        turn_ps = [ph.ps(f"turn{u}") for u in range(UT)]
        out_ps = [ph.ps(f"out{u}") for u in range(UT)]
        scaled, ready, turn, copied, product, biased, rowed, added = (
            ph.sem(n) for n in ("scaled", "ready", "turn", "copied", "product", "biased", "rowed", "added"))
        stored = [ph.sem(f"stored{u}") for u in range(UT)]
        block = ph.block()
        table_t = table.rearrange("(t p) d -> t p d", p=P)

        @block.vector
        def _(dve):
            def front(t, b, u):
                if l == 0:
                    wait(dve, turn, t + 1 - UT)
                    dve.tensor_scalar(node[:, u, :], tile_of(x, t), stat(g["stats"], t, 0), stat(g["stats"], t, 1),
                                      ALU.subtract, ALU.mult).then_inc(ready, 1)
                else:
                    wait(dve, ready, t + 1 - UT)
                    dve.scalar_tensor_tensor(out=sums[:, u, :], in0=tile_of(acc, t), scalar=g["norm_in"][:, at(t)],
                                             in1=channel_bias[:, l - 1, :], op0=ALU.mult, op1=ALU.add
                                             ).then_inc(scaled, 1)

            def back(t, b, u):
                dve.wait_ge(product, t + 1)
                if l < L:
                    wait(dve, rowed, t + 1 - UT)
                    dve.tensor_tensor(feat[:, u, :], out_ps[u][:, 0:D], bias[:, l, :], ALU.add
                                      ).then_inc(biased, 1)
                if l > 0:
                    xt = tile_of(x, t)
                    dve.tensor_tensor(xt, out_ps[u][:, D:2 * D], xt, ALU.add).then_inc(added, 1)
                if l == L:
                    dve.wait_ge(added, t + 1)
                    dve.tensor_tensor(xt, mlp_bias[:, :], xt, ALU.add).then_inc(biased, 1)

            pipeline(dve, [(front, 0), (back, 2)], NT, UT)
            if l < L:
                dve.wait_ge(biased, NT)
            if l > 0:
                dve.wait_ge(added, NT)

        @block.scalar
        def _(act):
            def front(t, b, u):
                if l > 0:
                    wait(act, scaled, t + 1)
                    wait(act, turn, t + 1 - UT)
                    act.activation(node[:, u, :], sums[:, u, :], ACT.Relu).then_inc(ready, 1)
                wait(act, turn, t + 1)
                wait(act, product, t + 1 - UT)
                act.activation(turned[:, u, :, :].rearrange("p c q -> p (c q)"), turn_ps[u][:, 0:D], ACT.Copy
                               ).then_inc(copied, 1)

            def back(t, b, u):
                if l < L:
                    act.wait_ge(biased, t + 1)
                    wait(act, stored[u], b * 16)
                    act.activation(row[:, u, :], feat[:, u, :], ACT.Copy, scale=g["norm_out"][:, at(t)]
                                   ).then_inc(rowed, 1)

            pipeline(act, [(front, 0), (back, 1)], NT, UT)

        @block.tensor
        def _(pe):
            def front(t, b, u):
                pe.wait_ge(ready, t + 1)
                wait(pe, copied, t + 1 - UT)
                for c in range(KC):
                    tr = pe.transpose(turn_ps[u][:, c * P:(c + 1) * P], node[:, u, c * P:(c + 1) * P],
                                      k["ident"][:, :])
                tr.then_inc(turn, 1)

            def back(t, b, u):
                pe.wait_ge(copied, t + 1)
                if l < L:
                    wait(pe, biased, t + 1 - UT)
                if l > 0:
                    wait(pe, added, t + 1 - UT)
                for c in range(KC):
                    mm = pe.matmul(out_ps[u][:, lo:hi], turned[:, u, c, :], mix[:, l, c, lo:hi],
                                   start=(c == 0), stop=(c == KC - 1))
                mm.then_inc(product, 1)

            pipeline(pe, [(front, 0), (back, 1)], NT, UT)

        if l < L:
            @block.sync
            def _(sp):
                def body(t, b, u):
                    wait(sp, rowed, t + 1)
                    sp.dma_start(table_t[at(t), :, :].rearrange("a p d -> (a p) d"), row[:, u, :]
                                 ).then_inc(stored[u], 16)
                each(sp, body, NT, UT)
                for u in range(UT):
                    sp.wait_ge(stored[u], 16 * ((NT - 1 - u) // UT + 1))


def normalised_columns(nc, name, k, x, stats, xT, score, score_w, score_b, gamma=None, beta=None, add_back=False):
    n = score.shape[2]
    with Phase(nc, name) as ph:
        node = ph.sb("node", [P, UT, D])
        turned = ph.sb("turned", [P, UT, KC, P])
        w = ph.sb("w", [P, KC, n])
        b_wide = ph.sb("b_wide", [P, n])
        affine = ph.sb("affine", [P, 2, KC])
        turn_ps = [ph.ps(f"turn{u}") for u in range(UT)]
        score_ps = [ph.ps(f"score{u}") for u in range(UT)]
        loaded, ready, turn, copied, kept, scored, taken, summed = (
            ph.sem(s) for s in ("loaded", "ready", "turn", "copied", "kept", "scored", "taken", "summed"))
        loads = 2 if gamma is None else 4
        block = ph.block()

        @block.sync
        def _(sp):
            with nc.allow_non_contiguous_dma(reason="few words, once"):
                sp.dma_start(w[:, :, :], score_w.rearrange("(c p) n -> p c n", p=P)).then_inc(loaded, 16)
                sp.dma_start(b_wide[:, :], bcast(score_b, P)).then_inc(loaded, 16)
                if gamma is not None:
                    sp.dma_start(affine[:, 0, :], gamma.rearrange("(c p) -> p c", p=P)).then_inc(loaded, 16)
                    sp.dma_start(affine[:, 1, :], beta.rearrange("(c p) -> p c", p=P)).then_inc(loaded, 16)

        @block.vector
        def _(dve):
            def front(t, b, u):
                wait(dve, turn, t + 1 - UT)
                dve.tensor_scalar(node[:, u, :], tile_of(x, t), stat(stats, t, 0), stat(stats, t, 1),
                                  ALU.subtract, ALU.mult).then_inc(ready, 1)
                if add_back:
                    dve.wait_ge(ready, t + 1)
                    dve.tensor_tensor(tile_of(x, t), tile_of(x, t), node[:, u, :], ALU.add).then_inc(summed, 1)

            def back(t, b, u):
                dve.wait_ge(scored, t + 1)
                dve.tensor_tensor(tile_of(score, t), score_ps[u][:, 0:n], b_wide[:, :], ALU.add
                                  ).then_inc(taken, 1)
            dve.wait_ge(loaded, 16 * loads)
            pipeline(dve, [(front, 0), (back, 2)], NT, UT)
            dve.wait_ge(taken, NT)
            if add_back:
                dve.wait_ge(summed, NT)

        @block.scalar
        def _(act):
            act.wait_ge(loaded, 16 * loads)

            def body(t, b, u):
                act.wait_ge(turn, t + 1)
                wait(act, scored, t + 1 - UT)
                wait(act, kept, t + 1 - UT)
                if gamma is None:
                    act.activation(turned[:, u, :, :].rearrange("p c q -> p (c q)"), turn_ps[u][:, 0:D], ACT.Copy
                                   ).then_inc(copied, 1)
                else:
                    for c in range(KC):
                        ins = act.activation(turned[:, u, c, :], turn_ps[u][:, c * P:(c + 1) * P], ACT.Identity,
                                             scale=affine[:, 0, c:c + 1], bias=affine[:, 1, c:c + 1])
                    ins.then_inc(copied, 1)
            each(act, body, NT, UT)

        @block.gpsimd
        def _(pool):
            def body(t, b, u):
                wait(pool, copied, t + 1)
                pool.tensor_copy(xT[:, :, bass.ds(t * P, P)], turned[:, u, :, :]).then_inc(kept, 1)
            each(pool, body, NT, UT)
            pool.wait_ge(kept, NT)

        @block.tensor
        def _(pe):
            pe.wait_ge(loaded, 16 * loads)

            def front(t, b, u):
                pe.wait_ge(ready, t + 1)
                wait(pe, copied, t + 1 - UT)
                for c in range(KC):
                    tr = pe.transpose(turn_ps[u][:, c * P:(c + 1) * P], node[:, u, c * P:(c + 1) * P],
                                      k["ident"][:, :])
                tr.then_inc(turn, 1)

            def back(t, b, u):
                pe.wait_ge(copied, t + 1)
                wait(pe, taken, t + 1 - UT)
                for c in range(KC):
                    mm = pe.matmul(score_ps[u][:, 0:n], turned[:, u, c, :], w[:, c, :],
                                   start=(c == 0), stop=(c == KC - 1))
                mm.then_inc(scored, 1)
            pipeline(pe, [(front, 0), (back, 1)], NT, UT)


def apply_norm(nc, name, src, stats, out):
    with Phase(nc, name) as ph:
        done = ph.sem("done")
        block = ph.block()

        @block.vector
        def _(dve):
            def body(t, b, u):
                dve.tensor_scalar(tile_of(out, t), tile_of(src, t), stat(stats, t, 0), stat(stats, t, 1),
                                  ALU.subtract, ALU.mult).then_inc(done, 1)
            each(dve, body, NT, UT)
            dve.wait_ge(done, NT)


def route_two(nc, k, logits, coef):
    with Phase(nc, "route") as ph:
        wide = [P, NT, NE]
        left = ph.sb("left", wide)
        best = ph.sb("best", wide)
        hot = [ph.sb(f"hot{j}", wide) for j in range(2)]
        rest = ph.sb("rest", wide)
        top = [ph.sb(f"top{j}", [P, NT]) for j in range(2)]
        pick = ph.sb("pick", [P, NT])
        ex = ph.sb("ex", [P, NT])
        share = [ph.sb(f"share{j}", [P, NT]) for j in range(2)]
        own, made, diff, exped = ph.sem("own"), ph.sem("made"), ph.sem("diff"), ph.sem("exped")
        block = ph.block()
        spread = lambda a: a[:, :].unsqueeze(2).to_broadcast(tuple(wide))

        @block.gpsimd
        def _(pool):
            pool.iota(left[:, :, :], pattern=[[0, NT], [-1, NE]], base=NE, channel_multiplier=0,
                      allow_small_or_imprecise_dtypes=True).then_inc(made, 1)

        @block.vector
        def _(dve):
            step = Steps(dve, own)

            def run(instruction):
                step(instruction)
                step.done()
            dve.wait_ge(made, 1)
            for j, given in enumerate((logits, rest)):
                run(dve.tensor_reduce(top[j][:, :], given[:, :, :], AX.X, ALU.max))
                run(dve.tensor_tensor(best[:, :, :], given[:, :, :], spread(top[j]), ALU.is_equal))
                run(dve.tensor_tensor(best[:, :, :], best[:, :, :], left[:, :, :], ALU.mult))
                run(dve.tensor_reduce(pick[:, :], best[:, :, :], AX.X, ALU.max))
                run(dve.tensor_tensor(hot[j][:, :, :], best[:, :, :], spread(pick), ALU.is_equal))
                if j == 0:
                    run(dve.scalar_tensor_tensor(out=rest[:, :, :], in0=hot[0][:, :, :], scalar=-3.0e38,
                                                 in1=logits[:, :, :], op0=ALU.mult, op1=ALU.add))
            run(dve.tensor_tensor(pick[:, :], top[1][:, :], top[0][:, :], ALU.subtract))
            dve.sem_inc(diff, 1)
            dve.wait_ge(exped, 1)
            run(dve.tensor_scalar(pick[:, :], ex[:, :], 1.0, None, ALU.add))
            run(dve.reciprocal(share[0][:, :], pick[:, :]))
            run(dve.tensor_tensor(share[1][:, :], ex[:, :], share[0][:, :], ALU.mult))
            for j in range(2):
                run(dve.tensor_tensor(hot[j][:, :, :], hot[j][:, :, :], spread(share[j]), ALU.mult))
            run(dve.tensor_tensor(coef[:, :, :].rearrange("p e t -> p t e"), hot[0][:, :, :], hot[1][:, :, :],
                                  ALU.add))

        @block.scalar
        def _(act):
            act.wait_ge(diff, 1)
            act.activation(ex[:, :], pick[:, :], ACT.Exp).then_inc(exped, 1)


def choose_half(nc, k, row_dram, weight, coef, chosen):
    with Phase(nc, "rank") as ph:
        wide = ph.sb("wide", [P, NP])
        junk = ph.sb("junk", [P, NP])
        before = ph.sb("before", [P, P])
        parts = ph.sb("parts", [P, NT, 4])
        rank = ph.sb("rank", [P, NT])
        out, here, made, zeroed, counted, own = (
            ph.sem(n) for n in ("out", "here", "made", "zeroed", "counted", "own"))
        block = ph.block()

        @block.sync
        def _(sp):
            with nc.allow_non_contiguous_dma(reason="3200 words, once"):
                sp.dma_start(row_dram.rearrange("(t p) -> p t", p=P), weight[:, :, 0]).then_inc(out, 16)
            sp.wait_ge(out, 16)
            sp.dma_start(wide[:, :], bcast(row_dram, P)).then_inc(here, 16)

        @block.gpsimd
        def _(pool):
            pool.affine_select(out=before[:, :], in_=k["ones"][:, :], compare_op=ALU.is_ge, fill=0.0,
                               base=-1, pattern=[[-1, P]], channel_multiplier=1).then_inc(made, 1)

        @block.vector
        def _(dve):
            step = Steps(dve, own)
            dve.memset(parts[:, :, :], 0.0).then_inc(zeroed, 1)
            dve.wait_ge(zeroed, 1)
            dve.wait_ge(here, 16)
            dve.wait_ge(made, 1)
            for t in range(NT):
                mine = weight[:, t, :]
                lo, hi = t * P, min((t + 1) * P, N)
                for j, (a, b, op) in enumerate(((0, lo, ALU.is_ge), (lo, N, ALU.is_gt))):
                    if b > a:
                        step.done() if step.n else None
                        step(dve.tensor_scalar(junk[:, a:b], wide[:, a:b], mine, None, op, ALU.add,
                                               accum_out=parts[:, t, j:j + 1]))
                step.done()
                step(dve.scalar_tensor_tensor(out=junk[:, lo:hi], in0=wide[:, lo:hi], scalar=mine,
                                              in1=before[:, 0:hi - lo], op0=ALU.is_equal, op1=ALU.mult,
                                              accum_out=parts[:, t, 2:3]))
            step.done()
            step(dve.tensor_reduce(rank[:, :], parts[:, :, :], AX.X, ALU.add))
            step.done()
            step(dve.scalar_tensor_tensor(out=coef[:, 0, :], in0=rank[:, :], scalar=float(chosen),
                                          in1=weight[:, :, 0], op0=ALU.is_lt, op1=ALU.mult))
            step.done()


def experts(nc, name, k, xT, x, coef, coef_of, w1, b1, w2, b2, count, gelu):
    FIFTH = 5
    TU = NT // FIFTH
    HALF = TU * P // 2
    HM = H // P
    UNITS = 2 * FIFTH
    with Phase(nc, name) as ph:
        w1_s = ph.sb("w1", [P, 2, KC, H])
        w2_s = ph.sb("w2", [P, 2, HM, D])
        b1_s = ph.sb("b1", [P, 2, HM])
        b2_s = ph.sb("b2", [P, 2, D])
        hidden = ph.sb("hidden", [P, 2, HM, TU * P])
        h_ps = [ph.ps(f"h{j}") for j in range(4)]
        y_ps = [ph.ps(f"y{j}") for j in range(4)]
        product, active, y_done, y_added, biased = (
            ph.sem(n) for n in ("product", "active", "y_done", "y_added", "biased"))
        here = [ph.sem(f"here{j}") for j in range(2)]
        block = ph.block()

        @block.sync
        def _(sp):
            def body(e, b, u):
                wait(sp, y_added, (e - 1) * FIFTH * TU)
                sp.dma_start(w1_s[:, u, :, :], w1(e)).then_inc(here[u], 16)
                sp.dma_start(w2_s[:, u, :, :], w2(e)).then_inc(here[u], 16)
                with nc.allow_non_contiguous_dma(reason="512 words for each block"):
                    sp.dma_start(b1_s[:, u, :], b1(e)).then_inc(here[u], 16)
                sp.dma_start(b2_s[:, u, :], b2(e)).then_inc(here[u], 16)
            each(sp, body, count, 2)

        @block.tensor
        def _(pe):
            def up(i, b, u):
                es, c = divmod(u, FIFTH)
                pe.wait_ge(here[es], (b + 1) * 64)
                for n in range(2 * HM):
                    m, half = divmod(n, 2)
                    wait(pe, active, i * 2 * HM + (n + 1 - 4))
                    for kc in range(KC):
                        mm = pe.matmul(h_ps[n % 4][:, 0:HALF], w1_s[:, es, kc, m * P:(m + 1) * P],
                                       xT[:, kc, c * TU * P + half * HALF:c * TU * P + (half + 1) * HALF],
                                       start=(kc == 0), stop=(kc == KC - 1))
                    mm.then_inc(product, 1)

            def down(i, b, u):
                es, c = divmod(u, FIFTH)
                pe.wait_ge(active, (i + 1) * 2 * HM)
                for j in range(TU):
                    n = (u * TU + j) % 4
                    wait(pe, y_added, i * TU + (j - 1) if u == 0 and j < 4 else i * TU + (j + 1 - 4))
                    for m in range(HM):
                        mm = pe.matmul(y_ps[n][:, 0:D], hidden[:, u % 2, m, j * P:(j + 1) * P],
                                       w2_s[:, es, m, :], start=(m == 0), stop=(m == HM - 1))
                    mm.then_inc(y_done, 1)
            pipeline(pe, [(up, 0), (down, 1)], count * FIFTH, UNITS)

        @block.scalar
        def _(act):
            def body(i, b, u):
                es, c = divmod(u, FIFTH)
                act.wait_ge(here[es], (b + 1) * 64)
                wait(act, y_done, (i - 1) * TU)
                for n in range(2 * HM):
                    m, half = divmod(n, 2)
                    act.wait_ge(product, i * 2 * HM + (n + 1))
                    act.activation(hidden[:, u % 2, m, half * HALF:(half + 1) * HALF], h_ps[n % 4][:, 0:HALF],
                                   gelu, bias=b1_s[:, es, m:m + 1]).then_inc(active, 1)
            each(act, body, count * FIFTH, UNITS)

        @block.vector
        def _(dve):
            def body(i, b, u):
                es, c = divmod(u, FIFTH)
                dve.wait_ge(here[es], (b + 1) * 64)
                for j in range(TU):
                    t, n = c * TU + j, (u * TU + j) % 4
                    weight = coef_of(b * 2 + es, t)
                    wait(dve, y_added, i * TU + j)
                    dve.scalar_tensor_tensor(out=x[:, t, :], in0=b2_s[:, es, :], scalar=weight, in1=x[:, t, :],
                                             op0=ALU.mult, op1=ALU.add).then_inc(biased, 1)
                    dve.wait_ge(biased, i * TU + (j + 1))
                    dve.wait_ge(y_done, i * TU + (j + 1))
                    dve.scalar_tensor_tensor(out=x[:, t, :], in0=y_ps[n][:, 0:D], scalar=weight, in1=x[:, t, :],
                                             op0=ALU.mult, op1=ALU.add).then_inc(y_added, 1)
            each(dve, body, count * FIFTH, UNITS)
            dve.wait_ge(y_added, count * FIFTH * TU)


PRE = D + KD + 2
T2 = 24
T3 = D + 4


def second_gnn_nodes(nc, k, t, x, stats, pre, wide_table):
    small = PRE - D
    with Phase(nc, "pre") as ph:
        w = ph.sb("w", [P, KC, PRE])
        b_wide = ph.sb("b_wide", [P, PRE])
        node = ph.sb("node", [P, UT, D])
        turned = ph.sb("turned", [P, UT, KC, P])
        row = ph.sb("row", [P, UT, T3])
        turn_ps = [ph.ps(f"turn{u}") for u in range(UT)]
        out_ps = [ph.ps(f"out{u}") for u in range(UT)]
        zeroed, set_, loaded, ready, turn, copied, product, biased, taken = (
            ph.sem(n) for n in ("zeroed", "set", "loaded", "ready", "turn", "copied", "product", "biased", "taken"))
        stored = [ph.sem(f"stored{u}") for u in range(UT)]
        block = ph.block()
        table_t = wide_table.rearrange("(t p) d -> t p d", p=P)
        LOADS = 7

        @block.gpsimd
        def _(pool):
            pool.memset(b_wide[:, :], 0.0).then_inc(zeroed, 1)
            pool.memset(row[:, :, D:T3], 1.0).then_inc(set_, 1)
            pool.wait_ge(set_, 1)

        @block.sync
        def _(sp):
            with nc.allow_non_contiguous_dma(reason="few words, once"):
                sp.dma_start(w[:, :, 0:D], t["Wn"].rearrange("(c p) n -> p c n", p=P)).then_inc(loaded, 16)
                sp.dma_start(w[:, :, D:D + KD], t["Wp"].rearrange("(c p) n -> p c n", p=P)).then_inc(loaded, 16)
                sp.dma_start(w[:, :, D + KD:D + KD + 1],
                             t["We"][D:2 * D, :].rearrange("(c p) n -> p c n", p=P)).then_inc(loaded, 16)
                sp.dma_start(w[:, :, D + KD + 1:PRE],
                             t["We"][0:D, :].rearrange("(c p) n -> p c n", p=P)).then_inc(loaded, 16)
                sp.wait_ge(zeroed, 1)
                sp.dma_start(b_wide[:, 0:D], bcast(t["bn"], P)).then_inc(loaded, 16)
                sp.dma_start(b_wide[:, D:D + KD], bcast(t["bp"], P)).then_inc(loaded, 16)
                sp.dma_start(b_wide[:, PRE - 1:PRE], bcast(t["be"], P)).then_inc(loaded, 16)
            sp.wait_ge(set_, 1)

            def body(i, b, u):
                wait(sp, biased, i + 1)
                sp.dma_start(table_t[at(i), :, :].rearrange("a p d -> (a p) d"), row[:, u, :]
                             ).then_inc(stored[u], 16)
            each(sp, body, NT, UT)
            for u in range(UT):
                sp.wait_ge(stored[u], 16 * ((NT - 1 - u) // UT + 1))

        @block.vector
        def _(dve):
            def front(i, b, u):
                wait(dve, turn, i + 1 - UT)
                dve.tensor_scalar(node[:, u, :], tile_of(x, i), stat(stats, i, 0), stat(stats, i, 1),
                                  ALU.subtract, ALU.mult).then_inc(ready, 1)

            def back(i, b, u):
                dve.wait_ge(product, i + 1)
                wait(dve, stored[u], b * 16)
                dve.tensor_tensor(row[:, u, 0:D], out_ps[u][:, 0:D], b_wide[:, 0:D], ALU.add).then_inc(biased, 1)
                dve.tensor_tensor(tile_of(pre, i), out_ps[u][:, D:PRE], b_wide[:, D:PRE], ALU.add
                                  ).then_inc(taken, 1)
            dve.wait_ge(loaded, 16 * LOADS)
            pipeline(dve, [(front, 0), (back, 2)], NT, UT)
            dve.wait_ge(taken, NT)

        @block.scalar
        def _(act):
            def body(i, b, u):
                act.wait_ge(turn, i + 1)
                wait(act, product, i + 1 - UT)
                act.activation(turned[:, u, :, :].rearrange("p c q -> p (c q)"), turn_ps[u][:, 0:D], ACT.Copy
                               ).then_inc(copied, 1)
            each(act, body, NT, UT)

        @block.tensor
        def _(pe):
            pe.wait_ge(loaded, 16 * LOADS)

            def front(i, b, u):
                pe.wait_ge(ready, i + 1)
                wait(pe, copied, i + 1 - UT)
                for c in range(KC):
                    tr = pe.transpose(turn_ps[u][:, c * P:(c + 1) * P], node[:, u, c * P:(c + 1) * P],
                                      k["ident"][:, :])
                tr.then_inc(turn, 1)

            def back(i, b, u):
                pe.wait_ge(copied, i + 1)
                wait(pe, taken, i + 1 - UT)
                for c in range(KC):
                    mm = pe.matmul(out_ps[u][:, 0:PRE], turned[:, u, c, :], w[:, c, :],
                                   start=(c == 0), stop=(c == KC - 1))
                mm.then_inc(product, 1)
            pipeline(pe, [(front, 0), (back, 1)], NT, UT)


def project_nodes(nc, k, t, pre, narrow, narrow_table):
    with Phase(nc, "proj") as ph:
        shape = [P, NT, KD]
        mid = ph.sb("mid", shape)
        sq = ph.sb("sq", shape)
        mean = ph.sb("mean", [P, NT])
        var = ph.sb("var", [P, NT])
        gb = ph.sb("gb", [P, 2, KD])
        rows = ph.sb("rows", [P, NT, T2])
        own, loaded, ready, rooted, finished, stored = (
            ph.sem(n) for n in ("own", "loaded", "ready", "rooted", "finished", "stored"))
        block = ph.block()
        per_node = lambda a: a.unsqueeze(2).to_broadcast(tuple(shape))
        per_col = lambda a: a.unsqueeze(1).to_broadcast(tuple(shape))

        @block.sync
        def _(sp):
            sp.dma_start(gb[:, 0, :], bcast(t["gp"], P)).then_inc(loaded, 16)
            sp.dma_start(gb[:, 1, :], bcast(t["betap"], P)).then_inc(loaded, 16)
            sp.wait_ge(finished, 1)
            sp.dma_start(narrow_table.rearrange("(t p) d -> p t d", p=P), rows[:, :, :]).then_inc(stored, 16)
            sp.wait_ge(stored, 16)

        @block.scalar
        def _(act):
            act.wait_ge(ready, 1)
            act.activation(var[:, :], var[:, :], ACT.Sqrt, bias=k["eps"][:, 0:1], scale=1.0 / KD).then_inc(rooted, 1)

        @block.vector
        def _(dve):
            step = Steps(dve, own)

            def run(instruction):
                step(instruction)
                step.done()
            p = pre[:, :, 0:KD]
            dve.wait_ge(loaded, 32)
            run(dve.memset(rows[:, :, :], 0.0))
            run(dve.tensor_reduce(mean[:, :], p, AX.X, ALU.add))
            run(dve.tensor_scalar(mean[:, :], mean[:, :], 1.0 / KD, None, ALU.mult))
            run(dve.tensor_tensor(mid[:, :, :], p, per_node(mean[:, :]), ALU.subtract))
            run(dve.tensor_tensor(sq[:, :, :], mid[:, :, :], mid[:, :, :], ALU.mult))
            run(dve.tensor_reduce(var[:, :], sq[:, :, :], AX.X, ALU.add))
            dve.sem_inc(ready, 1)
            dve.wait_ge(rooted, 1)
            run(dve.reciprocal(mean[:, :], var[:, :]))
            run(dve.tensor_tensor(mid[:, :, :], mid[:, :, :], per_node(mean[:, :]), ALU.mult))
            run(dve.tensor_tensor(mid[:, :, :], mid[:, :, :], per_col(gb[:, 0, :]), ALU.mult))
            run(dve.tensor_tensor(mid[:, :, :], mid[:, :, :], per_col(gb[:, 1, :]), ALU.add))
            run(dve.tensor_scalar(narrow[:, :, 0:KD], mid[:, :, :], 0.0, None, ALU.max))
            run(dve.tensor_scalar(rows[:, :, 0:KD], mid[:, :, :], 0.0, None, ALU.max))
            run(dve.tensor_copy(rows[:, :, KD:KD + 1], pre[:, :, KD:KD + 1]))
            run(dve.tensor_copy(narrow[:, :, KD:KD + 1], pre[:, :, KD + 1:KD + 2]))
            dve.sem_inc(finished, 1)


def kronecker_items(nc, k, t, g, narrow, narrow_table, kron_sum, below_max, item_max, tile_max):
    ND = KD + 1
    US = 4
    with Phase(nc, "kron") as ph:
        wk = ph.sb("wk", [KCH, 4, D])
        gain = ph.sb("gain", [P, D])
        shift = ph.sb("shift", [P, D])
        col = ph.sb("col", [P, U], I32)
        rows = ph.sb("rows", [P, U, T2])
        hot = ph.sb("hot", [P, U, P])
        hotT = ph.sb("hotT", [P, US, P])
        kron = ph.sb("kron", [P, US, 4, KCH])
        kronT = ph.sb("kronT", [P, US, 4, P])
        logit = ph.sb("logit", [P, U])
        diag = ph.sb("diag", [P, US, P])
        stats = ph.sb("stats", [P, US, 6])
        mv = ph.sb("mv", [P, US, 2])
        std = ph.sb("std", [P, US])
        rstd = ph.sb("rstd", [P, US])
        minus = ph.sb("minus", [P, US])
        normed = ph.sb("normed", [P, US, D])
        gained = ph.sb("gained", [P, US, D])
        shifted = ph.sb("shifted", [P, US, D])
        message = ph.sb("message", [P, US, D])
        top = ph.sb("top", [P, US])
        hotT_ps = ph.ps("hotT_ps")
        dst_ps = ph.ps("dst_ps")
        max_ps = ph.ps("max_ps")
        kronT_ps = [ph.ps(f"kronT_ps{j}") for j in range(2)]
        y_ps = [ph.ps(f"y_ps{j}") for j in range(2)]
        sum_ps = ph.ps("sum_ps")
        s = {n: ph.sem(n) for n in (
            "zeroed", "ones", "loaded", "col", "issued", "hot", "hotT", "hotT_read", "dst", "kron", "logit", "diag", "kronT",
            "kronT_read", "spread", "topped", "raised", "tops", "lowered", "y", "counted", "taken", "rooted",
            "rstd", "minus", "normed", "gained", "shifted", "message", "summed", "added", "cleared")}
        here = [ph.sem(f"here{u}") for u in range(U)]
        block = ph.block()
        LOADS = 4

        @block.sync
        def _(sp):
            sp.dma_start(gain[:, :], bcast(t["gk"], P)).then_inc(s["loaded"], 16)
            sp.dma_start(shift[:, :], bcast(t["betak"], P)).then_inc(s["loaded"], 16)
            sp.wait_ge(s["zeroed"], 1)
            sp.dma_start(wk[0:KCH - 1, :, :], t["Wk"].rearrange("(c p) n -> p c n", c=4)).then_inc(s["loaded"], 16)
            sp.dma_start(wk[KCH - 1:KCH, 3, :], t["bk"].rearrange("(a n) -> a n", a=1)).then_inc(s["loaded"], 16)

        @block.gpsimd
        def _(pool):
            pool.memset(wk[:, :, :], 0.0).then_inc(s["zeroed"], 1)
            pool.memset(kron[:, :, 0:3, KCH - 1:KCH], 0.0).then_inc(s["ones"], 1)
            pool.memset(kron[:, :, 3:4, KCH - 1:KCH], 1.0).then_inc(s["ones"], 1)
            pool.wait_ge(s["loaded"], 16 * LOADS)

            def gather(i, b, u):
                wait(pool, s["col"], i + 1)
                wait(pool, s["logit"], i + 1 - U)
                wait(pool, s["kron"], i + 1 - U)
                pool.sem_inc(s["issued"], 1)
                pool.indirect_dma_start(
                    out=rows[:, u, :], out_offset=None, in_=narrow_table,
                    in_offset=bass.IndirectOffsetOnAxis(ap=col[:, u:u + 1], axis=0)).then_inc(here[u], 16)

            def multiply(i, b, u):
                q = u % US
                wait(pool, s["normed"], i + 1)
                wait(pool, s["shifted"], i + 1 - US)
                pool.tensor_tensor(gained[:, q, :], normed[:, q, :], gain[:, :], ALU.mult).then_inc(s["gained"], 1)
            pipeline(pool, [(gather, 0), (multiply, 5)], NI, U)
            pool.wait_ge(s["gained"], NI)

        @block.scalar
        def _(act):
            act.wait_ge(s["ones"], 2)

            def column(i, b, u):
                wait(act, here[u], b * 16)
                act.activation(col[:, u:u + 1], g["item_src"][:, at(i)], ACT.Copy).then_inc(s["col"], 1)

            def hot_turned(i, b, u):
                act.wait_ge(s["hotT"], i + 1)
                wait(act, s["dst"], i + 1 - US)
                wait(act, s["tops"], i + 1 - US)
                act.activation(hotT[:, u % US, :], hotT_ps[:, 0:P], ACT.Copy).then_inc(s["hotT_read"], 1)

            def kron_turned(i, b, u):
                act.wait_ge(s["kronT"], i + 1)
                wait(act, s["y"], i + 1 - US)
                act.activation(kronT[0:KCH, u % US, :, :].rearrange("p c q -> p (c q)"),
                               kronT_ps[u % 2][0:KCH, :], ACT.Copy).then_inc(s["kronT_read"], 1)

            def root(i, b, u):
                q = u % US
                act.wait_ge(s["taken"], i + 1)
                wait(act, s["rstd"], i + 1 - US)
                act.activation(std[:, q:q + 1], mv[:, q, 1:2], ACT.Sqrt, bias=k["eps"][:, 0:1]
                               ).then_inc(s["rooted"], 1)

            def norm(i, b, u):
                q = u % US
                act.wait_ge(s["minus"], i + 1)
                wait(act, s["gained"], i + 1 - US)
                act.activation(normed[:, q, :], y_ps[u % 2][:, 0:D], ACT.Identity, scale=rstd[:, q:q + 1],
                               bias=minus[:, q:q + 1]).then_inc(s["normed"], 1)

            def relu(i, b, u):
                q = u % US
                act.wait_ge(s["shifted"], i + 1)
                wait(act, s["summed"], i + 1 - US)
                act.activation(message[:, q, :], shifted[:, q, :], ACT.Relu).then_inc(s["message"], 1)
            pipeline(act, [(relu, 10), (norm, 8), (column, 0), (hot_turned, 4), (kron_turned, 6), (root, 7)], NI, U)

        @block.tensor
        def _(pe):
            pe.wait_ge(s["loaded"], 16 * LOADS)

            def turn_hot(i, b, u):
                pe.wait_ge(s["hot"], i + 1)
                wait(pe, s["hotT_read"], i)
                pe.transpose(hotT_ps[:, 0:P], hot[:, u, :], k["ident"][:, :]).then_inc(s["hotT"], 1)

            def spread_dst(i, b, u):
                tile = pe.value_load(g["item_tile"][0:1, at(i)], min_val=0, max_val=NT - 1)
                pe.wait_ge(s["hotT_read"], i + 1)
                wait(pe, s["kron"], i)
                wait(pe, s["logit"], i)
                wait(pe, s["lowered"], i - 2)
                pe.matmul(dst_ps[:, 0:ND], hotT[:, u % US, :],
                          narrow[:, at(tile), 0:ND].rearrange("p a n -> p (a n)"),
                          start=True, stop=True).then_inc(s["dst"], 1)

            def turn_kron(i, b, u):
                q = u % US
                pe.wait_ge(s["kron"], i + 1)
                wait(pe, s["kronT_read"], i - 1)
                for c in range(4):
                    tr = pe.transpose(kronT_ps[u % 2][0:KCH, c * P:(c + 1) * P], kron[:, q, c, :], k["ident"][:, :])
                tr.then_inc(s["kronT"], 1)

            def spread_logits(i, b, u):
                pe.wait_ge(s["diag"], i + 1)
                wait(pe, s["topped"], i)
                pe.matmul(max_ps[:, 0:P], hot[:, u, :], diag[:, u % US, :], start=True, stop=True
                          ).then_inc(s["spread"], 1)

            def dense(i, b, u):
                q = u % US
                pe.wait_ge(s["kronT_read"], i + 1)
                wait(pe, s["normed"], i - 1)
                for c in range(4):
                    mm = pe.matmul(y_ps[u % 2][:, 0:D], kronT[0:KCH, q, c, :], wk[:, c, :],
                                   start=(c == 0), stop=(c == 3))
                mm.then_inc(s["y"], 1)

            def spread_tops(i, b, u):
                q = u % US
                pe.wait_ge(s["topped"], i + 1)
                wait(pe, s["kron"], i + 3 if not isinstance(i, int) else min(i + 3, NI))
                wait(pe, s["logit"], i + 3 if not isinstance(i, int) else min(i + 3, NI))
                wait(pe, s["lowered"], i)
                pe.matmul(dst_ps[:, ND + 1:ND + 2], hotT[:, q, :], top[:, q:q + 1], start=True, stop=True
                          ).then_inc(s["tops"], 1)

            def total(i, b, u):
                pe.wait_ge(s["message"], i + 1)
                wait(pe, s["added"], i)
                pe.matmul(sum_ps[:, 0:D], hot[:, u, :], message[:, u % US, :], start=True, stop=True
                          ).then_inc(s["summed"], 1)
            pipeline(pe, [(total, 6), (turn_hot, 0), (spread_dst, 1), (dense, 3), (spread_logits, 2), (turn_kron, 2),
                          (spread_tops, 3)], NI, U)

        @block.vector
        def _(dve):
            dve.memset(kron_sum[:, :, :], 0.0).then_inc(s["cleared"], 1)
            dve.memset(tile_max[:, :], 0.0).then_inc(s["cleared"], 1)
            dve.wait_ge(s["cleared"], 2)
            dve.wait_ge(s["ones"], 2)

            def one_hot(i, b, u):
                wait(dve, s["summed"], i + 1 - U)
                dve.tensor_scalar(hot[:, u, :], k["iota"][:, :], g["item_dst"][:, at(i)], None, ALU.is_equal
                                  ).then_inc(s["hot"], 1)

            def product(i, b, u):
                q = u % US
                shape = (P, 4, KD // 4, KD)
                wait(dve, here[u], (b + 1) * 16)
                dve.wait_ge(s["dst"], i + 1)
                wait(dve, s["spread"], i + 1 - US)
                dve.tensor_scalar(logit[:, u:u + 1], rows[:, u, KD:KD + 1], dst_ps[:, KD:KD + 1], 0.0, ALU.add,
                                  ALU.max).then_inc(s["logit"], 1)
                wait(dve, s["kronT"], i + 1 - US)
                dve.tensor_tensor(
                    kron[:, q, :, 0:KCH - 1].rearrange("p c (a k) -> p c a k", k=KD),
                    rows[:, u, 0:KD].rearrange("p (c a) -> p c a", c=4).unsqueeze(3).to_broadcast(shape),
                    dst_ps[:, 0:KD].unsqueeze(1).unsqueeze(1).to_broadcast(shape), ALU.mult).then_inc(s["kron"], 1)
                dve.wait_ge(s["logit"], i + 1)
                dve.tensor_scalar(diag[:, q, :], k["ident"][:, :], logit[:, u:u + 1], None, ALU.mult
                                  ).then_inc(s["diag"], 1)

            def item_tops(i, b, u):
                q = u % US
                tile = dve.value_load(g["item_tile"][0:1, at(i)], min_val=0, max_val=NT - 1)
                dve.wait_ge(s["spread"], i + 1)
                wait(dve, s["tops"], i + 1 - US)
                wait(dve, s["raised"], 2 * (i + 1 - US))
                dve.tensor_reduce(top[:, q:q + 1], max_ps[:, 0:P], AX.X, ALU.max).then_inc(s["topped"], 1)
                dve.wait_ge(s["topped"], i + 1)
                dve.tensor_copy(item_max[:, at(i)], top[:, q:q + 1]).then_inc(s["raised"], 1)
                wait(dve, s["raised"], 2 * i)
                dve.tensor_tensor(tile_max[:, at(tile)], tile_max[:, at(tile)], top[:, q:q + 1], ALU.max
                                  ).then_inc(s["raised"], 1)

            def lower(i, b, u):
                dve.wait_ge(s["tops"], i + 1)
                dve.tensor_scalar(below_max[:, at(i)], logit[:, u:u + 1], dst_ps[:, ND + 1:ND + 2], 0.0,
                                  ALU.subtract, ALU.min).then_inc(s["lowered"], 1)

            def count(i, b, u):
                q = u % US
                dve.wait_ge(s["y"], i + 1)
                wait(dve, s["taken"], i + 1 - US)
                dve.bn_stats(stats[:, q, :], y_ps[u % 2][:, 0:D]).then_inc(s["counted"], 1)

            def aggregate_(i, b, u):
                q = u % US
                dve.wait_ge(s["counted"], i + 1)
                wait(dve, s["minus"], i + 1 - US)
                wait(dve, s["rooted"], i + 1 - US)
                dve.sem_inc(s["cleared"], 1)
                dve.bn_aggr(mv[:, q, :], stats[:, q, :]).then_inc(s["taken"], 1)

            def invert(i, b, u):
                q = u % US
                dve.wait_ge(s["rooted"], i + 1)
                wait(dve, s["normed"], i + 1 - US)
                dve.reciprocal(rstd[:, q:q + 1], std[:, q:q + 1]).then_inc(s["rstd"], 1)
                dve.wait_ge(s["rstd"], i + 1)
                dve.tensor_scalar(minus[:, q:q + 1], mv[:, q, 0:1], rstd[:, q:q + 1], -1.0, ALU.mult, ALU.mult
                                  ).then_inc(s["minus"], 1)

            def add_shift(i, b, u):
                q = u % US
                dve.wait_ge(s["gained"], i + 1)
                wait(dve, s["message"], i + 1 - US)
                dve.tensor_tensor(shifted[:, q, :], gained[:, q, :], shift[:, :], ALU.add).then_inc(s["shifted"], 1)

            def add(i, b, u):
                tile = dve.value_load(g["item_tile"][0:1, at(i)], min_val=0, max_val=NT - 1)
                dst = tile_of(kron_sum, tile)
                wait(dve, s["added"], i)
                dve.wait_ge(s["summed"], i + 1)
                dve.tensor_tensor(dst, sum_ps[:, 0:D], dst, ALU.add).then_inc(s["added"], 1)
            pipeline(dve, [(one_hot, 0), (add, 6), (invert, 4), (product, 1), (item_tops, 2), (count, 3), (lower, 3),
                           (aggregate_, 3), (add_shift, 5)], NI, U)
            dve.wait_ge(s["added"], NI)
            dve.wait_ge(s["lowered"], NI)
            dve.wait_ge(s["raised"], 2 * NI)


def attention_weights(nc, k, g, below_max, item_max, tile_max, edge_w, factor):
    with Phase(nc, "attw") as ph:
        gap = ph.sb("gap", [P, NI])
        lowered, done = ph.sem("lowered"), ph.sem("done")
        block = ph.block()

        @block.vector
        def _(dve):
            def body(i, b, u):
                tile = dve.value_load(g["item_tile"][0:1, at(i)], min_val=0, max_val=NT - 1)
                dve.tensor_tensor(gap[:, at(i)], item_max[:, at(i)], tile_max[:, at(tile)], ALU.subtract
                                  ).then_inc(lowered, 1)
            each(dve, body, NI, U)

        @block.scalar
        def _(act):
            act.activation(edge_w[:, :], below_max[:, :], ACT.Exp).then_inc(done, 1)
            act.wait_ge(lowered, NI)
            act.activation(factor[:, :], gap[:, :], ACT.Exp).then_inc(done, 1)
            act.wait_ge(done, 2)


def gated_update(nc, k, t, x, stats, att, state):
    with Phase(nc, "gru") as ph:
        w_ih = ph.sb("w_ih", [P, KC, 3 * D])
        w_hh = ph.sb("w_hh", [P, KC, 3 * D])
        b_ih = ph.sb("b_ih", [P, 3 * D])
        b_hh = ph.sb("b_hh", [P, 3 * D])
        b_rz = ph.sb("b_rz", [P, 2 * D])
        inv = ph.sb("inv", [P, NT])
        both = ph.sb("both", [P, UT, 2, D])
        turned = ph.sb("turned", [P, UT, 2 * KC, P])
        rz = ph.sb("rz", [P, UT, 2 * D])
        gate = ph.sb("gate", [P, UT, 2 * D])
        i_n = ph.sb("i_n", [P, UT, D])
        h_n = ph.sb("h_n", [P, UT, D])
        cand = ph.sb("cand", [P, UT, D])
        mix = ph.sb("mix", [P, UT, D])
        turn_ps = [ph.ps(f"turn{j}") for j in range(2)]
        rz_ps = [ph.ps(f"rz{j}") for j in range(2)]
        n_ps = [ph.ps(f"n{j}") for j in range(2)]
        s = {n: ph.sem(n) for n in ("loaded", "own", "ready", "turn", "copied", "rz", "n", "rz_b", "gated", "n_read",
                                    "pre", "cand", "mixed", "out", "c1", "c2")}
        block = ph.block()

        @block.sync
        def _(sp):
            for w, name in ((w_ih, "W_ihT"), (w_hh, "W_hhT")):
                sp.dma_start(w[:, :, :], t[name].rearrange("(c p) n -> p c n", p=P)).then_inc(s["loaded"], 16)
            for w, name in ((b_ih, "b_ih"), (b_hh, "b_hh")):
                sp.dma_start(w[:, :], bcast(t[name], P)).then_inc(s["loaded"], 16)

        @block.vector
        def _(dve):
            step = Steps(dve, s["own"])
            step(dve.tensor_scalar(inv[:, :], att[:, :, D:D + 1].rearrange("p t a -> p (t a)"), 1.0e-30, None, ALU.max))
            dve.wait_ge(s["loaded"], 64)
            step.done()
            step(dve.reciprocal(inv[:, :], inv[:, :]))
            step(dve.tensor_tensor(b_rz[:, :], b_ih[:, 0:2 * D], b_hh[:, 0:2 * D], ALU.add))
            step.done()

            def front(i, b, u):
                wait(dve, s["turn"], i + 1 - UT)
                wait(dve, s["mixed"], 3 * (i + 1 - UT))
                dve.tensor_scalar(both[:, u, 0, :], att[:, at(i), 0:D].rearrange("p a d -> p (a d)"), inv[:, at(i)],
                                  0.0, ALU.mult, ALU.max).then_inc(s["ready"], 1)
                dve.tensor_scalar(both[:, u, 1, :], tile_of(x, i), stat(stats, i, 0), stat(stats, i, 1),
                                  ALU.subtract, ALU.mult).then_inc(s["ready"], 1)

            def gates(i, b, u):
                dve.wait_ge(s["rz"], i + 1)
                wait(dve, s["gated"], i + 1 - UT)
                dve.tensor_tensor(rz[:, u, :], rz_ps[u % 2][:, :], b_rz[:, :], ALU.add).then_inc(s["rz_b"], 1)
                dve.wait_ge(s["n"], i + 1)
                wait(dve, s["pre"], 2 * (i + 1 - UT))
                dve.tensor_tensor(h_n[:, u, :], n_ps[u % 2][:, D:2 * D], b_hh[:, 2 * D:3 * D], ALU.add
                                  ).then_inc(s["n_read"], 1)
                wait(dve, s["cand"], i + 1 - UT)
                dve.tensor_tensor(i_n[:, u, :], n_ps[u % 2][:, 0:D], b_ih[:, 2 * D:3 * D], ALU.add
                                  ).then_inc(s["n_read"], 1)

            def candidate(i, b, u):
                dve.wait_ge(s["gated"], i + 1)
                dve.wait_ge(s["n_read"], 2 * (i + 1))
                dve.tensor_tensor(h_n[:, u, :], h_n[:, u, :], gate[:, u, 0:D], ALU.mult).then_inc(s["pre"], 1)
                dve.wait_ge(s["pre"], 2 * i + 1)
                dve.tensor_tensor(i_n[:, u, :], i_n[:, u, :], h_n[:, u, :], ALU.add).then_inc(s["pre"], 1)

            def blend(i, b, u):
                dve.wait_ge(s["cand"], i + 1)
                wait(dve, s["out"], i + 1 - UT)
                dve.tensor_tensor(mix[:, u, :], both[:, u, 1, :], cand[:, u, :], ALU.subtract
                                  ).then_inc(s["mixed"], 1)
                dve.wait_ge(s["mixed"], 3 * i + 1)
                dve.tensor_tensor(mix[:, u, :], mix[:, u, :], gate[:, u, D:2 * D], ALU.mult).then_inc(s["mixed"], 1)
                dve.wait_ge(s["mixed"], 3 * i + 2)
                dve.tensor_tensor(mix[:, u, :], mix[:, u, :], cand[:, u, :], ALU.add).then_inc(s["mixed"], 1)
            pipeline(dve, [(front, 0), (gates, 2), (candidate, 3), (blend, 3)], NT, UT)
            dve.wait_ge(s["mixed"], 3 * NT)

        @block.scalar
        def _(act):
            def copy(i, b, u):
                act.wait_ge(s["turn"], i + 1)
                wait(act, s["n"], i + 1 - UT)
                act.activation(turned[:, u, :, :].rearrange("p c q -> p (c q)"), turn_ps[u % 2][:, :], ACT.Copy
                               ).then_inc(s["copied"], 1)

            def sigmoid(i, b, u):
                act.wait_ge(s["rz_b"], i + 1)
                wait(act, s["mixed"], 3 * (i + 1 - UT))
                act.activation(gate[:, u, :], rz[:, u, :], ACT.Sigmoid).then_inc(s["gated"], 1)

            def tanh(i, b, u):
                act.wait_ge(s["pre"], 2 * (i + 1))
                wait(act, s["mixed"], 3 * (i + 1 - UT))
                act.activation(cand[:, u, :], i_n[:, u, :], ACT.Tanh).then_inc(s["cand"], 1)

            def relu(i, b, u):
                act.wait_ge(s["mixed"], 3 * (i + 1))
                act.activation(tile_of(state, i), mix[:, u, :], ACT.Relu).then_inc(s["out"], 1)
            pipeline(act, [(copy, 0), (sigmoid, 2), (tanh, 3), (relu, 3)], NT, UT)
            act.wait_ge(s["out"], NT)

        @block.tensor
        def _(pe):
            pe.wait_ge(s["loaded"], 64)

            def turn(i, b, u):
                pe.wait_ge(s["ready"], 2 * (i + 1))
                wait(pe, s["copied"], i - 1)
                for c in range(2 * KC):
                    tr = pe.transpose(turn_ps[u % 2][:, c * P:(c + 1) * P],
                                      both[:, u, c // KC, (c % KC) * P:(c % KC + 1) * P], k["ident"][:, :])
                tr.then_inc(s["turn"], 1)

            def products(i, b, u):
                pe.wait_ge(s["copied"], i + 1)
                wait(pe, s["rz_b"], i - 1)
                for c in range(2 * KC):
                    w = w_ih if c < KC else w_hh
                    mm = pe.matmul(rz_ps[u % 2][:, :], turned[:, u, c, :], w[:, c % KC, 0:2 * D],
                                   start=(c == 0), stop=(c == 2 * KC - 1))
                mm.then_inc(s["rz"], 1)
                wait(pe, s["n_read"], 2 * (i - 1))
                for h, w in enumerate((w_ih, w_hh)):
                    for c in range(KC):
                        mm = pe.matmul(n_ps[u % 2][:, h * D:(h + 1) * D], turned[:, u, h * KC + c, :],
                                       w[:, c, 2 * D:3 * D], start=(c == 0), stop=(c == KC - 1))
                mm.then_inc(s["n"], 1)
            pipeline(pe, [(turn, 0), (products, 1)], NT, UT)


def combine(nc, k, t, state, stats, kron_sum, out):
    with Phase(nc, "comb") as ph:
        w = ph.sb("w", [P, 2 * KC, D])
        bias = ph.sb("bias", [P, D])
        gain = ph.sb("gain", [P, D])
        shift = ph.sb("shift", [P, D])
        both = ph.sb("both", [P, UT, 2, D])
        turned = ph.sb("turned", [P, UT, 2 * KC, P])
        turn_ps = [ph.ps(f"turn{u}") for u in range(UT)]
        out_ps = [ph.ps(f"out{u}") for u in range(UT)]
        s = {n: ph.sem(n) for n in ("loaded", "steps", "ready", "turn", "copied", "product", "done", "second")}
        block = ph.block()

        @block.sync
        def _(sp):
            sp.dma_start(w[:, :, :], t["Wc"].rearrange("(c p) n -> p c n", p=P)).then_inc(s["loaded"], 16)
            for b, name in ((bias, "bc"), (gain, "g_ln"), (shift, "beta_ln")):
                sp.dma_start(b[:, :], bcast(t[name], P)).then_inc(s["loaded"], 16)

        @block.vector
        def _(dve):
            dve.wait_ge(s["loaded"], 64)

            def front(i, b, u):
                h = both[:, u, 0, :]
                wait(dve, s["turn"], i + 1 - UT)
                dve.tensor_scalar(h, tile_of(state, i), stat(stats, i, 0), stat(stats, i, 1),
                                  ALU.subtract, ALU.mult).then_inc(s["steps"], 1)
                dve.wait_ge(s["steps"], 2 * i + 1)
                dve.tensor_tensor(h, h, gain[:, :], ALU.mult).then_inc(s["steps"], 1)
                dve.wait_ge(s["steps"], 2 * i + 2)
                dve.tensor_tensor(h, h, shift[:, :], ALU.add).then_inc(s["ready"], 1)

            def back(i, b, u):
                dve.wait_ge(s["product"], i + 1)
                dve.tensor_tensor(tile_of(out, i, D), out_ps[u][:, 0:D], bias[:, :], ALU.add).then_inc(s["done"], 1)
            pipeline(dve, [(front, 0), (back, 2)], NT, UT)
            dve.wait_ge(s["done"], NT)

        @block.gpsimd
        def _(pool):
            def body(i, b, u):
                wait(pool, s["turn"], i + 1 - UT)
                pool.tensor_copy(both[:, u, 1, :], tile_of(kron_sum, i)).then_inc(s["second"], 1)
            each(pool, body, NT, UT)

        @block.scalar
        def _(act):
            def body(i, b, u):
                act.wait_ge(s["turn"], i + 1)
                wait(act, s["product"], i + 1 - UT)
                act.activation(turned[:, u, :, :].rearrange("p c q -> p (c q)"), turn_ps[u][:, :], ACT.Copy
                               ).then_inc(s["copied"], 1)
            each(act, body, NT, UT)

        @block.tensor
        def _(pe):
            pe.wait_ge(s["loaded"], 64)

            def front(i, b, u):
                pe.wait_ge(s["ready"], i + 1)
                pe.wait_ge(s["second"], i + 1)
                wait(pe, s["copied"], i + 1 - UT)
                for c in range(2 * KC):
                    tr = pe.transpose(turn_ps[u][:, c * P:(c + 1) * P],
                                      both[:, u, c // KC, (c % KC) * P:(c % KC + 1) * P], k["ident"][:, :])
                tr.then_inc(s["turn"], 1)

            def back(i, b, u):
                pe.wait_ge(s["copied"], i + 1)
                wait(pe, s["done"], i + 1 - UT)
                for c in range(2 * KC):
                    mm = pe.matmul(out_ps[u][:, 0:D], turned[:, u, c, :], w[:, c, :],
                                   start=(c == 0), stop=(c == 2 * KC - 1))
                mm.then_inc(s["product"], 1)
            pipeline(pe, [(front, 0), (back, 1)], NT, UT)


def add_normalised(nc, t, y, stats, x):
    with Phase(nc, "fin") as ph:
        gain = ph.sb("gain", [P, D])
        shift = ph.sb("shift", [P, D])
        tmp = ph.sb("tmp", [P, UT, D])
        loaded, steps, positive, done = (ph.sem(n) for n in ("loaded", "steps", "positive", "done"))
        block = ph.block()

        @block.sync
        def _(sp):
            sp.dma_start(gain[:, :], bcast(t["gc"], P)).then_inc(loaded, 16)
            sp.dma_start(shift[:, :], bcast(t["betac"], P)).then_inc(loaded, 16)

        @block.vector
        def _(dve):
            dve.wait_ge(loaded, 32)

            def front(i, b, u):
                h = tmp[:, u, :]
                wait(dve, done, i + 1 - UT)
                dve.tensor_scalar(h, tile_of(y, i, D), stat(stats, i, 0), stat(stats, i, 1),
                                  ALU.subtract, ALU.mult).then_inc(steps, 1)
                dve.wait_ge(steps, 3 * i + 1)
                dve.tensor_tensor(h, h, gain[:, :], ALU.mult).then_inc(steps, 1)
                dve.wait_ge(steps, 3 * i + 2)
                dve.tensor_tensor(h, h, shift[:, :], ALU.add).then_inc(steps, 1)

            def back(i, b, u):
                dve.wait_ge(positive, i + 1)
                dve.tensor_tensor(tile_of(x, i), tmp[:, u, :], tile_of(x, i), ALU.add).then_inc(done, 1)
            pipeline(dve, [(front, 0), (back, 1)], NT, UT)
            dve.wait_ge(done, NT)

        @block.scalar
        def _(act):
            def body(i, b, u):
                act.wait_ge(steps, 3 * (i + 1))
                act.activation(tmp[:, u, :], tmp[:, u, :], ACT.Relu).then_inc(positive, 1)
            each(act, body, NT, UT)


def load_nodes(nc, t, x):
    with Phase(nc, "load") as ph:
        here = ph.sem("here")
        block = ph.block()

        @block.sync
        def _(sp):
            sp.dma_start(x[:, :, :], t["x"].rearrange("(t p) d -> p t d", p=P)).then_inc(here, 16)
            sp.wait_ge(here, 16)


def store_nodes(nc, x, out):
    with Phase(nc, "store") as ph:
        stored = ph.sem("stored")
        block = ph.block()
        whole = N // P

        @block.sync
        def _(sp):
            sp.dma_start(out[0:whole * P, :].rearrange("(t p) d -> p t d", p=P), x[:, 0:whole, :]
                         ).then_inc(stored, 16)
            sp.dma_start(out[whole * P:N, :], x[0:N - whole * P, whole, :]).then_inc(stored, 16)
            sp.wait_ge(stored, 32)


def program(nc, t, out, stop=9):
    USED.clear()
    edges = {n: nc.dram_tensor(f"edges_{n}", (EP,), I32 if n != "weight" else F32, kind="Internal").ap()
             for n in ("src", "dst", "weight")}
    tile_row = nc.dram_tensor("tile_row", (NI,), I32, kind="Internal").ap()
    table = nc.dram_tensor("table", (NP, D), F32, kind="Internal").ap()
    wide_table = nc.dram_tensor("wide_table", (NP, T3), F32, kind="Internal").ap()
    narrow_table = nc.dram_tensor("narrow_table", (NP, T2), F32, kind="Internal").ap()
    weight_row = nc.dram_tensor("weight_row", (NP,), F32, kind="Internal").ap()
    with Phase(nc, "all") as top:
        k = constants(nc, top)
        x = top.sb("x", [P, NT, D])
        acc = top.sb("acc", [P, NT, D])
        g = {n: top.sb(n, [P, NI]) for n in ("item_dst", "item_w")}
        g["item_src"] = top.sb("item_src", [P, NI], I32)
        g["item_tile"] = top.sb("item_tile", [1, NI], I32)
        g["norm_in"] = top.sb("norm_in", [P, NT])
        g["norm_out"] = top.sb("norm_out", [P, NT])
        g["stats"] = top.sb("stats", [P, NT, 2])
        load_nodes(nc, t, x)
        order_edges(nc, t, k, edges)
        degrees_and_items(nc, t, k, edges, g, tile_row)
        with Phase(nc, "gnn0") as ph:
            mix = ph.sb("mix", [P, L + 1, KC, 2 * D])
            bias = ph.sb("bias", [P, L, D])
            channel_bias = ph.sb("channel_bias", [P, L, D])
            mlp_bias = ph.sb("mlp_bias", [P, D])
            first_gnn_weights(nc, t, k, mix, bias, channel_bias, mlp_bias)
            layer_stats(nc, "st0", k, x, g["stats"])
            for l in range(L + 1):
                first_gnn_nodes(nc, l, k, g, x, acc, mix, bias, channel_bias, mlp_bias, table)
                if l < L:
                    aggregate(nc, f"agg{l}", k, g, table, D, acc, g["item_w"])
        clear_semaphores(nc)
        if stop >= 2:
            with Phase(nc, "moe") as ph:
                xT = ph.sb("xT", [P, KC, NP])
                logits = ph.sb("logits", [P, NT, NE])
                coef = ph.sb("coef", [P, NE, NT])
                layer_stats(nc, "st1", k, x, g["stats"])
                apply_norm(nc, "an1", x, g["stats"], acc)
                layer_stats(nc, "st2", k, acc, g["stats"])
                normalised_columns(nc, "nc1", k, acc, g["stats"], xT, logits, t["Wr"], t["br"],
                                   t["gamma"], t["beta"])
                route_two(nc, k, logits, coef)
                experts(nc, "moe", k, xT, x, coef,
                        lambda e, n: coef[:, at(e), n:n + 1].rearrange("p a b -> p (a b)"),
                        lambda e: t["W1"][at(e)].rearrange("a (c p) n -> p (a c) n", p=P),
                        lambda e: t["b1"][at(e)].rearrange("a (m p) -> p (a m)", p=P),
                        lambda e: t["W2"][at(e)].rearrange("a (m p) n -> p (a m) n", p=P),
                        lambda e: t["b2"][at(e)].to_broadcast((P, D)),
                        NE, ACT.Gelu)
        clear_semaphores(nc)
        if stop >= 3:
            with Phase(nc, "gnn1") as ph:
                att = ph.sb("att", [P, NT, T3])
                kron_sum = ph.sb("kron_sum", [P, NT, D])
                edge_w = ph.sb("edge_w", [P, NI])
                factor = ph.sb("factor", [P, NI])
                layer_stats(nc, "st3", k, x, g["stats"])
                with Phase(nc, "items1") as at_items:
                    pre = at_items.sb("pre", [P, NT, PRE - D])
                    narrow = at_items.sb("narrow", [P, NT, KD + 1])
                    below_max = at_items.sb("below_max", [P, NI])
                    item_max = at_items.sb("item_max", [P, NI])
                    tile_max = at_items.sb("tile_max", [P, NT])
                    second_gnn_nodes(nc, k, t, x, g["stats"], pre, wide_table)
                    project_nodes(nc, k, t, pre, narrow, narrow_table)
                    kronecker_items(nc, k, t, g, narrow, narrow_table, kron_sum, below_max, item_max, tile_max)
                    attention_weights(nc, k, g, below_max, item_max, tile_max, edge_w, factor)
                aggregate(nc, "agga", k, g, wide_table, T3, att, edge_w, factor)
                gated_update(nc, k, t, x, g["stats"], att, acc)
                layer_stats(nc, "st4", k, acc, g["stats"])
                combine(nc, k, t, acc, g["stats"], kron_sum, att)
                layer_stats(nc, "st5", k, att, g["stats"])
                add_normalised(nc, t, att, g["stats"], x)
        clear_semaphores(nc)
        if stop >= 4:
            with Phase(nc, "ffn1") as ph:
                xT = ph.sb("xT", [P, KC, NP])
                weight = ph.sb("weight", [P, NT, 1])
                coef = ph.sb("coef", [P, 1, NT])
                layer_stats(nc, "st6", k, x, g["stats"])
                normalised_columns(nc, "nc2", k, x, g["stats"], xT, weight, t["wr"], t["ffn_br"], add_back=True)
                choose_half(nc, k, weight_row, weight, coef, max(1, N // 2) - 1)
                experts(nc, "dense", k, xT, x, coef, lambda e, n: coef[:, 0, n:n + 1],
                        lambda e: t["w1"][:, bass.ds(e * H, H)].rearrange("(c p) n -> p c n", p=P),
                        lambda e: t["ffn_b1"][bass.ds(e * H, H)].rearrange("(m p) -> p m", p=P),
                        lambda e: t["w2"][bass.ds(e * H, H), :].rearrange("(m p) n -> p m n", p=P),
                        lambda e: bcast(t["ffn_b2"][e], P), 2, ACT.Gelu_apprx_tanh)
        store_nodes(nc, x, out)


def laid_out(**a):
    src, dst = (np.concatenate([np.asarray(a[n]), np.full(EP - E, NP - 1, np.int32)]) for n in ("src", "dst"))
    return {
        "x": np.concatenate([np.asarray(a["x"]), np.zeros((NP - N, D), np.float32)]),
        "src": src, "dst": dst,
        "weight": np.concatenate([np.asarray(a["edge_weight"]), np.zeros(EP - E, np.float32)]),
        "fc_w": np.asarray(a["L0_gnn_fc_w"]), "fc_b": np.asarray(a["L0_gnn_fc_b"]),
        "ch_w": np.asarray(a["L0_gnn_ch_w"]), "ch_b": np.asarray(a["L0_gnn_ch_b"]),
        "mlp_wT": np.ascontiguousarray(np.asarray(a["L0_gnn_mlp_w"]).T), "mlp_b": np.asarray(a["L0_gnn_mlp_b"]),
        **{n: np.asarray(a["L0_ffn_" + n]) for n in ("gamma", "beta", "Wr", "br", "W1", "b1", "W2", "b2")},
        **{n: np.asarray(a["L1_gnn_" + n]) for n in (
            "Wp", "bp", "gp", "betap", "Wk", "bk", "gk", "betak", "We", "be", "Wn", "bn", "b_ih", "b_hh",
            "g_ln", "beta_ln", "Wc", "bc", "gc", "betac")},
        "W_ihT": np.ascontiguousarray(np.asarray(a["L1_gnn_W_ih"]).T),
        "W_hhT": np.ascontiguousarray(np.asarray(a["L1_gnn_W_hh"]).T),
        "wr": np.asarray(a["L1_ffn_wr"]), "ffn_br": np.asarray(a["L1_ffn_br"]),
        "w1": np.asarray(a["L1_ffn_w1"]), "ffn_b1": np.asarray(a["L1_ffn_b1"]),
        "w2": np.asarray(a["L1_ffn_w2"]),
        "ffn_b2": np.stack([np.asarray(a["L1_ffn_b2"]), np.zeros(D, np.float32)]),
    }


def kernel(**inputs):
    from concourse import bacc
    from concourse.bass_utils import run_bass_kernel_spmd

    nc = bacc.Bacc("TRN2", target_bir_lowering=False, num_devices=1)
    arrays = laid_out(**inputs)
    t = {n: nc.dram_tensor(n, a.shape, mybir.dt.from_np(a.dtype), kind="ExternalInput").ap()
         for n, a in arrays.items()}
    out = nc.dram_tensor("out", (N, D), F32, kind="ExternalOutput").ap()
    program(nc, t, out)
    return run_bass_kernel_spmd(nc, [arrays], core_ids=[0]).results[0]["out"]
```

```python
from contextlib import ExitStack

import concourse.bass as bass
import numpy as np
from concourse import mybir

F32 = mybir.dt.float32
BF16 = mybir.dt.bfloat16
I32 = mybir.dt.int32
ALU = mybir.AluOpType
ACT = mybir.ActivationFunctionType
AX = mybir.AxisListType

P = 128
N, D, E = 3125, 256, 50000
KC = D // P
NT = -(-N // P)
NP = NT * P
ET = 392
EP = ET * P
IG = 4
NI = 416
IP = NI // IG
L = 3
C, DH = 4, 64
NE, H = 8, 512
KD = 20
ND = KD + 1
KCH = 111
NS = 32
G = 4
NG = NI // G
UG = 8
T2 = 24
T3 = D + 4
EPS = 1e-5
UT = 4
assert NI >= ET + NT - 1 and NI == IG * IP and NG % UG == 0 and 4 * KCH >= ND * ND


USED = []


def clear_semaphores(nc):
    nc.clear_and_free_semaphores(list(USED))
    USED.clear()
    nc.all_engine_barrier()


class Phase:

    def __init__(self, nc, name):
        self.nc, self.name = nc, name

    def __enter__(self):
        self.stack = ExitStack()
        return self

    def __exit__(self, *exc):
        return self.stack.__exit__(*exc)

    def sb(self, name, shape, dt=F32):
        return self.stack.enter_context(self.nc.sbuf_tensor(f"{self.name}_{name}", shape, dt))

    def ps(self, name, shape=(P, 512)):
        return self.stack.enter_context(self.nc.psum_tensor(f"{self.name}_{name}", list(shape), F32))

    def sem(self, name):
        handle = self.nc.alloc_semaphore(f"{self.name}_{name}")
        USED.append(handle)
        return handle

    def block(self):
        return self.stack.enter_context(self.nc.Block())


def wait(eng, sem, value):
    if not (isinstance(value, int) and value <= 0):
        eng.wait_ge(sem, value)


class Steps:

    def __init__(self, eng, sem):
        self.eng, self.sem, self.n = eng, sem, 0

    def __call__(self, instruction):
        self.n += 1
        instruction.then_inc(self.sem, 1)
        return self

    def done(self):
        self.eng.wait_ge(self.sem, self.n)


def pipeline(eng, stages, count, unroll):
    last = max(lag for _, lag in stages)
    peeled, blocks = 1 + -(-last // unroll), count // unroll

    def tick(block, u):
        for body, lag in stages:
            over, slot = divmod(u - lag, unroll)
            if not isinstance(block, int):
                body(block * unroll + (u - lag), block + over if over else block, slot)
            elif 0 <= (block + over) * unroll + slot < count:
                body((block + over) * unroll + slot, block + over, slot)

    looped = blocks > peeled
    for n in range(peeled * unroll if looped else count + last):
        tick(n // unroll, n % unroll)
    if not looped:
        return
    with eng.Fori(peeled, blocks) as b:
        for u in range(unroll):
            tick(b, u)
    for n in range(blocks * unroll, count + last):
        tick(n // unroll, n % unroll)


def each(eng, body, count, unroll):
    pipeline(eng, [(body, 0)], count, unroll)


def at(i):
    return bass.ds(i, 1)


def tile_of(t, i, width=None):
    return t[:, at(i), 0:width or t.shape[2]].rearrange("p a d -> p (a d)")


def group(table, i):
    return table[:, bass.ds(i * G, G)]


def flat_places(nc, engine, table, first, n, largest):
    return nc.values_load_multi_w_load_instructions(
        table[:, bass.ds(first, n)], engines=(engine,), min_val=0, max_val=largest,
        skip_runtime_bounds_check_because="they are made from clamped tiles")[1]


def stat(mean_rstd, t, n):
    return mean_rstd[:, at(t), n:n + 1].rearrange("p a b -> p (a b)")


def bcast(vector, rows):
    return vector.rearrange("(a n) -> a n", a=1).to_broadcast((rows, vector.shape[0]))


def constants(nc, top):
    k = {}
    k["ident"] = top.sb("ident", [P, P])
    k["iota"] = top.sb("iota", [P, P])
    k["ones"] = top.sb("ones", [P, P])
    k["eps"] = top.sb("eps", [P, 1])
    with Phase(nc, "const") as ph:
        made, ready = ph.sem("made"), ph.sem("ready")
        block = ph.block()

        @block.gpsimd
        def _(pool):
            pool.memset(k["ident"][:, :], 0.0).then_inc(made, 1)
            pool.memset(k["ones"][:, :], 1.0).then_inc(ready, 1)
            pool.memset(k["eps"][:, :], EPS).then_inc(ready, 1)
            pool.iota(k["iota"][:, :], pattern=[[1, P]], base=0, channel_multiplier=0,
                      allow_small_or_imprecise_dtypes=True).then_inc(ready, 1)
            pool.wait_ge(made, 1)
            pool.affine_select(out=k["ident"][:, :], in_=k["ident"][:, :], compare_op=ALU.not_equal, fill=1.0,
                               base=0, pattern=[[-1, P]], channel_multiplier=1).then_inc(ready, 1)
            pool.wait_ge(ready, 4)
    return k


def order_edges(nc, t, k, edges):
    with Phase(nc, "order") as ph:
        cols = EP // P
        dst_i = ph.sb("dst_i", [P, cols], I32)
        dst_f = ph.sb("dst_f", [P, cols])
        nxt_i = ph.sb("nxt_i", [P, cols], I32)
        nxt_f = ph.sb("nxt_f", [P, cols])
        src_i = ph.sb("src_i", [P, cols], I32)
        wgt = ph.sb("wgt", [P, cols])
        fall = ph.sb("fall", [P, cols])
        falls = ph.sb("falls", [P, 1])
        unordered = ph.sb("unordered", [P, 1], I32)
        bin_i = ph.sb("bin_i", [P, cols], I32)
        bin_f = ph.sb("bin_f", [P, cols])
        mask = ph.sb("mask", [P, cols])
        rank = ph.sb("rank", [P, cols])
        none = ph.sb("none", [P, cols])
        place = ph.sb("place", [P, cols])
        place_i = ph.sb("place_i", [P, cols], I32)
        count = ph.sb("count", [P, NT])
        total = ph.sb("total", [P, NT])
        start = ph.sb("start", [P, NT])
        zero = ph.sb("zero", [P, NT])
        below = ph.sb("below", [P, P])
        slot = ph.sb("slot", [P, 1], I32)
        one_s = ph.sb("one_s", [P, 1], I32)
        one_d = ph.sb("one_d", [P, 1], I32)
        one_w = ph.sb("one_w", [P, 1])
        tot_ps = ph.ps("tot_ps")
        pre_ps = ph.ps("pre_ps")
        flag_ps = ph.ps("flag_ps")

        loaded, own, pool_own = ph.sem("loaded"), ph.sem("own"), ph.sem("pool_own")
        below_ready, falls_ready, flag_sum = ph.sem("below_ready"), ph.sem("falls_ready"), ph.sem("flag_sum")
        flag_ready, counts_ready, prefix = ph.sem("flag_ready"), ph.sem("counts_ready"), ph.sem("prefix")
        place_ready, slot_ready = ph.sem("place_ready"), ph.sem("slot_ready")
        copied, stored, issued = ph.sem("copied"), ph.sem("stored"), ph.sem("issued")
        block = ph.block()

        rows = lambda a: a.rearrange("(p c) -> p c", p=P)

        @block.sync
        def _(sp):
            sp.dma_start(dst_i[:, :], rows(t["dst"])).then_inc(loaded, 16)
            sp.dma_start(nxt_i[0:P - 1, :], t["dst"][1:1 + (P - 1) * cols].rearrange("(p c) -> p c", c=cols)
                         ).then_inc(loaded, 16)
            sp.dma_start(nxt_i[P - 1:P, 0:cols - 1],
                         t["dst"][1 + (P - 1) * cols:EP].rearrange("(a c) -> a c", a=1)).then_inc(loaded, 16)
            sp.dma_start(nxt_i[P - 1:P, cols - 1:cols],
                         t["dst"][EP - 1:EP].rearrange("(a c) -> a c", a=1)).then_inc(loaded, 16)
            sp.dma_start(src_i[:, :], rows(t["src"])).then_inc(loaded, 16)
            sp.dma_start(wgt[:, :], rows(t["weight"])).then_inc(loaded, 16)
            sp.wait_ge(flag_ready, 1)
            flag = sp.value_load(unordered[0:1, 0:1], min_val=0, max_val=EP)
            with sp.If(flag < 1):
                sp.dma_start(rows(edges["src"]), rows(t["src"])).then_inc(copied, 16)
                sp.dma_start(rows(edges["dst"]), rows(t["dst"])).then_inc(copied, 16)
                sp.dma_start(rows(edges["weight"]), rows(t["weight"])).then_inc(copied, 16)
                sp.wait_ge(copied, 48)
            with sp.Else():
                sp.nop()

        @block.vector
        def _(dve):
            step = Steps(dve, own)
            step(dve.memset(none[:, :], 0.0))
            step(dve.memset(place[:, :], 0.0))
            step(dve.memset(zero[:, :], 0.0))
            dve.wait_ge(loaded, 96)
            step(dve.tensor_copy(dst_f[:, :], dst_i[:, :]))
            step(dve.tensor_copy(nxt_f[:, :], nxt_i[:, :]))
            step(dve.tensor_scalar(bin_i[:, :], dst_i[:, :], 7, None, ALU.arith_shift_right))
            step.done()
            step(dve.tensor_tensor(fall[:, :], nxt_f[:, :], dst_f[:, :], ALU.is_lt))
            step(dve.tensor_copy(bin_f[:, :], bin_i[:, :]))
            step.done()
            dve.tensor_reduce(falls[:, :], fall[:, :], AX.X, ALU.add).then_inc(falls_ready, 1)
            for b in range(NT):
                step(dve.tensor_scalar(mask[:, :], bin_f[:, :], float(b), None, ALU.is_equal))
                step.done()
                step(dve.tensor_reduce(count[:, b:b + 1], mask[:, :], AX.X, ALU.add))
                step.done()
            dve.sem_inc(counts_ready, 1)
            dve.wait_ge(prefix, 2)
            step(dve.tensor_copy(total[:, :], tot_ps[:, 0:NT]))
            step.done()
            step(dve.tensor_tensor_scan(start[:, :], total[:, :], zero[:, :], 0.0, ALU.add, ALU.add))
            step.done()
            step(dve.tensor_tensor(start[:, :], start[:, :], total[:, :], ALU.subtract))
            step.done()
            step(dve.tensor_tensor(start[:, :], start[:, :], pre_ps[:, 0:NT], ALU.add))
            dve.wait_ge(flag_sum, 1)
            dve.tensor_copy(unordered[:, :], flag_ps[:, 0:1]).then_inc(flag_ready, 1)
            step.done()
            dve.wait_ge(flag_ready, 1)
            flag = dve.value_load(unordered[0:1, 0:1], min_val=0, max_val=EP)
            with dve.If(flag < 1):
                dve.nop()
            with dve.Else():
                for b in range(NT):
                    step(dve.tensor_scalar(mask[:, :], bin_f[:, :], float(b), None, ALU.is_equal))
                    step.done()
                    step(dve.tensor_tensor_scan(rank[:, :], mask[:, :], none[:, :], 0.0, ALU.add, ALU.add))
                    step.done()
                    step(dve.tensor_scalar(rank[:, :], rank[:, :], start[:, b:b + 1], -1.0, ALU.add, ALU.add))
                    step.done()
                    step(dve.tensor_tensor(rank[:, :], rank[:, :], mask[:, :], ALU.mult))
                    step.done()
                    step(dve.tensor_tensor(place[:, :], place[:, :], rank[:, :], ALU.add))
                    step.done()
                dve.tensor_copy(place_i[:, :], place[:, :]).then_inc(place_ready, 1)

        @block.tensor
        def _(pe):
            pe.wait_ge(falls_ready, 1)
            pe.matmul(flag_ps[:, 0:1], k["ones"][:, :], falls[:, :], start=True, stop=True).then_inc(flag_sum, 1)
            pe.wait_ge(counts_ready, 1)
            pe.wait_ge(below_ready, 1)
            pe.matmul(tot_ps[:, 0:NT], k["ones"][:, :], count[:, :], start=True, stop=True).then_inc(prefix, 1)
            pe.matmul(pre_ps[:, 0:NT], below[:, :], count[:, :], start=True, stop=True).then_inc(prefix, 1)

        @block.gpsimd
        def _(pool):
            pool.affine_select(out=below[:, :], in_=k["ones"][:, :], compare_op=ALU.is_ge, fill=0.0,
                               base=-1, pattern=[[1, P]], channel_multiplier=-1).then_inc(below_ready, 1)
            pool.wait_ge(flag_ready, 1)
            flag = pool.value_load(unordered[0:1, 0:1], min_val=0, max_val=EP)
            with pool.If(flag < 1):
                pool.nop()
            with pool.Else():
                pool.wait_ge(place_ready, 1)
                pool.wait_ge(loaded, 96)
                with pool.Fori(0, cols) as c:
                    pool.tensor_copy(slot[:, :], place_i[:, at(c)]).then_inc(slot_ready, 1)
                    pool.tensor_copy(one_s[:, :], src_i[:, at(c)]).then_inc(slot_ready, 1)
                    pool.tensor_copy(one_d[:, :], dst_i[:, at(c)]).then_inc(slot_ready, 1)
                    pool.tensor_copy(one_w[:, :], wgt[:, at(c)]).then_inc(slot_ready, 1)
                    pool.wait_ge(slot_ready, (c + 1) * 4)
                    pool.sem_inc(issued, 1)
                    for name, one in (("src", one_s), ("dst", one_d), ("weight", one_w)):
                        pool.indirect_dma_start(
                            out=edges[name].rearrange("(e a) -> e a", a=1),
                            out_offset=bass.IndirectOffsetOnAxis(ap=slot[:, :], axis=0),
                            in_=one[:, :], in_offset=None).then_inc(stored, 16)
                    pool.wait_ge(stored, (c + 1) * 48)


def degrees_and_items(nc, t, k, edges, g, tile_row):
    with Phase(nc, "items") as ph:
        cols = EP // P
        B = 14
        assert cols % B == 0
        raw = {n: ph.sb(f"{n}_raw", [P, cols], I32) for n in ("src", "dst")}
        part_i = ph.sb("part_i", [P, cols], I32)
        lo = {n: ph.sb(f"{n}_lo", [P, cols]) for n in ("src", "dst")}
        hi = {n: ph.sb(f"{n}_hi", [P, cols]) for n in ("src", "dst")}
        hot_lo = ph.sb("hot_lo", [P, 2, B, P], BF16)
        hot_hi = ph.sb("hot_hi", [P, 2, B, NT], BF16)
        deg = {n: ph.sb(f"{n}_deg", [P, NT]) for n in ("src", "dst")}
        root = {n: ph.sb(f"{n}_root", [P, NT]) for n in ("src", "dst")}
        deg_ps = {n: ph.ps(f"{n}_deg_ps") for n in ("src", "dst")}
        cnt_ps = ph.ps("cnt_ps")
        v = {n: ph.sb(n, [P, NT]) for n in ("cnt", "end", "zero", "some", "shift", "first", "span", "cum", "firstf",
                                            "lastf", "iota25")}
        vi = {n: ph.sb(n, [P, NT], I32) for n in ("starti", "endi")}
        w = {n: ph.sb(n, [P, IG, NT]) for n in ("past", "hot", "pick")}
        it = {n: ph.sb(n, [P, IG]) for n in ("idx", "tile", "tclamp", "etile", "valid", "off")}
        it_i = ph.sb("it_i", [P, IG], I32)
        tl_i = ph.sb("tl_i", [P, IG], I32)
        tiles_i = ph.sb("tiles_i", [1, NI], I32)
        tiles_f = ph.sb("tiles_f", [1, NI])
        places = ph.sb("places", [1, NI])
        rec = {n: ph.sb(f"rec_{n}", [P, IG, P], d) for n, d in (("src", I32), ("dst", I32), ("w", F32))}
        recf = {n: ph.sb(f"recf_{n}", [P, IG, P]) for n in ("src", "dst")}
        tp = [ph.ps(f"tp{j}", (P, 512)) for j in range(4)]

        s = {n: ph.sem(n) for n in ("loaded", "own", "hot", "used", "deg", "root", "cnt", "idx", "gathered", "recf",
                                    "turned", "table", "row_out", "row_in", "rooted", "const", "rowmade")}
        block = ph.block()
        names = ("src", "dst")

        @block.sync
        def _(sp):
            sp.dma_start(raw["src"][:, :], edges["src"].rearrange("(p c) -> p c", p=P)).then_inc(s["loaded"], 16)
            sp.dma_start(raw["dst"][:, :], edges["dst"].rearrange("(p c) -> p c", p=P)).then_inc(s["loaded"], 16)
            sp.wait_ge(s["rowmade"], 1)
            with nc.allow_non_contiguous_dma(reason="416 words, once"):
                sp.dma_start(tile_row.rearrange("(g p) -> p g", p=IP), tl_i[0:IP, :]).then_inc(s["row_out"], 16)
            sp.wait_ge(s["row_out"], 16)
            sp.dma_start(tiles_i[:, :], tile_row.rearrange("(a n) -> a n", a=1)).then_inc(s["row_in"], 16)

        @block.vector
        def _(dve):
            step = Steps(dve, s["own"])
            dve.wait_ge(s["loaded"], 32)
            for n in names:
                step(dve.tensor_scalar(part_i[:, :], raw[n][:, :], P - 1, None, ALU.bitwise_and))
                step.done()
                step(dve.tensor_copy(lo[n][:, :], part_i[:, :]))
                step.done()
                step(dve.tensor_scalar(part_i[:, :], raw[n][:, :], 7, None, ALU.arith_shift_right))
                step.done()
                step(dve.tensor_copy(hi[n][:, :], part_i[:, :]))
                step.done()
            blocks = cols // B

            def one_hots(n, first):
                def body(j, b, u):
                    wait(dve, s["used"], first + j - 1)
                    col = bass.ds(j * B, B)
                    dve.tensor_tensor(hot_lo[:, u, :, :], lo[n][:, col].unsqueeze(2).to_broadcast((P, B, P)),
                                      k["iota"][:, :].unsqueeze(1).to_broadcast((P, B, P)),
                                      ALU.is_equal).then_inc(s["hot"], 1)
                    dve.tensor_tensor(hot_hi[:, u, :, :], hi[n][:, col].unsqueeze(2).to_broadcast((P, B, NT)),
                                      k["iota"][:, 0:NT].unsqueeze(1).to_broadcast((P, B, NT)),
                                      ALU.is_equal).then_inc(s["hot"], 1)
                each(dve, body, blocks, 2)
            one_hots("dst", 0)
            one_hots("src", blocks)
            for j, n in enumerate(("dst", "src")):
                dve.wait_ge(s["deg"], j + 1)
                step(dve.tensor_copy(deg[n][:, :], deg_ps[n][:, 0:NT]))
                step.done()
                if n == "dst":
                    dve.sem_inc(s["idx"], 1)
            for n in names:
                step(dve.tensor_scalar(root[n][:, :], deg[n][:, :], 1.0, None, ALU.max))
            step.done()
            dve.sem_inc(s["root"], 1)
            dve.wait_ge(s["rooted"], 2)
            step(dve.reciprocal(g["norm_out"][:, :], root["src"][:, :]))
            step(dve.reciprocal(g["norm_in"][:, :], root["dst"][:, :]))
            dve.wait_ge(s["cnt"], 1)
            dve.wait_ge(s["const"], 1)
            step(dve.tensor_copy(v["cnt"][:, :], cnt_ps[:, 0:NT]))
            step(dve.memset(v["zero"][:, :], 0.0))
            step.done()
            step(dve.tensor_tensor_scan(v["end"][:, :], v["cnt"][:, :], v["zero"][:, :], 0.0, ALU.add, ALU.add))
            step(dve.tensor_scalar(v["some"][:, :], v["cnt"][:, :], 0.0, None, ALU.is_gt))
            step.done()
            step(dve.tensor_tensor(v["first"][:, :], v["end"][:, :], v["cnt"][:, :], ALU.subtract))
            step(dve.tensor_scalar(v["shift"][:, :], v["end"][:, :], -1.0, 0.0, ALU.add, ALU.max))
            step.done()
            step(dve.tensor_copy(vi["starti"][:, :], v["first"][:, :]))
            step(dve.tensor_copy(vi["endi"][:, :], v["shift"][:, :]))
            step.done()
            for n in ("starti", "endi"):
                step(dve.tensor_scalar(vi[n][:, :], vi[n][:, :], 7, None, ALU.arith_shift_right))
            step.done()
            step(dve.tensor_copy(v["firstf"][:, :], vi["starti"][:, :]))
            step(dve.tensor_copy(v["lastf"][:, :], vi["endi"][:, :]))
            step.done()
            step(dve.tensor_tensor(v["span"][:, :], v["lastf"][:, :], v["firstf"][:, :], ALU.subtract))
            step.done()
            step(dve.scalar_tensor_tensor(out=v["span"][:, :], in0=v["span"][:, :], scalar=1.0,
                                          in1=v["some"][:, :], op0=ALU.add, op1=ALU.mult))
            step.done()
            step(dve.tensor_tensor_scan(v["cum"][:, :], v["span"][:, :], v["zero"][:, :], 0.0, ALU.add, ALU.add))
            step.done()
            step(dve.tensor_tensor(v["shift"][:, :], v["span"][:, :], v["cum"][:, :], ALU.subtract))
            step.done()
            step(dve.tensor_tensor(v["shift"][:, :], v["shift"][:, :], v["firstf"][:, :], ALU.add))
            step.done()
            wide = (P, IG, NT)
            step(dve.tensor_tensor(w["past"][:, :, :], v["cum"][:, :].unsqueeze(1).to_broadcast(wide),
                                   it["idx"][:, :].unsqueeze(2).to_broadcast(wide), ALU.is_le))
            step.done()
            step(dve.tensor_reduce(it["tile"][:, :], w["past"][:, :, :], AX.X, ALU.add))
            step.done()
            step(dve.tensor_tensor(w["hot"][:, :, :], v["iota25"][:, :].unsqueeze(1).to_broadcast(wide),
                                   it["tile"][:, :].unsqueeze(2).to_broadcast(wide), ALU.is_equal))
            step(dve.tensor_scalar(it["valid"][:, :], it["tile"][:, :], float(NT), None, ALU.is_lt))
            step(dve.tensor_scalar(it["tclamp"][:, :], it["tile"][:, :], float(NT - 1), None, ALU.min))
            step.done()
            step(dve.tensor_tensor(w["pick"][:, :, :], w["hot"][:, :, :],
                                   v["shift"][:, :].unsqueeze(1).to_broadcast(wide), ALU.mult))
            step(dve.tensor_copy(tl_i[:, :], it["tclamp"][:, :]))
            step.done()
            dve.sem_inc(s["rowmade"], 1)
            step(dve.tensor_reduce(it["etile"][:, :], w["pick"][:, :, :], AX.X, ALU.add))
            step.done()
            step(dve.tensor_tensor(it["etile"][:, :], it["etile"][:, :], it["idx"][:, :], ALU.add))
            step.done()
            step(dve.tensor_scalar(it["etile"][:, :], it["etile"][:, :], 0.0, float(ET - 1), ALU.max, ALU.min))
            step.done()
            step(dve.tensor_copy(it_i[:, :], it["etile"][:, :]))
            step(dve.tensor_scalar(it["off"][:, :], it["valid"][:, :], -1.0e6, 1.0e6, ALU.mult, ALU.add))
            step.done()
            dve.sem_inc(s["idx"], 1)
            step(dve.scalar_tensor_tensor(out=it["off"][:, :], in0=it["tclamp"][:, :], scalar=float(P),
                                          in1=it["off"][:, :], op0=ALU.mult, op1=ALU.add))
            step.done()
            dve.wait_ge(s["gathered"], 16 * 3 * IG)
            for j in range(IG):
                step(dve.tensor_copy(recf["src"][0:IP, j, :], rec["src"][0:IP, j, :]))
                step(dve.tensor_copy(recf["dst"][0:IP, j, :], rec["dst"][0:IP, j, :]))
                step.done()
                step(dve.tensor_scalar(recf["dst"][0:IP, j, :], recf["dst"][0:IP, j, :], it["off"][0:IP, j:j + 1],
                                       None, ALU.subtract))
                step.done()
            dve.sem_inc(s["recf"], 1)
            for n, table in enumerate(("item_src", "item_dst", "item_w")):
                dve.wait_ge(s["turned"], n + 1)
                dve.tensor_copy(g[table][:, :], tp[n][:, 0:NI]).then_inc(s["table"], 1)
            dve.wait_ge(s["row_in"], 16)
            step(dve.tensor_copy(tiles_f[:, :], tiles_i[:, :]))
            step.done()
            for n, places_i in g["item_at"].items():
                step(dve.tensor_scalar(places[:, :], tiles_f[:, :], float(n), None, ALU.mult))
                step.done()
                step(dve.tensor_copy(places_i[:, :], places[:, :]))
                step.done()
            dve.wait_ge(s["table"], 3)

        @block.scalar
        def _(act):
            act.wait_ge(s["root"], 1)
            for n in names:
                act.activation(root[n][:, :], root[n][:, :], ACT.Sqrt).then_inc(s["rooted"], 1)

        @block.tensor
        def _(pe):
            blocks = cols // B
            for first, n in ((0, "dst"), (blocks, "src")):
                def body(j, b, u, n=n, first=first):
                    wait(pe, s["hot"], (first + j + 1) * 2)
                    for c in range(B):
                        mm = pe.matmul(deg_ps[n][:, 0:NT], hot_lo[:, u, c, :], hot_hi[:, u, c, :],
                                       start=(isinstance(j, int) and j == 0 and c == 0),
                                       stop=(isinstance(j, int) and j == blocks - 1 and c == B - 1),
                                       skip_group_check=True)
                    mm.then_inc(s["used"], 1)
                each(pe, body, blocks, 2)
                pe.wait_ge(s["used"], first + blocks)
                pe.sem_inc(s["deg"], 1)
            pe.wait_ge(s["idx"], 1)
            pe.matmul(cnt_ps[:, 0:NT], k["ones"][:, :], deg["dst"][:, :], start=True, stop=True).then_inc(s["cnt"], 1)
            pe.wait_ge(s["recf"], 1)
            for n, r in enumerate((recf["src"], recf["dst"], rec["w"])):
                for j in range(IG):
                    tr = pe.transpose(tp[n][:, j * IP:(j + 1) * IP], r[0:IP, j, :], k["ident"][0:IP, 0:IP])
                tr.then_inc(s["turned"], 1)

        @block.gpsimd
        def _(pool):
            pool.iota(v["iota25"][:, :], pattern=[[1, NT]], base=0, channel_multiplier=0,
                      allow_small_or_imprecise_dtypes=True)
            pool.iota(it["idx"][:, :], pattern=[[IP, IG]], base=0, channel_multiplier=1,
                      allow_small_or_imprecise_dtypes=True).then_inc(s["const"], 1)
            pool.wait_ge(s["idx"], 2)
            for j in range(IG):
                for n, e, dt in (("src", "src", I32), ("dst", "dst", I32), ("w", "weight", F32)):
                    pool.indirect_dma_start(
                        out=rec[n][0:IP, j, :], out_offset=None,
                        in_=edges[e].rearrange("(r c) -> r c", c=P),
                        in_offset=bass.IndirectOffsetOnAxis(ap=it_i[0:IP, j:j + 1], axis=0)
                    ).then_inc(s["gathered"], 16)


def aggregate(nc, name, k, g, table, width, acc, weights, factors=None):
    S = 4
    with Phase(nc, name) as ph:
        col = ph.sb("col", [P, S, G], I32)
        dst = ph.sb("dst", [P, S, G])
        wgt = ph.sb("wgt", [P, S, G])
        fac = ph.sb("fac", [P, S, G])
        rows = ph.sb("rows", [P, S, G, width])
        hot = ph.sb("hot", [P, S, G, P])
        out = [ph.ps(f"out{u}") for u in range(2 * G)]
        col_ready, scalars, issued, hot_ready, summed, added, zeroed = (
            ph.sem(n) for n in ("col_ready", "scalars", "issued", "hot_ready", "summed", "added", "zeroed"))
        here = [ph.sem(f"here{u}") for u in range(S)]
        block = ph.block()
        largest = (NT - 1) * acc.shape[2]
        flat = acc[:, :, :].rearrange("p t d -> p (t d)")

        @block.scalar
        def _(act):
            def body(i, b, u):
                wait(act, here[u], b * 16 * G)
                act.activation(col[:, u, :], group(g["item_src"], i), ACT.Copy).then_inc(col_ready, 1)
                wait(act, added, (i + 1 - S) * G)
                act.activation(dst[:, u, :], group(g["item_dst"], i), ACT.Copy)
                scalar = act.activation(wgt[:, u, :], group(weights, i), ACT.Copy)
                if factors is not None:
                    scalar = act.activation(fac[:, u, :], group(factors, i), ACT.Copy)
                scalar.then_inc(scalars, 1)
            each(act, body, NG, S)

        @block.gpsimd
        def _(pool):
            def body(i, b, u):
                wait(pool, col_ready, i + 1)
                wait(pool, summed, i + 1 - S)
                pool.sem_inc(issued, 1)
                for j in range(G):
                    pool.indirect_dma_start(
                        out=rows[:, u, j, :], out_offset=None, in_=table,
                        in_offset=bass.IndirectOffsetOnAxis(ap=col[:, u, j:j + 1], axis=0)).then_inc(here[u], 16)
            each(pool, body, NG, S)

        @block.vector
        def _(dve):
            dve.memset(acc[:, :, :], 0.0).then_inc(zeroed, 1)
            dve.wait_ge(zeroed, 1)

            def body(i, b, u):
                wait(dve, scalars, i + 1)
                wait(dve, summed, i + 1 - S)
                for j in range(G):
                    one_hot = dve.tensor_scalar(hot[:, u, j, :], k["iota"][:, :], dst[:, u, j:j + 1],
                                                wgt[:, u, j:j + 1], ALU.is_equal, ALU.mult)
                one_hot.then_inc(hot_ready, 1)

            def add(i, b, u):
                places = flat_places(nc, mybir.EngineType.DVE, g["item_at"][acc.shape[2]], i * G, G, largest)
                wait(dve, summed, i + 1)
                for j in range(G):
                    total = flat[:, bass.ds(places[j], width)]
                    product = out[u % 2 * G + j][:, 0:width]
                    wait(dve, added, i * G + j)
                    if factors is None:
                        dve.tensor_tensor(total, product, total, ALU.add).then_inc(added, 1)
                    else:
                        dve.scalar_tensor_tensor(out=total, in0=product, scalar=fac[:, u, j:j + 1], in1=total,
                                                 op0=ALU.mult, op1=ALU.add).then_inc(added, 1)
            pipeline(dve, [(body, 0), (add, 2)], NG, S)
            dve.wait_ge(added, NI)

        @block.tensor
        def _(pe):
            def body(i, b, u):
                wait(pe, hot_ready, i + 1)
                wait(pe, added, (i - 1) * G)
                wait(pe, here[u], (b + 1) * 16 * G)
                for j in range(G):
                    mm = pe.matmul(out[u % 2 * G + j][:, 0:width], hot[:, u, j, :], rows[:, u, j, :],
                                   start=True, stop=True)
                mm.then_inc(summed, 1)
            each(pe, body, NG, S)


def layer_stats(nc, name, k, src, mean_rstd, width=D):
    with Phase(nc, name) as ph:
        stats = ph.sb("stats", [P, NT, 6])
        counted, taken, rooted, done = (ph.sem(n) for n in ("counted", "taken", "rooted", "done"))
        block = ph.block()

        @block.vector
        def _(dve):
            for t in range(NT):
                dve.bn_stats(stats[:, t, :], src[:, t, 0:width]).then_inc(counted, 1)
            for t in range(NT):
                dve.wait_ge(counted, t + 1)
                dve.bn_aggr(mean_rstd[:, t, :], stats[:, t, :]).then_inc(taken, 1)
            dve.wait_ge(rooted, 1)
            dve.reciprocal(mean_rstd[:, :, 1], mean_rstd[:, :, 1]).then_inc(done, 1)
            dve.wait_ge(done, 1)

        @block.scalar
        def _(act):
            act.wait_ge(taken, NT)
            act.activation(mean_rstd[:, :, 1], mean_rstd[:, :, 1], ACT.Sqrt, bias=k["eps"][:, 0:1]
                           ).then_inc(rooted, 1)


def first_gnn_weights(nc, t, k, mix, bias, channel_bias, mlp_bias):
    with Phase(nc, "w0") as ph:
        fc = ph.sb("fc", [P, L, KC, D])
        diag = ph.sb("diag", [P, L, KC, D])
        fcb = ph.sb("fcb", [P, L, KC])
        fcb_wide = ph.sb("fcb_wide", [P, L, KC, P])
        mix_ps = [ph.ps(f"mix_ps{j}") for j in range(KC)]
        bias_ps = ph.ps("bias_ps")
        zeroed, loaded, diag_in, wide, made, read, bmade, bread = (
            ph.sem(n) for n in ("zeroed", "loaded", "diag_in", "wide", "made", "read", "bmade", "bread"))
        block = ph.block()

        @block.sync
        def _(sp):
            for l in range(L):
                sp.dma_start(fc[:, l, :, :], t["fc_w"][l].rearrange("(c p) n -> p c n", p=P)).then_inc(loaded, 16)
                sp.dma_start(mix[:, l + 1, :, D:2 * D],
                             t["mlp_wT"][l * D:(l + 1) * D, :].rearrange("(c p) n -> p c n", p=P)
                             ).then_inc(loaded, 16)
                sp.dma_start(channel_bias[:, l, :], bcast(t["ch_b"][l].rearrange("c d -> (c d)"), P)
                             ).then_inc(loaded, 16)
            with nc.allow_non_contiguous_dma(reason="768 words, once"):
                sp.dma_start(fcb[:, :, :], t["fc_b"].rearrange("l (c p) -> p l c", p=P)).then_inc(loaded, 16)
            sp.dma_start(mlp_bias[:, :], bcast(t["mlp_b"], P)).then_inc(loaded, 16)
            sp.wait_ge(zeroed, 1)
            for l in range(L):
                for c in range(C):
                    p0 = (c * DH) % P
                    sp.dma_start(diag[p0:p0 + DH, l, c * DH // P, c * DH:(c + 1) * DH], t["ch_w"][l, c]
                                 ).then_inc(diag_in, 16)
            sp.wait_ge(loaded, 16 * (3 * L + 2))

        @block.gpsimd
        def _(pool):
            pool.memset(diag[:, :, :, :], 0.0).then_inc(zeroed, 1)

        @block.vector
        def _(dve):
            dve.wait_ge(loaded, 16 * (3 * L + 2))
            for l in range(L):
                for c in range(KC):
                    dve.tensor_scalar(fcb_wide[:, l, c, :], k["ones"][:, :], fcb[:, l, c:c + 1], None, ALU.mult
                                      ).then_inc(wide, 1)
            for l in range(L):
                for m in range(KC):
                    dve.wait_ge(made, l * KC + m + 1)
                    dve.tensor_copy(mix[:, l, m, 0:D], mix_ps[m][:, 0:D]).then_inc(read, 1)
                dve.wait_ge(bmade, l + 1)
                dve.tensor_copy(bias[:, l, :], bias_ps[:, 0:D]).then_inc(bread, 1)
            dve.wait_ge(read, L * KC)
            dve.wait_ge(bread, L)

        @block.tensor
        def _(pe):
            pe.wait_ge(loaded, 16 * (3 * L + 2))
            pe.wait_ge(diag_in, 16 * L * C)
            pe.wait_ge(wide, L * KC)
            for l in range(L):
                for m in range(KC):
                    wait(pe, read, (l - 1) * KC + m + 1)
                    for c in range(KC):
                        mm = pe.matmul(mix_ps[m][:, 0:D], fc[:, l, c, m * P:(m + 1) * P], diag[:, l, c, :],
                                       start=(c == 0), stop=(c == KC - 1))
                    mm.then_inc(made, 1)
                wait(pe, bread, l)
                for c in range(KC):
                    mm = pe.matmul(bias_ps[:, 0:D], fcb_wide[:, l, c, :], diag[:, l, c, :],
                                   start=(c == 0), stop=(c == KC - 1))
                mm.then_inc(bmade, 1)


def first_gnn_nodes(nc, l, k, g, x, acc, mix, bias, channel_bias, mlp_bias, table):
    lo, hi = (0 if l < L else D), (D if l == 0 else 2 * D)
    with Phase(nc, f"n{l}") as ph:
        sums = ph.sb("sums", [P, UT, D])
        node = ph.sb("node", [P, UT, D])
        turned = ph.sb("turned", [P, UT, KC, P])
        feat = ph.sb("feat", [P, UT, D])
        row = ph.sb("row", [P, UT, D])
        turn_ps = [ph.ps(f"turn{u}") for u in range(UT)]
        out_ps = [ph.ps(f"out{u}") for u in range(UT)]
        scaled, ready, turn, copied, product, biased, rowed, added = (
            ph.sem(n) for n in ("scaled", "ready", "turn", "copied", "product", "biased", "rowed", "added"))
        stored = [ph.sem(f"stored{u}") for u in range(UT)]
        block = ph.block()
        table_t = table.rearrange("(t p) d -> t p d", p=P)

        @block.vector
        def _(dve):
            def front(t, b, u):
                if l == 0:
                    wait(dve, turn, t + 1 - UT)
                    dve.tensor_scalar(node[:, u, :], tile_of(x, t), stat(g["stats"], t, 0), stat(g["stats"], t, 1),
                                      ALU.subtract, ALU.mult).then_inc(ready, 1)
                else:
                    wait(dve, ready, t + 1 - UT)
                    dve.scalar_tensor_tensor(out=sums[:, u, :], in0=tile_of(acc, t), scalar=g["norm_in"][:, at(t)],
                                             in1=channel_bias[:, l - 1, :], op0=ALU.mult, op1=ALU.add
                                             ).then_inc(scaled, 1)

            def back(t, b, u):
                dve.wait_ge(product, t + 1)
                if l < L:
                    wait(dve, rowed, t + 1 - UT)
                    dve.tensor_tensor(feat[:, u, :], out_ps[u][:, 0:D], bias[:, l, :], ALU.add
                                      ).then_inc(biased, 1)
                if l > 0:
                    xt = tile_of(x, t)
                    dve.tensor_tensor(xt, out_ps[u][:, D:2 * D], xt, ALU.add).then_inc(added, 1)
                if l == L:
                    dve.wait_ge(added, t + 1)
                    dve.tensor_tensor(xt, mlp_bias[:, :], xt, ALU.add).then_inc(biased, 1)

            pipeline(dve, [(front, 0), (back, 3)], NT, UT)
            if l < L:
                dve.wait_ge(biased, NT)
            if l > 0:
                dve.wait_ge(added, NT)

        @block.scalar
        def _(act):
            def front(t, b, u):
                if l > 0:
                    wait(act, scaled, t + 1)
                    wait(act, turn, t + 1 - UT)
                    act.activation(node[:, u, :], sums[:, u, :], ACT.Relu).then_inc(ready, 1)

            def copy(t, b, u):
                wait(act, turn, t + 1)
                wait(act, product, t + 1 - UT)
                act.activation(turned[:, u, :, :].rearrange("p c q -> p (c q)"), turn_ps[u][:, 0:D], ACT.Copy
                               ).then_inc(copied, 1)

            def back(t, b, u):
                if l < L:
                    act.wait_ge(biased, t + 1)
                    wait(act, stored[u], b * 16)
                    act.activation(row[:, u, :], feat[:, u, :], ACT.Copy, scale=g["norm_out"][:, at(t)]
                                   ).then_inc(rowed, 1)

            pipeline(act, [(front, 0), (copy, 1), (back, 3)], NT, UT)

        @block.tensor
        def _(pe):
            def front(t, b, u):
                pe.wait_ge(ready, t + 1)
                wait(pe, copied, t + 1 - UT)
                for c in range(KC):
                    tr = pe.transpose(turn_ps[u][:, c * P:(c + 1) * P], node[:, u, c * P:(c + 1) * P],
                                      k["ident"][:, :])
                tr.then_inc(turn, 1)

            def back(t, b, u):
                pe.wait_ge(copied, t + 1)
                if l < L:
                    wait(pe, biased, t + 1 - UT)
                if l > 0:
                    wait(pe, added, t + 1 - UT)
                for c in range(KC):
                    mm = pe.matmul(out_ps[u][:, lo:hi], turned[:, u, c, :], mix[:, l, c, lo:hi],
                                   start=(c == 0), stop=(c == KC - 1))
                mm.then_inc(product, 1)

            pipeline(pe, [(front, 0), (back, 1)], NT, UT)

        if l < L:
            @block.sync
            def _(sp):
                def body(t, b, u):
                    wait(sp, rowed, t + 1)
                    sp.dma_start(table_t[at(t), :, :].rearrange("a p d -> (a p) d"), row[:, u, :]
                                 ).then_inc(stored[u], 16)
                each(sp, body, NT, UT)
                for u in range(UT):
                    sp.wait_ge(stored[u], 16 * ((NT - 1 - u) // UT + 1))


def normalised_columns(nc, name, k, x, stats, xT, score, score_w, score_b, gamma=None, beta=None, add_back=False):
    n = score.shape[2]
    with Phase(nc, name) as ph:
        node = ph.sb("node", [P, UT, D])
        turned = ph.sb("turned", [P, UT, KC, P])
        w = ph.sb("w", [P, KC, n])
        b_wide = ph.sb("b_wide", [P, n])
        affine = ph.sb("affine", [P, 2, KC])
        turn_ps = [ph.ps(f"turn{u}") for u in range(UT)]
        score_ps = [ph.ps(f"score{u}") for u in range(UT)]
        loaded, ready, turn, copied, kept, scored, taken, summed = (
            ph.sem(s) for s in ("loaded", "ready", "turn", "copied", "kept", "scored", "taken", "summed"))
        loads = 2 if gamma is None else 4
        block = ph.block()

        @block.sync
        def _(sp):
            with nc.allow_non_contiguous_dma(reason="few words, once"):
                sp.dma_start(w[:, :, :], score_w.rearrange("(c p) n -> p c n", p=P)).then_inc(loaded, 16)
                sp.dma_start(b_wide[:, :], bcast(score_b, P)).then_inc(loaded, 16)
                if gamma is not None:
                    sp.dma_start(affine[:, 0, :], gamma.rearrange("(c p) -> p c", p=P)).then_inc(loaded, 16)
                    sp.dma_start(affine[:, 1, :], beta.rearrange("(c p) -> p c", p=P)).then_inc(loaded, 16)

        @block.vector
        def _(dve):
            def front(t, b, u):
                wait(dve, turn, t + 1 - UT)
                dve.tensor_scalar(node[:, u, :], tile_of(x, t), stat(stats, t, 0), stat(stats, t, 1),
                                  ALU.subtract, ALU.mult).then_inc(ready, 1)
                if add_back:
                    dve.wait_ge(ready, t + 1)
                    dve.tensor_tensor(tile_of(x, t), tile_of(x, t), node[:, u, :], ALU.add).then_inc(summed, 1)

            def back(t, b, u):
                dve.wait_ge(scored, t + 1)
                dve.tensor_tensor(tile_of(score, t), score_ps[u][:, 0:n], b_wide[:, :], ALU.add
                                  ).then_inc(taken, 1)
            dve.wait_ge(loaded, 16 * loads)
            pipeline(dve, [(front, 0), (back, 2)], NT, UT)
            dve.wait_ge(taken, NT)
            if add_back:
                dve.wait_ge(summed, NT)

        @block.scalar
        def _(act):
            act.wait_ge(loaded, 16 * loads)

            def body(t, b, u):
                act.wait_ge(turn, t + 1)
                wait(act, scored, t + 1 - UT)
                wait(act, kept, t + 1 - UT)
                if gamma is None:
                    act.activation(turned[:, u, :, :].rearrange("p c q -> p (c q)"), turn_ps[u][:, 0:D], ACT.Copy
                                   ).then_inc(copied, 1)
                else:
                    for c in range(KC):
                        ins = act.activation(turned[:, u, c, :], turn_ps[u][:, c * P:(c + 1) * P], ACT.Identity,
                                             scale=affine[:, 0, c:c + 1], bias=affine[:, 1, c:c + 1])
                    ins.then_inc(copied, 1)
            each(act, body, NT, UT)

        @block.gpsimd
        def _(pool):
            def body(t, b, u):
                wait(pool, copied, t + 1)
                pool.tensor_copy(xT[:, :, bass.ds(t * P, P)], turned[:, u, :, :]).then_inc(kept, 1)
            each(pool, body, NT, UT)
            pool.wait_ge(kept, NT)

        @block.tensor
        def _(pe):
            pe.wait_ge(loaded, 16 * loads)

            def front(t, b, u):
                pe.wait_ge(ready, t + 1)
                wait(pe, copied, t + 1 - UT)
                for c in range(KC):
                    tr = pe.transpose(turn_ps[u][:, c * P:(c + 1) * P], node[:, u, c * P:(c + 1) * P],
                                      k["ident"][:, :])
                tr.then_inc(turn, 1)

            def back(t, b, u):
                pe.wait_ge(copied, t + 1)
                wait(pe, taken, t + 1 - UT)
                for c in range(KC):
                    mm = pe.matmul(score_ps[u][:, 0:n], turned[:, u, c, :], w[:, c, :],
                                   start=(c == 0), stop=(c == KC - 1))
                mm.then_inc(scored, 1)
            pipeline(pe, [(front, 0), (back, 1)], NT, UT)


def apply_norm(nc, name, src, stats, out):
    with Phase(nc, name) as ph:
        done = ph.sem("done")
        block = ph.block()

        @block.vector
        def _(dve):
            def body(t, b, u):
                dve.tensor_scalar(tile_of(out, t), tile_of(src, t), stat(stats, t, 0), stat(stats, t, 1),
                                  ALU.subtract, ALU.mult).then_inc(done, 1)
            each(dve, body, NT, UT)
            dve.wait_ge(done, NT)


ST = 2 * NT + NE - 1
HM = H // P


def expert_rows(nc, k, t, x, stats, logits, w):
    with Phase(nc, "rows") as ph:
        node = ph.sb("node", [P, UT, D])
        scaled = ph.sb("scaled", [P, UT, D])
        row = ph.sb("row", [P, UT, D])
        turned = ph.sb("turned", [P, UT, KC, P])
        wr = ph.sb("wr", [P, KC, NE])
        br = ph.sb("br", [P, NE])
        affine = ph.sb("affine", [P, 2, D])
        zeros = ph.sb("zeros", [P, D])
        turn_ps = [ph.ps(f"turn{u}") for u in range(UT)]
        score_ps = [ph.ps(f"score{u}") for u in range(UT)]
        loaded, zeroed, ready, gained, rowed, turn, copied, kept, scored, taken = (
            ph.sem(s) for s in ("loaded", "zeroed", "ready", "gained", "rowed", "turn", "copied", "kept", "scored",
                                "taken"))
        block = ph.block()

        @block.sync
        def _(sp):
            with nc.allow_non_contiguous_dma(reason="few words, once"):
                sp.dma_start(wr[:, :, :], t["Wr"].rearrange("(c p) n -> p c n", p=P)).then_inc(loaded, 16)
                sp.dma_start(br[:, :], bcast(t["br"], P)).then_inc(loaded, 16)
            sp.dma_start(affine[:, 0, :], bcast(t["gamma"], P)).then_inc(loaded, 16)
            sp.dma_start(affine[:, 1, :], bcast(t["beta"], P)).then_inc(loaded, 16)
            sp.wait_ge(zeroed, 1)
            sp.dma_start(w["slot_rows"].rearrange("(s p) d -> p s d", p=P),
                         zeros[:, :].unsqueeze(1).to_broadcast((P, ST, D))).then_inc(w["cleared"], 16)
            for e in range(NE):
                sp.dma_start(w["w1"][:, e, :, :], t["W1"][e].rearrange("(c p) n -> p c n", p=P)
                             ).then_inc(w["here"], 16)
                sp.dma_start(w["w2"][:, e, :, :], t["W2"][e].rearrange("(m p) n -> p m n", p=P)
                             ).then_inc(w["here"], 16)
            sp.dma_start(w["b1"][:, :], bcast(t["b1"].rearrange("e n -> (e n)"), P)).then_inc(w["here"], 16)
            sp.dma_start(w["b2"][:, :], bcast(t["b2"].rearrange("e n -> (e n)"), P)).then_inc(w["here"], 16)
            sp.wait_ge(w["cleared"], 16)

        @block.vector
        def _(dve):
            dve.memset(zeros[:, :], 0.0).then_inc(zeroed, 1)

            def front(i, b, u):
                wait(dve, gained, i + 1 - UT)
                dve.tensor_scalar(node[:, u, :], tile_of(x, i), stat(stats, i, 0), stat(stats, i, 1),
                                  ALU.subtract, ALU.mult).then_inc(ready, 1)

            def mid(i, b, u):
                dve.wait_ge(gained, i + 1)
                wait(dve, turn, i + 1 - UT)
                wait(dve, kept, i + 1 - UT)
                dve.tensor_tensor(row[:, u, :], scaled[:, u, :], affine[:, 1, :], ALU.add).then_inc(rowed, 1)

            def back(i, b, u):
                dve.wait_ge(scored, i + 1)
                dve.tensor_tensor(tile_of(logits, i), score_ps[u][:, 0:NE], br[:, :], ALU.add).then_inc(taken, 1)
            dve.wait_ge(loaded, 64)
            pipeline(dve, [(back, 3), (front, 0), (mid, 1)], NT, UT)
            dve.wait_ge(taken, NT)

        @block.gpsimd
        def _(pool):
            pool.wait_ge(loaded, 64)

            def body(i, b, u):
                pool.wait_ge(ready, i + 1)
                wait(pool, rowed, i + 1 - UT)
                pool.tensor_tensor(scaled[:, u, :], node[:, u, :], affine[:, 0, :], ALU.mult).then_inc(gained, 1)
            each(pool, body, NT, UT)

        @block.scalar
        def _(act):
            def keep(i, b, u):
                act.wait_ge(rowed, i + 1)
                act.activation(tile_of(x, i), row[:, u, :], ACT.Copy).then_inc(kept, 1)

            def body(i, b, u):
                act.wait_ge(turn, i + 1)
                wait(act, scored, i + 1 - UT)
                act.activation(turned[:, u, :, :].rearrange("p c q -> p (c q)"), turn_ps[u][:, 0:D], ACT.Copy
                               ).then_inc(copied, 1)
            pipeline(act, [(body, 1), (keep, 0)], NT, UT)
            act.wait_ge(kept, NT)

        @block.tensor
        def _(pe):
            pe.wait_ge(loaded, 64)

            def front(i, b, u):
                pe.wait_ge(rowed, i + 1)
                wait(pe, copied, i + 1 - UT)
                for c in range(KC):
                    tr = pe.transpose(turn_ps[u][:, c * P:(c + 1) * P], row[:, u, c * P:(c + 1) * P],
                                      k["ident"][:, :])
                tr.then_inc(turn, 1)

            def back(i, b, u):
                pe.wait_ge(copied, i + 1)
                wait(pe, taken, i + 1 - UT)
                for c in range(KC):
                    mm = pe.matmul(score_ps[u][:, 0:NE], turned[:, u, c, :], wr[:, c, :],
                                   start=(c == 0), stop=(c == KC - 1))
                mm.then_inc(scored, 1)
            pipeline(pe, [(front, 0), (back, 1)], NT, UT)


def route_two(nc, k, logits, share, slot, places):
    with Phase(nc, "route") as ph:
        wide, turned = [P, NT, NE], [P, NE, NT]
        left = ph.sb("left", wide)
        best = ph.sb("best", wide)
        hot = [ph.sb(f"hot{j}", wide) for j in range(2)]
        rest = ph.sb("rest", wide)
        top = [ph.sb(f"top{j}", [P, NT]) for j in range(2)]
        pick = ph.sb("pick", [P, NT])
        ex = ph.sb("ex", [P, NT])
        found = ph.sb("found", [P, NT])
        both = ph.sb("both", turned)
        zero = ph.sb("zero", turned)
        totals = ph.sb("totals", turned)
        begun = ph.sb("begun", turned)
        spot = ph.sb("spot", turned)
        e8 = {n: ph.sb(n, [P, NE]) for n in ("count", "ceil", "tiles", "cum", "cumcount", "shift")}
        e8_i = ph.sb("e8_i", [P, NE], I32)
        tile_iota = ph.sb("tile_iota", [P, ST])
        past = ph.sb("past", [P, ST, NE])
        expert = ph.sb("expert", [P, ST])
        offsets = ph.sb("offsets", [P, ST, 3])
        below = ph.sb("below", [P, P])
        total_ps = ph.ps("total_ps")
        within_ps = ph.ps("within_ps")
        own, made, diff, exped, pairs, summed = (
            ph.sem(n) for n in ("own", "made", "diff", "exped", "pairs", "summed"))
        block = ph.block()
        spread = lambda a: a.unsqueeze(2).to_broadcast(tuple(wide))
        flat = lambda a: a[:, :, :].rearrange("p e t -> p (e t)")

        @block.gpsimd
        def _(pool):
            pool.iota(left[:, :, :], pattern=[[0, NT], [-1, NE]], base=NE, channel_multiplier=0,
                      allow_small_or_imprecise_dtypes=True).then_inc(made, 1)
            pool.iota(tile_iota[:, :], pattern=[[1, ST]], base=0, channel_multiplier=0,
                      allow_small_or_imprecise_dtypes=True).then_inc(made, 1)
            pool.affine_select(out=below[:, :], in_=k["ones"][:, :], compare_op=ALU.is_ge, fill=0.0,
                               base=-1, pattern=[[1, P]], channel_multiplier=-1).then_inc(made, 1)

        @block.tensor
        def _(pe):
            pe.wait_ge(made, 3)
            pe.wait_ge(pairs, 1)
            pe.matmul(total_ps[:, 0:NE * NT], k["ones"][:, :], flat(both), start=True, stop=True
                      ).then_inc(summed, 1)
            pe.matmul(within_ps[:, 0:NE * NT], below[:, :], flat(both), start=True, stop=True
                      ).then_inc(summed, 1)

        @block.vector
        def _(dve):
            step = Steps(dve, own)

            def run(instruction):
                step(instruction)
                step.done()
            dve.wait_ge(made, 3)
            for j, given in enumerate((logits, rest)):
                run(dve.tensor_reduce(top[j][:, :], given[:, :, :], AX.X, ALU.max))
                run(dve.tensor_tensor(best[:, :, :], given[:, :, :], spread(top[j][:, :]), ALU.is_equal))
                run(dve.tensor_tensor(best[:, :, :], best[:, :, :], left[:, :, :], ALU.mult))
                run(dve.tensor_reduce(pick[:, :], best[:, :, :], AX.X, ALU.max))
                run(dve.tensor_tensor(hot[j][:, :, :], best[:, :, :], spread(pick[:, :]), ALU.is_equal))
                if j == 0:
                    run(dve.scalar_tensor_tensor(out=rest[:, :, :], in0=hot[0][:, :, :], scalar=-3.0e38,
                                                 in1=logits[:, :, :], op0=ALU.mult, op1=ALU.add))
            run(dve.tensor_tensor(both[:, :, :].rearrange("p e t -> p t e"), hot[0][:, :, :], hot[1][:, :, :],
                                  ALU.add))
            dve.sem_inc(pairs, 1)
            run(dve.tensor_tensor(pick[:, :], top[1][:, :], top[0][:, :], ALU.subtract))
            dve.sem_inc(diff, 1)
            run(dve.memset(zero[:, :, :], 0.0))
            dve.wait_ge(summed, 2)
            run(dve.tensor_copy(flat(totals), total_ps[:, 0:NE * NT]))
            run(dve.tensor_tensor_scan(flat(begun), flat(totals), flat(zero), 0.0, ALU.add, ALU.add))
            run(dve.tensor_tensor(flat(spot), flat(begun), flat(totals), ALU.subtract))
            run(dve.tensor_tensor(flat(spot), flat(spot), within_ps[:, 0:NE * NT], ALU.add))
            run(dve.tensor_reduce(e8["count"][:, :], totals[:, :, :], AX.X, ALU.add))
            run(dve.tensor_scalar(e8["ceil"][:, :], e8["count"][:, :], float(P - 1), None, ALU.add))
            run(dve.tensor_copy(e8_i[:, :], e8["ceil"][:, :]))
            run(dve.tensor_scalar(e8_i[:, :], e8_i[:, :], 7, None, ALU.arith_shift_right))
            run(dve.tensor_copy(e8["tiles"][:, :], e8_i[:, :]))
            none = zero[:, :, 0:1].rearrange("p e a -> p (e a)")
            run(dve.tensor_tensor_scan(e8["cum"][:, :], e8["tiles"][:, :], none, 0.0, ALU.add, ALU.add))
            run(dve.tensor_tensor_scan(e8["cumcount"][:, :], e8["count"][:, :], none, 0.0, ALU.add, ALU.add))
            run(dve.tensor_tensor(e8["shift"][:, :], e8["cum"][:, :], e8["tiles"][:, :], ALU.subtract))
            run(dve.scalar_tensor_tensor(out=e8["shift"][:, :], in0=e8["shift"][:, :], scalar=float(P),
                                         in1=e8["cumcount"][:, :], op0=ALU.mult, op1=ALU.subtract))
            run(dve.tensor_tensor(e8["shift"][:, :], e8["shift"][:, :], e8["count"][:, :], ALU.add))
            run(dve.tensor_tensor(spot[:, :, :], spot[:, :, :],
                                  e8["shift"][:, :].unsqueeze(2).to_broadcast(tuple(turned)), ALU.add))
            for j in range(2):
                run(dve.tensor_tensor(best[:, :, :], hot[j][:, :, :], spot[:, :, :].rearrange("p e t -> p t e"),
                                      ALU.mult))
                run(dve.tensor_reduce(found[:, :], best[:, :, :], AX.X, ALU.add))
                run(dve.tensor_copy(slot[:, :, j:j + 1].rearrange("p t a -> p (t a)"), found[:, :]))
            many = (P, ST, NE)
            run(dve.tensor_tensor(past[:, :, :], e8["cum"][:, :].unsqueeze(1).to_broadcast(many),
                                  tile_iota[:, :].unsqueeze(2).to_broadcast(many), ALU.is_le))
            run(dve.tensor_reduce(expert[:, :], past[:, :, :], AX.X, ALU.add))
            for j, size in enumerate((KC * H, H, D)):
                run(dve.tensor_scalar(offsets[:, :, j:j + 1].rearrange("p s a -> p (s a)"), expert[:, :],
                                      float(NE - 1), float(size), ALU.min, ALU.mult))
            run(dve.tensor_copy(places[:, :], offsets[0:1, :, :].rearrange("p s a -> p (s a)")))
            dve.wait_ge(exped, 1)
            shares = [share[:, :, j:j + 1].rearrange("p t a -> p (t a)") for j in range(2)]
            run(dve.tensor_scalar(pick[:, :], ex[:, :], 1.0, None, ALU.add))
            run(dve.reciprocal(shares[0], pick[:, :]))
            run(dve.tensor_tensor(shares[1], ex[:, :], shares[0], ALU.mult))

        @block.scalar
        def _(act):
            act.wait_ge(diff, 1)
            act.activation(ex[:, :], pick[:, :], ACT.Exp).then_inc(exped, 1)
            act.wait_ge(exped, 1)


def scatter_rows(nc, xn, slot, slot_rows):
    with Phase(nc, "scatter") as ph:
        row = ph.sb("row", [P, UT, D])
        col = ph.sb("col", [P, UT, 2], I32)
        ready, issued = ph.sem("ready"), ph.sem("issued")
        sent = [ph.sem(f"sent{u}") for u in range(UT)]
        block = ph.block()

        @block.scalar
        def _(act):
            def body(i, b, u):
                wait(act, sent[u], b * 32)
                act.activation(col[:, u, :], slot[:, at(i), :].rearrange("p a j -> p (a j)"), ACT.Copy)
                act.activation(row[:, u, :], tile_of(xn, i), ACT.Copy).then_inc(ready, 1)
            each(act, body, NT, UT)

        @block.gpsimd
        def _(pool):
            def body(i, b, u):
                wait(pool, ready, i + 1)
                pool.sem_inc(issued, 1)
                for j in range(2):
                    pool.indirect_dma_start(
                        out=slot_rows, out_offset=bass.IndirectOffsetOnAxis(ap=col[:, u, j:j + 1], axis=0),
                        in_=row[:, u, :], in_offset=None).then_inc(sent[u], 16)
            each(pool, body, NT, UT)
            for u in range(UT):
                pool.wait_ge(sent[u], 32 * ((NT - 1 - u) // UT + 1))


def routed_experts(nc, k, w, places, y_rows):
    S = 4
    with Phase(nc, "moe") as ph:
        row = ph.sb("row", [P, S, D])
        rowT = ph.sb("rowT", [P, 2, KC, P])
        biased = ph.sb("biased", [P, 2, H])
        hidden = ph.sb("hidden", [P, 2, H])
        hiddenT = ph.sb("hiddenT", [P, 2, HM, P])
        y = ph.sb("y", [P, S, D])
        rowT_ps, h_ps, hiddenT_ps, y_ps = ([ph.ps(f"{n}{j}") for j in range(2)]
                                           for n in ("rowT_ps", "h_ps", "hiddenT_ps", "y_ps"))
        s = {n: ph.sem(n) for n in ("turned", "copied", "up", "biased", "active", "hturned", "hcopied", "down",
                                    "done")}
        here = [ph.sem(f"here{u}") for u in range(S)]
        stored = [ph.sem(f"stored{u}") for u in range(S)]
        block = ph.block()
        slots = w["slot_rows"].rearrange("(s p) d -> s p d", p=P)
        outs = y_rows.rearrange("(s p) d -> s p d", p=P)
        w1 = w["w1"][:, :, :, :].rearrange("p e c n -> p (e c n)")
        w2 = w["w2"][:, :, :, :].rearrange("p e m n -> p (e m n)")
        LARGEST = (NE - 1) * KC * H

        @block.sync
        def _(sp):
            def load(i, b, u):
                wait(sp, s["turned"], i + 1 - S)
                sp.dma_start(row[:, u, :], slots[at(i), :, :].rearrange("a p d -> (a p) d")).then_inc(here[u], 16)

            def store(i, b, u):
                sp.wait_ge(s["done"], i + 1)
                sp.dma_start(outs[at(i), :, :].rearrange("a p d -> (a p) d"), y[:, u, :]).then_inc(stored[u], 16)
            pipeline(sp, [(load, 0), (store, 5)], ST, S)
            for u in range(S):
                sp.wait_ge(stored[u], 16 * ((ST - 1 - u) // S + 1))

        @block.tensor
        def _(pe):
            def turn_row(i, b, u):
                pe.wait_ge(here[u], (b + 1) * 16)
                wait(pe, s["copied"], i - 1)
                for c in range(KC):
                    tr = pe.transpose(rowT_ps[u % 2][:, c * P:(c + 1) * P], row[:, u, c * P:(c + 1) * P],
                                      k["ident"][:, :])
                tr.then_inc(s["turned"], 1)

            def up(i, b, u):
                at_w = flat_places(nc, mybir.EngineType.PE, places, i * 3, 1, LARGEST)[0]
                pe.wait_ge(s["copied"], i + 1)
                wait(pe, s["biased"], i - 1)
                for c in range(KC):
                    mm = pe.matmul(h_ps[u % 2][:, :], rowT[:, u % 2, c, :], w1[:, bass.ds(at_w + c * H, H)],
                                   start=(c == 0), stop=(c == KC - 1))
                mm.then_inc(s["up"], 1)

            def turn_hidden(i, b, u):
                pe.wait_ge(s["active"], i + 1)
                wait(pe, s["hcopied"], i - 1)
                for m in range(HM):
                    tr = pe.transpose(hiddenT_ps[u % 2][:, m * P:(m + 1) * P], hidden[:, u % 2, m * P:(m + 1) * P],
                                      k["ident"][:, :])
                tr.then_inc(s["hturned"], 1)

            def down(i, b, u):
                at_w = flat_places(nc, mybir.EngineType.PE, places, i * 3, 1, LARGEST)[0]
                pe.wait_ge(s["hcopied"], i + 1)
                wait(pe, s["done"], i - 1)
                for m in range(HM):
                    mm = pe.matmul(y_ps[u % 2][:, 0:D], hiddenT[:, u % 2, m, :], w2[:, bass.ds(at_w + m * D, D)],
                                   start=(m == 0), stop=(m == HM - 1))
                mm.then_inc(s["down"], 1)
            pe.wait_ge(w["here"], 16 * (2 * NE + 2))
            pipeline(pe, [(up, 1), (down, 3), (turn_row, 0), (turn_hidden, 2)], ST, S)

        @block.scalar
        def _(act):
            def activate(i, b, u):
                act.wait_ge(s["biased"], i + 1)
                wait(act, s["hturned"], i - 1)
                act.activation(hidden[:, u % 2, :], biased[:, u % 2, :], ACT.Gelu).then_inc(s["active"], 1)

            def copy_row(i, b, u):
                act.wait_ge(s["turned"], i + 1)
                act.activation(rowT[:, u % 2, :, :].rearrange("p c q -> p (c q)"), rowT_ps[u % 2][:, 0:D],
                               ACT.Copy).then_inc(s["copied"], 1)

            def copy_hidden(i, b, u):
                act.wait_ge(s["hturned"], i + 1)
                act.activation(hiddenT[:, u % 2, :, :].rearrange("p m q -> p (m q)"), hiddenT_ps[u % 2][:, :],
                               ACT.Copy).then_inc(s["hcopied"], 1)
            pipeline(act, [(activate, 1), (copy_row, 0), (copy_hidden, 2)], ST, S)

        @block.vector
        def _(dve):
            def bias(i, b, u):
                at_b = flat_places(nc, mybir.EngineType.DVE, places, i * 3 + 1, 1, (NE - 1) * H)[0]
                dve.wait_ge(s["up"], i + 1)
                wait(dve, s["active"], i - 1)
                dve.tensor_tensor(biased[:, u % 2, :], h_ps[u % 2][:, :], w["b1"][:, bass.ds(at_b, H)], ALU.add
                                  ).then_inc(s["biased"], 1)

            def finish(i, b, u):
                at_b = flat_places(nc, mybir.EngineType.DVE, places, i * 3 + 2, 1, (NE - 1) * D)[0]
                dve.wait_ge(s["down"], i + 1)
                wait(dve, stored[u], b * 16)
                dve.tensor_tensor(y[:, u, :], y_ps[u % 2][:, 0:D], w["b2"][:, bass.ds(at_b, D)], ALU.add
                                  ).then_inc(s["done"], 1)
            dve.wait_ge(w["here"], 16 * (2 * NE + 2))
            pipeline(dve, [(bias, 1), (finish, 3)], ST, S)


def gather_experts(nc, x, share, slot, y_rows):
    with Phase(nc, "back") as ph:
        col = ph.sb("col", [P, UT, 2], I32)
        got = ph.sb("got", [P, UT, 2, D])
        ready, issued, added = ph.sem("ready"), ph.sem("issued"), ph.sem("added")
        here = [ph.sem(f"here{u}") for u in range(UT)]
        block = ph.block()

        @block.scalar
        def _(act):
            def body(i, b, u):
                wait(act, here[u], b * 32)
                act.activation(col[:, u, :], slot[:, at(i), :].rearrange("p a j -> p (a j)"), ACT.Copy
                               ).then_inc(ready, 1)
            each(act, body, NT, UT)

        @block.gpsimd
        def _(pool):
            def body(i, b, u):
                wait(pool, ready, i + 1)
                wait(pool, added, 2 * (i + 1 - UT))
                pool.sem_inc(issued, 1)
                for j in range(2):
                    pool.indirect_dma_start(
                        out=got[:, u, j, :], out_offset=None, in_=y_rows,
                        in_offset=bass.IndirectOffsetOnAxis(ap=col[:, u, j:j + 1], axis=0)).then_inc(here[u], 16)
            each(pool, body, NT, UT)

        @block.vector
        def _(dve):
            def body(i, b, u):
                wait(dve, here[u], (b + 1) * 32)
                for j in range(2):
                    wait(dve, added, 2 * i + j)
                    dve.scalar_tensor_tensor(out=tile_of(x, i), in0=got[:, u, j, :], scalar=stat(share, i, j),
                                             in1=tile_of(x, i), op0=ALU.mult, op1=ALU.add).then_inc(added, 1)
            each(dve, body, NT, UT)
            dve.wait_ge(added, 2 * NT)


def choose_half(nc, k, row_dram, weight, coef, chosen):
    with Phase(nc, "rank") as ph:
        wide = ph.sb("wide", [P, NP])
        junk = ph.sb("junk", [P, NP])
        before = ph.sb("before", [P, P])
        parts = ph.sb("parts", [P, NT, 4])
        rank = ph.sb("rank", [P, NT])
        out, here, made, zeroed, counted, own = (
            ph.sem(n) for n in ("out", "here", "made", "zeroed", "counted", "own"))
        block = ph.block()

        @block.sync
        def _(sp):
            with nc.allow_non_contiguous_dma(reason="3200 words, once"):
                sp.dma_start(row_dram.rearrange("(t p) -> p t", p=P), weight[:, :, 0]).then_inc(out, 16)
            sp.wait_ge(out, 16)
            sp.dma_start(wide[:, :], bcast(row_dram, P)).then_inc(here, 16)

        @block.gpsimd
        def _(pool):
            pool.affine_select(out=before[:, :], in_=k["ones"][:, :], compare_op=ALU.is_ge, fill=0.0,
                               base=-1, pattern=[[-1, P]], channel_multiplier=1).then_inc(made, 1)

        @block.vector
        def _(dve):
            step = Steps(dve, own)
            dve.memset(parts[:, :, :], 0.0).then_inc(zeroed, 1)
            dve.wait_ge(zeroed, 1)
            dve.wait_ge(here, 16)
            dve.wait_ge(made, 1)
            for t in range(NT):
                mine = weight[:, t, :]
                lo, hi = t * P, min((t + 1) * P, N)
                for j, (a, b, op) in enumerate(((0, lo, ALU.is_ge), (lo, N, ALU.is_gt))):
                    if b > a:
                        step.done() if step.n else None
                        step(dve.tensor_scalar(junk[:, a:b], wide[:, a:b], mine, None, op, ALU.add,
                                               accum_out=parts[:, t, j:j + 1]))
                step.done()
                step(dve.scalar_tensor_tensor(out=junk[:, lo:hi], in0=wide[:, lo:hi], scalar=mine,
                                              in1=before[:, 0:hi - lo], op0=ALU.is_equal, op1=ALU.mult,
                                              accum_out=parts[:, t, 2:3]))
            step.done()
            step(dve.tensor_reduce(rank[:, :], parts[:, :, :], AX.X, ALU.add))
            step.done()
            step(dve.scalar_tensor_tensor(out=coef[:, 0, :], in0=rank[:, :], scalar=float(chosen),
                                          in1=weight[:, :, 0], op0=ALU.is_lt, op1=ALU.mult))
            step.done()


def experts(nc, name, k, xT, x, coef, coef_of, w1, b1, w2, b2, count, gelu):
    FIFTH = 5
    TU = NT // FIFTH
    HALF = TU * P // 2
    HM = H // P
    UNITS = 2 * FIFTH
    with Phase(nc, name) as ph:
        w1_s = ph.sb("w1", [P, 2, KC, H])
        w2_s = ph.sb("w2", [P, 2, HM, D])
        b1_s = ph.sb("b1", [P, 2, HM])
        b2_s = ph.sb("b2", [P, 2, D])
        hidden = ph.sb("hidden", [P, 2, HM, TU * P])
        h_ps = [ph.ps(f"h{j}") for j in range(4)]
        y_ps = [ph.ps(f"y{j}") for j in range(4)]
        product, active, y_done, y_added, biased = (
            ph.sem(n) for n in ("product", "active", "y_done", "y_added", "biased"))
        here = [ph.sem(f"here{j}") for j in range(2)]
        block = ph.block()

        @block.sync
        def _(sp):
            def body(e, b, u):
                wait(sp, y_added, (e - 1) * FIFTH * TU)
                sp.dma_start(w1_s[:, u, :, :], w1(e)).then_inc(here[u], 16)
                sp.dma_start(w2_s[:, u, :, :], w2(e)).then_inc(here[u], 16)
                with nc.allow_non_contiguous_dma(reason="512 words for each block"):
                    sp.dma_start(b1_s[:, u, :], b1(e)).then_inc(here[u], 16)
                sp.dma_start(b2_s[:, u, :], b2(e)).then_inc(here[u], 16)
            each(sp, body, count, 2)

        @block.tensor
        def _(pe):
            def up(i, b, u):
                es, c = divmod(u, FIFTH)
                pe.wait_ge(here[es], (b + 1) * 64)
                for n in range(2 * HM):
                    m, half = divmod(n, 2)
                    wait(pe, active, i * 2 * HM + (n + 1 - 4))
                    for kc in range(KC):
                        mm = pe.matmul(h_ps[n % 4][:, 0:HALF], w1_s[:, es, kc, m * P:(m + 1) * P],
                                       xT[:, kc, c * TU * P + half * HALF:c * TU * P + (half + 1) * HALF],
                                       start=(kc == 0), stop=(kc == KC - 1))
                    mm.then_inc(product, 1)

            def down(i, b, u):
                es, c = divmod(u, FIFTH)
                pe.wait_ge(active, (i + 1) * 2 * HM)
                for j in range(TU):
                    n = (u * TU + j) % 4
                    wait(pe, y_added, i * TU + (j - 1) if u == 0 and j < 4 else i * TU + (j + 1 - 4))
                    for m in range(HM):
                        mm = pe.matmul(y_ps[n][:, 0:D], hidden[:, u % 2, m, j * P:(j + 1) * P],
                                       w2_s[:, es, m, :], start=(m == 0), stop=(m == HM - 1))
                    mm.then_inc(y_done, 1)
            pipeline(pe, [(up, 0), (down, 1)], count * FIFTH, UNITS)

        @block.scalar
        def _(act):
            def body(i, b, u):
                es, c = divmod(u, FIFTH)
                act.wait_ge(here[es], (b + 1) * 64)
                wait(act, y_done, (i - 1) * TU)
                for n in range(2 * HM):
                    m, half = divmod(n, 2)
                    act.wait_ge(product, i * 2 * HM + (n + 1))
                    act.activation(hidden[:, u % 2, m, half * HALF:(half + 1) * HALF], h_ps[n % 4][:, 0:HALF],
                                   gelu, bias=b1_s[:, es, m:m + 1]).then_inc(active, 1)
            each(act, body, count * FIFTH, UNITS)

        @block.vector
        def _(dve):
            def body(i, b, u):
                es, c = divmod(u, FIFTH)
                dve.wait_ge(here[es], (b + 1) * 64)
                for j in range(TU):
                    t, n = c * TU + j, (u * TU + j) % 4
                    weight = coef_of(b * 2 + es, t)
                    wait(dve, y_added, i * TU + j)
                    dve.scalar_tensor_tensor(out=x[:, t, :], in0=b2_s[:, es, :], scalar=weight, in1=x[:, t, :],
                                             op0=ALU.mult, op1=ALU.add).then_inc(biased, 1)
                    dve.wait_ge(biased, i * TU + (j + 1))
                    dve.wait_ge(y_done, i * TU + (j + 1))
                    dve.scalar_tensor_tensor(out=x[:, t, :], in0=y_ps[n][:, 0:D], scalar=weight, in1=x[:, t, :],
                                             op0=ALU.mult, op1=ALU.add).then_inc(y_added, 1)
            each(dve, body, count * FIFTH, UNITS)
            dve.wait_ge(y_added, count * FIFTH * TU)


PRE = D + KD + 2


def second_gnn_nodes(nc, k, t, x, stats, pre, wide_table):
    small = PRE - D
    with Phase(nc, "pre") as ph:
        w = ph.sb("w", [P, KC, PRE])
        b_wide = ph.sb("b_wide", [P, PRE])
        node = ph.sb("node", [P, UT, D])
        turned = ph.sb("turned", [P, UT, KC, P])
        row = ph.sb("row", [P, UT, T3])
        turn_ps = [ph.ps(f"turn{u}") for u in range(UT)]
        out_ps = [ph.ps(f"out{u}") for u in range(UT)]
        zeroed, set_, loaded, ready, turn, copied, product, biased, taken = (
            ph.sem(n) for n in ("zeroed", "set", "loaded", "ready", "turn", "copied", "product", "biased", "taken"))
        stored = [ph.sem(f"stored{u}") for u in range(UT)]
        block = ph.block()
        table_t = wide_table.rearrange("(t p) d -> t p d", p=P)
        LOADS = 7

        @block.gpsimd
        def _(pool):
            pool.memset(b_wide[:, :], 0.0).then_inc(zeroed, 1)
            pool.memset(row[:, :, D:T3], 1.0).then_inc(set_, 1)
            pool.wait_ge(set_, 1)

        @block.sync
        def _(sp):
            with nc.allow_non_contiguous_dma(reason="few words, once"):
                sp.dma_start(w[:, :, 0:D], t["Wn"].rearrange("(c p) n -> p c n", p=P)).then_inc(loaded, 16)
                sp.dma_start(w[:, :, D:D + KD], t["Wp"].rearrange("(c p) n -> p c n", p=P)).then_inc(loaded, 16)
                sp.dma_start(w[:, :, D + KD:D + KD + 1],
                             t["We"][D:2 * D, :].rearrange("(c p) n -> p c n", p=P)).then_inc(loaded, 16)
                sp.dma_start(w[:, :, D + KD + 1:PRE],
                             t["We"][0:D, :].rearrange("(c p) n -> p c n", p=P)).then_inc(loaded, 16)
                sp.wait_ge(zeroed, 1)
                sp.dma_start(b_wide[:, 0:D], bcast(t["bn"], P)).then_inc(loaded, 16)
                sp.dma_start(b_wide[:, D:D + KD], bcast(t["bp"], P)).then_inc(loaded, 16)
                sp.dma_start(b_wide[:, PRE - 1:PRE], bcast(t["be"], P)).then_inc(loaded, 16)
            sp.wait_ge(set_, 1)

            def body(i, b, u):
                wait(sp, biased, i + 1)
                sp.dma_start(table_t[at(i), :, :].rearrange("a p d -> (a p) d"), row[:, u, :]
                             ).then_inc(stored[u], 16)
            each(sp, body, NT, UT)
            for u in range(UT):
                sp.wait_ge(stored[u], 16 * ((NT - 1 - u) // UT + 1))

        @block.vector
        def _(dve):
            def front(i, b, u):
                wait(dve, turn, i + 1 - UT)
                dve.tensor_scalar(node[:, u, :], tile_of(x, i), stat(stats, i, 0), stat(stats, i, 1),
                                  ALU.subtract, ALU.mult).then_inc(ready, 1)

            def back(i, b, u):
                dve.wait_ge(product, i + 1)
                wait(dve, stored[u], b * 16)
                dve.tensor_tensor(row[:, u, 0:D], out_ps[u][:, 0:D], b_wide[:, 0:D], ALU.add).then_inc(biased, 1)
                dve.tensor_tensor(tile_of(pre, i), out_ps[u][:, D:PRE], b_wide[:, D:PRE], ALU.add
                                  ).then_inc(taken, 1)
            dve.wait_ge(loaded, 16 * LOADS)
            pipeline(dve, [(front, 0), (back, 2)], NT, UT)
            dve.wait_ge(taken, NT)

        @block.scalar
        def _(act):
            def body(i, b, u):
                act.wait_ge(turn, i + 1)
                wait(act, product, i + 1 - UT)
                act.activation(turned[:, u, :, :].rearrange("p c q -> p (c q)"), turn_ps[u][:, 0:D], ACT.Copy
                               ).then_inc(copied, 1)
            each(act, body, NT, UT)

        @block.tensor
        def _(pe):
            pe.wait_ge(loaded, 16 * LOADS)

            def front(i, b, u):
                pe.wait_ge(ready, i + 1)
                wait(pe, copied, i + 1 - UT)
                for c in range(KC):
                    tr = pe.transpose(turn_ps[u][:, c * P:(c + 1) * P], node[:, u, c * P:(c + 1) * P],
                                      k["ident"][:, :])
                tr.then_inc(turn, 1)

            def back(i, b, u):
                pe.wait_ge(copied, i + 1)
                wait(pe, taken, i + 1 - UT)
                for c in range(KC):
                    mm = pe.matmul(out_ps[u][:, 0:PRE], turned[:, u, c, :], w[:, c, :],
                                   start=(c == 0), stop=(c == KC - 1))
                mm.then_inc(product, 1)
            pipeline(pe, [(front, 0), (back, 1)], NT, UT)


def project_nodes(nc, k, t, pre, narrow, narrow_table):
    with Phase(nc, "proj") as ph:
        shape = [P, NT, KD]
        mid = ph.sb("mid", shape)
        sq = ph.sb("sq", shape)
        mean = ph.sb("mean", [P, NT])
        var = ph.sb("var", [P, NT])
        gb = ph.sb("gb", [P, 2, KD])
        rows = ph.sb("rows", [P, NT, T2])
        own, loaded, ready, rooted, finished, stored = (
            ph.sem(n) for n in ("own", "loaded", "ready", "rooted", "finished", "stored"))
        block = ph.block()
        per_node = lambda a: a.unsqueeze(2).to_broadcast(tuple(shape))
        per_col = lambda a: a.unsqueeze(1).to_broadcast(tuple(shape))

        @block.sync
        def _(sp):
            sp.dma_start(gb[:, 0, :], bcast(t["gp"], P)).then_inc(loaded, 16)
            sp.dma_start(gb[:, 1, :], bcast(t["betap"], P)).then_inc(loaded, 16)
            sp.wait_ge(finished, 1)
            sp.dma_start(narrow_table.rearrange("(t p) d -> p t d", p=P), rows[:, :, :]).then_inc(stored, 16)
            sp.wait_ge(stored, 16)

        @block.scalar
        def _(act):
            act.wait_ge(ready, 1)
            act.activation(var[:, :], var[:, :], ACT.Sqrt, bias=k["eps"][:, 0:1], scale=1.0 / KD).then_inc(rooted, 1)

        @block.vector
        def _(dve):
            step = Steps(dve, own)

            def run(instruction):
                step(instruction)
                step.done()
            p = pre[:, :, 0:KD]
            dve.wait_ge(loaded, 32)
            run(dve.memset(rows[:, :, :], 0.0))
            run(dve.tensor_reduce(mean[:, :], p, AX.X, ALU.add))
            run(dve.tensor_scalar(mean[:, :], mean[:, :], 1.0 / KD, None, ALU.mult))
            run(dve.tensor_tensor(mid[:, :, :], p, per_node(mean[:, :]), ALU.subtract))
            run(dve.tensor_tensor(sq[:, :, :], mid[:, :, :], mid[:, :, :], ALU.mult))
            run(dve.tensor_reduce(var[:, :], sq[:, :, :], AX.X, ALU.add))
            dve.sem_inc(ready, 1)
            dve.wait_ge(rooted, 1)
            run(dve.reciprocal(mean[:, :], var[:, :]))
            run(dve.tensor_tensor(mid[:, :, :], mid[:, :, :], per_node(mean[:, :]), ALU.mult))
            run(dve.tensor_tensor(mid[:, :, :], mid[:, :, :], per_col(gb[:, 0, :]), ALU.mult))
            run(dve.tensor_tensor(mid[:, :, :], mid[:, :, :], per_col(gb[:, 1, :]), ALU.add))
            run(dve.tensor_scalar(narrow[:, :, 0:KD], mid[:, :, :], 0.0, None, ALU.max))
            run(dve.tensor_scalar(rows[:, :, 0:KD], mid[:, :, :], 0.0, None, ALU.max))
            run(dve.memset(rows[:, :, KD:KD + 1], 1.0))
            run(dve.memset(narrow[:, :, KD:KD + 1], 1.0))
            run(dve.tensor_copy(rows[:, :, ND:ND + 1], pre[:, :, KD:KD + 1]))
            run(dve.tensor_copy(narrow[:, :, ND:ND + 1], pre[:, :, KD + 1:KD + 2]))
            dve.sem_inc(finished, 1)


def kronecker_items(nc, k, t, g, narrow, narrow_table, kron_sum, below_max, item_max):
    with Phase(nc, "kron") as ph:
        wk = ph.sb("wk", [KCH, 4, D])
        gain = ph.sb("gain", [P, D])
        shift = ph.sb("shift", [P, D])
        col = ph.sb("col", [P, UG, G], I32)
        rows = ph.sb("rows", [P, UG, G, T2])
        hot = ph.sb("hot", [P, UG, G, P])
        hotT = ph.sb("hotT", [P, 2, G, P])
        kron = ph.sb("kron", [P, 2, G, 4 * KCH])
        kronT = ph.sb("kronT", [KCH, G, 4, P])
        logit = ph.sb("logit", [P, 4, G])
        diag = ph.sb("diag", [P, 2, G, P])
        stats = ph.sb("stats", [P, 2, 2, 6])
        mv = ph.sb("mv", [P, 2, 2, 2])
        std = ph.sb("std", [P, 2, 2])
        rstd = ph.sb("rstd", [P, 2, 2])
        minus = ph.sb("minus", [P, 2, 2])
        normed = ph.sb("normed", [P, 2, G, D])
        gained = ph.sb("gained", [P, G, D])
        shifted = ph.sb("shifted", [P, 2, G, D])
        message = ph.sb("message", [P, 2, G, D])
        hotT_ps = ph.ps("hotT_ps")
        dst_ps = ph.ps("dst_ps")
        max_ps = ph.ps("max_ps")
        kronT_ps = ph.ps("kronT_ps")
        y_ps = [ph.ps(f"y_ps{h}") for h in range(2)]
        sum_ps = [ph.ps(f"sum_ps{h}") for h in range(2)]
        s = {n: ph.sem(n) for n in (
            "ones", "loaded", "col", "issued", "hot", "hotT", "hotT_read", "dst", "kron", "logit", "diag",
            "kronT", "kronT_read", "spread", "topped", "tops", "lowered", "y", "counted", "taken", "rooted",
            "rstd", "minus", "normed", "gained", "shifted", "message", "summed", "added", "cleared")}
        here = [ph.sem(f"here{u}") for u in range(UG)]
        block = ph.block()
        LOADS = 3
        sums = kron_sum[:, :, :].rearrange("p t d -> p (t d)")
        features = narrow[:, :, :].rearrange("p t n -> p (t n)")
        half = lambda j: slice(j % 2 * D, j % 2 * D + D)
        W = ND + 1

        @block.sync
        def _(sp):
            sp.dma_start(gain[:, :], bcast(t["gk"], P)).then_inc(s["loaded"], 16)
            sp.dma_start(shift[:, :], bcast(t["betak"], P)).then_inc(s["loaded"], 16)
            sp.dma_start(wk[:, :, :], t["Wk"].rearrange("(c p) n -> p c n", c=4)).then_inc(s["loaded"], 16)

        @block.gpsimd
        def _(pool):
            pool.memset(kron[:, :, :, ND * ND:4 * KCH], 0.0).then_inc(s["ones"], 1)
            pool.wait_ge(s["loaded"], 16 * LOADS)

            def gather(i, b, u):
                wait(pool, s["col"], i + 1)
                wait(pool, s["kron"], i + 1 - UG)
                pool.sem_inc(s["issued"], 1)
                for j in range(G):
                    pool.indirect_dma_start(
                        out=rows[:, u, j, :], out_offset=None, in_=narrow_table,
                        in_offset=bass.IndirectOffsetOnAxis(ap=col[:, u, j:j + 1], axis=0)).then_inc(here[u], 16)

            def affine(i, b, u):
                wait(pool, s["normed"], 2 * i + 2)
                wait(pool, s["shifted"], i)
                pool.tensor_tensor(gained[:, :, :], normed[:, u % 2, :, :],
                                   gain[:, :].unsqueeze(1).to_broadcast((P, G, D)), ALU.mult
                                   ).then_inc(s["gained"], 1)
                wait(pool, s["gained"], i + 1)
                wait(pool, s["message"], i - 1)
                pool.tensor_tensor(shifted[:, u % 2, :, :], gained[:, :, :],
                                   shift[:, :].unsqueeze(1).to_broadcast((P, G, D)), ALU.add
                                   ).then_inc(s["shifted"], 1)
            pipeline(pool, [(gather, 0), (affine, 4)], NG, UG)

        @block.scalar
        def _(act):
            def column(i, b, u):
                wait(act, here[u], b * 16 * G)
                act.activation(col[:, u, :], group(g["item_src"], i), ACT.Copy).then_inc(s["col"], 1)

            def hot_turned(i, b, u):
                act.wait_ge(s["hotT"], i + 1)
                act.activation(hotT[:, u % 2, :, :].rearrange("p g q -> p (g q)"), hotT_ps[:, :], ACT.Copy
                               ).then_inc(s["hotT_read"], 1)

            def kron_turned(j):
                def body(i, b, u):
                    act.wait_ge(s["kronT"], i * G + j + 1)
                    act.activation(kronT[:, j, :, :].rearrange("p c q -> p (c q)"), kronT_ps[0:KCH, :], ACT.Copy
                                   ).then_inc(s["kronT_read"], 1)
                return body

            def root(h):
                def body(i, b, u):
                    act.wait_ge(s["taken"], 2 * i + h + 1)
                    act.activation(std[:, h, :], mv[:, h, :, 1:2].rearrange("p a b -> p (a b)"), ACT.Sqrt,
                                   bias=k["eps"][:, 0:1]).then_inc(s["rooted"], 1)
                return body

            def norm(h):
                def body(i, b, u):
                    act.wait_ge(s["minus"], 2 * i + h + 1)
                    if h == 0:
                        wait(act, s["gained"], i - 1)
                    for j in (2 * h, 2 * h + 1):
                        last = act.activation(normed[:, u % 2, j, :], y_ps[h][:, half(j)], ACT.Identity,
                                              scale=rstd[:, h, j % 2:j % 2 + 1], bias=minus[:, h, j % 2:j % 2 + 1])
                    last.then_inc(s["normed"], 1)
                return body

            def relu(i, b, u):
                act.wait_ge(s["shifted"], i + 1)
                wait(act, s["summed"], (i - 1) * G)
                act.activation(message[:, u % 2, :, :].rearrange("p g d -> p (g d)"),
                               shifted[:, u % 2, :, :].rearrange("p g d -> p (g d)"), ACT.Relu
                               ).then_inc(s["message"], 1)
            pipeline(act, [(column, 0), (hot_turned, 3), (kron_turned(0), 4), (root(1), 5), (norm(1), 5),
                           (kron_turned(1), 4), (relu, 6), (kron_turned(2), 4), (root(0), 4),
                           (norm(0), 4), (kron_turned(3), 4)], NG, UG)

        @block.tensor
        def _(pe):
            pe.wait_ge(s["loaded"], 16 * LOADS)

            def turn_hot(i, b, u):
                pe.wait_ge(s["hot"], i + 1)
                wait(pe, s["hotT_read"], i)
                for j in range(G):
                    tr = pe.transpose(hotT_ps[:, j * P:(j + 1) * P], hot[:, u, j, :], k["ident"][:, :])
                tr.then_inc(s["hotT"], 1)

            def spread_dst(i, b, u):
                places = flat_places(nc, mybir.EngineType.PE, g["item_at"][NS], i * G, G, (NT - 1) * NS)
                pe.wait_ge(s["hotT_read"], i + 1)
                wait(pe, s["kron"], i)
                for j in range(G):
                    mm = pe.matmul(dst_ps[:, j * NS:j * NS + W], hotT[:, u % 2, j, :],
                                   features[:, bass.ds(places[j], W)], start=True, stop=True)
                mm.then_inc(s["dst"], 1)

            def turn_kron(j):
                def body(i, b, u):
                    if j == 0:
                        pe.wait_ge(s["kron"], i + 1)
                    wait(pe, s["kronT_read"], i * G + j)
                    for c in range(4):
                        tr = pe.transpose(kronT_ps[0:KCH, c * P:(c + 1) * P],
                                          kron[:, u % 2, j, c * KCH:(c + 1) * KCH], k["ident"][:, :])
                    tr.then_inc(s["kronT"], 1)
                return body

            def dense(j):
                def body(i, b, u):
                    h = j // 2
                    pe.wait_ge(s["kronT_read"], i * G + j + 1)
                    if j % 2 == 0:
                        wait(pe, s["normed"], 2 * i + h - 1)
                    for c in range(4):
                        mm = pe.matmul(y_ps[h][:, half(j)], kronT[:, j, c, :], wk[:, c, :],
                                       start=(c == 0), stop=(c == 3))
                    if j % 2 == 1:
                        mm.then_inc(s["y"], 1)
                return body

            def spread_logits(i, b, u):
                pe.wait_ge(s["diag"], i + 1)
                wait(pe, s["lowered"], i)
                for j in range(G):
                    mm = pe.matmul(max_ps[:, j * P:(j + 1) * P], hot[:, u, j, :], diag[:, u % 2, j, :],
                                   start=True, stop=True)
                mm.then_inc(s["spread"], 1)

            def spread_tops(i, b, u):
                pe.wait_ge(s["topped"], i + 1)
                for j in range(G):
                    mm = pe.matmul(max_ps[:, j:j + 1], hotT[:, u % 2, j, :], item_max[:, at(i * G + j)],
                                   start=True, stop=True)
                mm.then_inc(s["tops"], 1)

            def total(j):
                def body(i, b, u):
                    h = j // 2
                    if j == 0:
                        pe.wait_ge(s["message"], i + 1)
                    if j % 2 == 0:
                        wait(pe, s["added"], (i - 1) * G + 2 * h + 2)
                    mm = pe.matmul(sum_ps[h][:, half(j)], hot[:, u, j, :], message[:, u % 2, j, :],
                                   start=True, stop=True)
                    if j % 2 == 1:
                        mm.then_inc(s["summed"], 2)
                return body
            pipeline(pe, [(total(0), 4), (total(1), 4), (turn_hot, 0), (turn_kron(0), 1), (dense(3), 2),
                          (spread_dst, 0), (turn_kron(1), 1), (dense(0), 1),
                          (total(2), 4), (total(3), 4), (spread_logits, 1), (turn_kron(2), 1), (dense(1), 1),
                          (turn_kron(3), 1), (dense(2), 1), (spread_tops, 1)], NG, UG)

        @block.vector
        def _(dve):
            dve.memset(kron_sum[:, :, :], 0.0).then_inc(s["cleared"], 1)
            dve.wait_ge(s["cleared"], 1)
            dve.wait_ge(s["ones"], 1)
            many = (P, G, P)

            def one_hot(i, b, u):
                dve.tensor_tensor(hot[:, u, :, :], k["iota"][:, :].unsqueeze(1).to_broadcast(many),
                                  group(g["item_dst"], i).unsqueeze(2).to_broadcast(many), ALU.is_equal
                                  ).then_inc(s["hot"], 1)

            def product(i, b, u):
                shape = (P, ND, ND)
                dsts = dst_ps[:, 0:G * NS].rearrange("p (g n) -> p g n", n=NS)
                wait(dve, here[u], (b + 1) * 16 * G)
                dve.wait_ge(s["dst"], i + 1)
                dve.tensor_tensor(logit[:, u % 4, :], rows[:, u, :, ND:ND + 1].rearrange("p g a -> p (g a)"),
                                  dsts[:, :, ND:ND + 1].rearrange("p g a -> p (g a)"), ALU.add
                                  ).then_inc(s["logit"], 1)
                for j in range(G):
                    last = dve.tensor_tensor(
                        kron[:, u % 2, j, 0:ND * ND].rearrange("p (a k) -> p a k", k=ND),
                        rows[:, u, j, 0:ND].unsqueeze(2).to_broadcast(shape),
                        dsts[:, j, 0:ND].unsqueeze(1).to_broadcast(shape), ALU.mult)
                last.then_inc(s["kron"], 1)

            def diagonal(i, b, u):
                dve.wait_ge(s["logit"], i + 1)
                dve.scalar_tensor_tensor(
                    out=diag[:, u % 2, :, :], in0=logit[:, u % 4, :].unsqueeze(2).to_broadcast(many), scalar=0.0,
                    in1=k["ident"][:, :].unsqueeze(1).to_broadcast(many), op0=ALU.max, op1=ALU.mult
                ).then_inc(s["diag"], 1)

            def item_tops(i, b, u):
                dve.wait_ge(s["spread"], i + 1)
                dve.tensor_reduce(group(item_max, i), max_ps[:, :].rearrange("p (g q) -> p g q", q=P), AX.X,
                                  ALU.max).then_inc(s["topped"], 1)

            def lower(i, b, u):
                dve.wait_ge(s["tops"], i + 1)
                dve.scalar_tensor_tensor(out=group(below_max, i), in0=logit[:, u % 4, :], scalar=0.0,
                                         in1=max_ps[:, 0:G], op0=ALU.max, op1=ALU.subtract
                                         ).then_inc(s["lowered"], 1)

            def count(h):
                def body(i, b, u):
                    dve.wait_ge(s["y"], 2 * i + h + 1)
                    for j in range(2):
                        last = dve.bn_stats(stats[:, h, j, :], y_ps[h][:, half(j)])
                    last.then_inc(s["counted"], 1)
                    dve.wait_ge(s["counted"], 2 * i + h + 1)
                    dve.sem_inc(s["cleared"], 1)
                    for j in range(2):
                        last = dve.bn_aggr(mv[:, h, j, :], stats[:, h, j, :])
                    last.then_inc(s["taken"], 1)
                return body

            def invert(h):
                def body(i, b, u):
                    dve.wait_ge(s["rooted"], 2 * i + h + 1)
                    dve.reciprocal(rstd[:, h, :], std[:, h, :]).then_inc(s["rstd"], 1)
                    dve.wait_ge(s["rstd"], 2 * i + h + 1)
                    dve.scalar_tensor_tensor(
                        out=minus[:, h, :], in0=mv[:, h, :, 0:1].rearrange("p a b -> p (a b)"), scalar=-1.0,
                        in1=rstd[:, h, :], op0=ALU.mult, op1=ALU.mult).then_inc(s["minus"], 1)
                return body

            def add(h):
                def body(i, b, u):
                    places = flat_places(nc, mybir.EngineType.DVE, g["item_at"][D], i * G + 2 * h, 2, (NT - 1) * D)
                    wait(dve, s["summed"], i * G + 2 * h + 2)
                    for j in (2 * h, 2 * h + 1):
                        wait(dve, s["added"], i * G + j)
                        here_ = sums[:, bass.ds(places[j % 2], D)]
                        dve.tensor_tensor(here_, sum_ps[h][:, half(j)], here_, ALU.add).then_inc(s["added"], 1)
                return body
            pipeline(dve, [(count(1), 3), (one_hot, 0), (invert(1), 3), (add(0), 5), (item_tops, 2), (product, 1),
                           (count(0), 2), (diagonal, 1), (invert(0), 2), (lower, 2), (add(1), 5)], NG, UG)
            dve.wait_ge(s["added"], NI)
            dve.wait_ge(s["lowered"], NG)


def attention_weights(nc, k, tile_row, below_max, item_max, edge_w, factor):
    with Phase(nc, "attw") as ph:
        tiles_i = ph.sb("tiles_i", [P, NI], I32)
        tiles = ph.sb("tiles", [P, NI])
        own_max = ph.sb("own_max", [P, 2, NI])
        tile_max = ph.sb("tile_max", [P, NT])
        spread = ph.sb("spread", [P, 2, NI])
        gap = ph.sb("gap", [P, NI])
        loaded, own, clipped, ready, done = (ph.sem(n) for n in ("loaded", "own", "clipped", "ready", "done"))
        block = ph.block()

        @block.sync
        def _(sp):
            sp.dma_start(tiles_i[:, :], bcast(tile_row, P)).then_inc(loaded, 16)

        @block.vector
        def _(dve):
            step = Steps(dve, own)
            dve.tensor_scalar(below_max[:, :], below_max[:, :], 0.0, None, ALU.min).then_inc(clipped, 1)
            dve.wait_ge(loaded, 16)
            step(dve.tensor_copy(tiles[:, :], tiles_i[:, :]))
            step(dve.tensor_copy(gap[:, :], item_max[:, :]))
            step.done()
            for t in range(NT):
                step(dve.scalar_tensor_tensor(out=own_max[:, t % 2, :], in0=tiles[:, :], scalar=float(t),
                                              in1=item_max[:, :], op0=ALU.is_equal, op1=ALU.mult))
                step.done()
                step(dve.tensor_reduce(tile_max[:, t:t + 1], own_max[:, t % 2, :], AX.X, ALU.max))
            step.done()
            for t in range(NT):
                step(dve.tensor_scalar(spread[:, t % 2, :], tiles[:, :], float(t), tile_max[:, t:t + 1],
                                       ALU.is_equal, ALU.mult))
                step.done()
                step(dve.tensor_tensor(gap[:, :], gap[:, :], spread[:, t % 2, :], ALU.subtract))
            step.done()
            dve.sem_inc(ready, 1)

        @block.scalar
        def _(act):
            act.wait_ge(clipped, 1)
            act.activation(edge_w[:, :], below_max[:, :], ACT.Exp).then_inc(done, 1)
            act.wait_ge(ready, 1)
            act.activation(factor[:, :], gap[:, :], ACT.Exp).then_inc(done, 1)
            act.wait_ge(done, 2)


def gated_update(nc, k, t, x, stats, att, state):
    with Phase(nc, "gru") as ph:
        w_ih = ph.sb("w_ih", [P, KC, 3 * D])
        w_hh = ph.sb("w_hh", [P, KC, 3 * D])
        b_ih = ph.sb("b_ih", [P, 3 * D])
        b_hh = ph.sb("b_hh", [P, 3 * D])
        b_rz = ph.sb("b_rz", [P, 2 * D])
        inv = ph.sb("inv", [P, NT])
        both = ph.sb("both", [P, UT, 2, D])
        turned = ph.sb("turned", [P, UT, 2 * KC, P])
        rz = ph.sb("rz", [P, UT, 2 * D])
        gate = ph.sb("gate", [P, UT, 2 * D])
        i_n = ph.sb("i_n", [P, UT, D])
        h_n = ph.sb("h_n", [P, UT, D])
        cand = ph.sb("cand", [P, UT, D])
        mix = ph.sb("mix", [P, UT, D])
        turn_ps = [ph.ps(f"turn{j}") for j in range(2)]
        rz_ps = [ph.ps(f"rz{j}") for j in range(2)]
        n_ps = [ph.ps(f"n{j}") for j in range(2)]
        s = {n: ph.sem(n) for n in ("loaded", "own", "ready", "turn", "copied", "rz", "n", "rz_b", "gated", "n_read",
                                    "pre", "cand", "mixed", "out", "c1", "c2")}
        block = ph.block()

        @block.sync
        def _(sp):
            for w, name in ((w_ih, "W_ihT"), (w_hh, "W_hhT")):
                sp.dma_start(w[:, :, :], t[name].rearrange("(c p) n -> p c n", p=P)).then_inc(s["loaded"], 16)
            for w, name in ((b_ih, "b_ih"), (b_hh, "b_hh")):
                sp.dma_start(w[:, :], bcast(t[name], P)).then_inc(s["loaded"], 16)

        @block.vector
        def _(dve):
            step = Steps(dve, s["own"])
            step(dve.tensor_scalar(inv[:, :], att[:, :, D:D + 1].rearrange("p t a -> p (t a)"), 1.0e-30, None, ALU.max))
            dve.wait_ge(s["loaded"], 64)
            step.done()
            step(dve.reciprocal(inv[:, :], inv[:, :]))
            step(dve.tensor_tensor(b_rz[:, :], b_ih[:, 0:2 * D], b_hh[:, 0:2 * D], ALU.add))
            step.done()

            def front(i, b, u):
                wait(dve, s["turn"], i + 1 - UT)
                wait(dve, s["mixed"], 3 * (i + 1 - UT))
                dve.tensor_scalar(both[:, u, 0, :], att[:, at(i), 0:D].rearrange("p a d -> p (a d)"), inv[:, at(i)],
                                  0.0, ALU.mult, ALU.max).then_inc(s["ready"], 1)
                dve.tensor_scalar(both[:, u, 1, :], tile_of(x, i), stat(stats, i, 0), stat(stats, i, 1),
                                  ALU.subtract, ALU.mult).then_inc(s["ready"], 1)

            def gates(i, b, u):
                dve.wait_ge(s["rz"], i + 1)
                wait(dve, s["gated"], i + 1 - UT)
                dve.tensor_tensor(rz[:, u, :], rz_ps[u % 2][:, :], b_rz[:, :], ALU.add).then_inc(s["rz_b"], 1)
                dve.wait_ge(s["n"], i + 1)
                wait(dve, s["pre"], 2 * (i + 1 - UT))
                dve.tensor_tensor(h_n[:, u, :], n_ps[u % 2][:, D:2 * D], b_hh[:, 2 * D:3 * D], ALU.add
                                  ).then_inc(s["n_read"], 1)
                wait(dve, s["cand"], i + 1 - UT)
                dve.tensor_tensor(i_n[:, u, :], n_ps[u % 2][:, 0:D], b_ih[:, 2 * D:3 * D], ALU.add
                                  ).then_inc(s["n_read"], 1)

            def candidate(i, b, u):
                dve.wait_ge(s["gated"], i + 1)
                dve.wait_ge(s["n_read"], 2 * (i + 1))
                dve.tensor_tensor(h_n[:, u, :], h_n[:, u, :], gate[:, u, 0:D], ALU.mult).then_inc(s["pre"], 1)
                dve.wait_ge(s["pre"], 2 * i + 1)
                dve.tensor_tensor(i_n[:, u, :], i_n[:, u, :], h_n[:, u, :], ALU.add).then_inc(s["pre"], 1)

            def blend(i, b, u):
                dve.wait_ge(s["cand"], i + 1)
                wait(dve, s["out"], i + 1 - UT)
                dve.tensor_tensor(mix[:, u, :], both[:, u, 1, :], cand[:, u, :], ALU.subtract
                                  ).then_inc(s["mixed"], 1)
                dve.wait_ge(s["mixed"], 3 * i + 1)
                dve.tensor_tensor(mix[:, u, :], mix[:, u, :], gate[:, u, D:2 * D], ALU.mult).then_inc(s["mixed"], 1)
                dve.wait_ge(s["mixed"], 3 * i + 2)
                dve.tensor_tensor(mix[:, u, :], mix[:, u, :], cand[:, u, :], ALU.add).then_inc(s["mixed"], 1)
            pipeline(dve, [(front, 0), (gates, 2), (candidate, 3), (blend, 3)], NT, UT)
            dve.wait_ge(s["mixed"], 3 * NT)

        @block.scalar
        def _(act):
            def copy(i, b, u):
                act.wait_ge(s["turn"], i + 1)
                wait(act, s["n"], i + 1 - UT)
                act.activation(turned[:, u, :, :].rearrange("p c q -> p (c q)"), turn_ps[u % 2][:, :], ACT.Copy
                               ).then_inc(s["copied"], 1)

            def sigmoid(i, b, u):
                act.wait_ge(s["rz_b"], i + 1)
                wait(act, s["mixed"], 3 * (i + 1 - UT))
                act.activation(gate[:, u, :], rz[:, u, :], ACT.Sigmoid).then_inc(s["gated"], 1)

            def tanh(i, b, u):
                act.wait_ge(s["pre"], 2 * (i + 1))
                wait(act, s["mixed"], 3 * (i + 1 - UT))
                act.activation(cand[:, u, :], i_n[:, u, :], ACT.Tanh).then_inc(s["cand"], 1)

            def relu(i, b, u):
                act.wait_ge(s["mixed"], 3 * (i + 1))
                act.activation(tile_of(state, i), mix[:, u, :], ACT.Relu).then_inc(s["out"], 1)
            pipeline(act, [(copy, 0), (sigmoid, 2), (tanh, 3), (relu, 3)], NT, UT)
            act.wait_ge(s["out"], NT)

        @block.tensor
        def _(pe):
            pe.wait_ge(s["loaded"], 64)

            def turn(i, b, u):
                pe.wait_ge(s["ready"], 2 * (i + 1))
                wait(pe, s["copied"], i - 1)
                for c in range(2 * KC):
                    tr = pe.transpose(turn_ps[u % 2][:, c * P:(c + 1) * P],
                                      both[:, u, c // KC, (c % KC) * P:(c % KC + 1) * P], k["ident"][:, :])
                tr.then_inc(s["turn"], 1)

            def products(i, b, u):
                pe.wait_ge(s["copied"], i + 1)
                wait(pe, s["rz_b"], i - 1)
                for c in range(2 * KC):
                    w = w_ih if c < KC else w_hh
                    mm = pe.matmul(rz_ps[u % 2][:, :], turned[:, u, c, :], w[:, c % KC, 0:2 * D],
                                   start=(c == 0), stop=(c == 2 * KC - 1))
                mm.then_inc(s["rz"], 1)
                wait(pe, s["n_read"], 2 * (i - 1))
                for h, w in enumerate((w_ih, w_hh)):
                    for c in range(KC):
                        mm = pe.matmul(n_ps[u % 2][:, h * D:(h + 1) * D], turned[:, u, h * KC + c, :],
                                       w[:, c, 2 * D:3 * D], start=(c == 0), stop=(c == KC - 1))
                mm.then_inc(s["n"], 1)
            pipeline(pe, [(turn, 0), (products, 1)], NT, UT)


def combine(nc, k, t, state, stats, kron_sum, out):
    with Phase(nc, "comb") as ph:
        w = ph.sb("w", [P, 2 * KC, D])
        bias = ph.sb("bias", [P, D])
        gain = ph.sb("gain", [P, D])
        shift = ph.sb("shift", [P, D])
        both = ph.sb("both", [P, UT, 2, D])
        turned = ph.sb("turned", [P, UT, 2 * KC, P])
        turn_ps = [ph.ps(f"turn{u}") for u in range(UT)]
        out_ps = [ph.ps(f"out{u}") for u in range(UT)]
        s = {n: ph.sem(n) for n in ("loaded", "steps", "ready", "turn", "copied", "product", "done", "second")}
        block = ph.block()

        @block.sync
        def _(sp):
            sp.dma_start(w[:, :, :], t["Wc"].rearrange("(c p) n -> p c n", p=P)).then_inc(s["loaded"], 16)
            for b, name in ((bias, "bc"), (gain, "g_ln"), (shift, "beta_ln")):
                sp.dma_start(b[:, :], bcast(t[name], P)).then_inc(s["loaded"], 16)

        @block.vector
        def _(dve):
            dve.wait_ge(s["loaded"], 64)

            def front(i, b, u):
                h = both[:, u, 0, :]
                wait(dve, s["turn"], i + 1 - UT)
                dve.tensor_scalar(h, tile_of(state, i), stat(stats, i, 0), stat(stats, i, 1),
                                  ALU.subtract, ALU.mult).then_inc(s["steps"], 1)
                dve.wait_ge(s["steps"], 2 * i + 1)
                dve.tensor_tensor(h, h, gain[:, :], ALU.mult).then_inc(s["steps"], 1)
                dve.wait_ge(s["steps"], 2 * i + 2)
                dve.tensor_tensor(h, h, shift[:, :], ALU.add).then_inc(s["ready"], 1)

            def back(i, b, u):
                dve.wait_ge(s["product"], i + 1)
                dve.tensor_tensor(tile_of(out, i, D), out_ps[u][:, 0:D], bias[:, :], ALU.add).then_inc(s["done"], 1)
            pipeline(dve, [(front, 0), (back, 2)], NT, UT)
            dve.wait_ge(s["done"], NT)

        @block.gpsimd
        def _(pool):
            def body(i, b, u):
                wait(pool, s["turn"], i + 1 - UT)
                pool.tensor_copy(both[:, u, 1, :], tile_of(kron_sum, i)).then_inc(s["second"], 1)
            each(pool, body, NT, UT)

        @block.scalar
        def _(act):
            def body(i, b, u):
                act.wait_ge(s["turn"], i + 1)
                wait(act, s["product"], i + 1 - UT)
                act.activation(turned[:, u, :, :].rearrange("p c q -> p (c q)"), turn_ps[u][:, :], ACT.Copy
                               ).then_inc(s["copied"], 1)
            each(act, body, NT, UT)

        @block.tensor
        def _(pe):
            pe.wait_ge(s["loaded"], 64)

            def front(i, b, u):
                pe.wait_ge(s["ready"], i + 1)
                pe.wait_ge(s["second"], i + 1)
                wait(pe, s["copied"], i + 1 - UT)
                for c in range(2 * KC):
                    tr = pe.transpose(turn_ps[u][:, c * P:(c + 1) * P],
                                      both[:, u, c // KC, (c % KC) * P:(c % KC + 1) * P], k["ident"][:, :])
                tr.then_inc(s["turn"], 1)

            def back(i, b, u):
                pe.wait_ge(s["copied"], i + 1)
                wait(pe, s["done"], i + 1 - UT)
                for c in range(2 * KC):
                    mm = pe.matmul(out_ps[u][:, 0:D], turned[:, u, c, :], w[:, c, :],
                                   start=(c == 0), stop=(c == 2 * KC - 1))
                mm.then_inc(s["product"], 1)
            pipeline(pe, [(front, 0), (back, 1)], NT, UT)


def add_normalised(nc, t, y, stats, x):
    with Phase(nc, "fin") as ph:
        gain = ph.sb("gain", [P, D])
        shift = ph.sb("shift", [P, D])
        tmp = ph.sb("tmp", [P, UT, D])
        loaded, steps, positive, done = (ph.sem(n) for n in ("loaded", "steps", "positive", "done"))
        block = ph.block()

        @block.sync
        def _(sp):
            sp.dma_start(gain[:, :], bcast(t["gc"], P)).then_inc(loaded, 16)
            sp.dma_start(shift[:, :], bcast(t["betac"], P)).then_inc(loaded, 16)

        @block.vector
        def _(dve):
            dve.wait_ge(loaded, 32)

            def front(i, b, u):
                h = tmp[:, u, :]
                wait(dve, done, i + 1 - UT)
                dve.tensor_scalar(h, tile_of(y, i, D), stat(stats, i, 0), stat(stats, i, 1),
                                  ALU.subtract, ALU.mult).then_inc(steps, 1)
                dve.wait_ge(steps, 3 * i + 1)
                dve.tensor_tensor(h, h, gain[:, :], ALU.mult).then_inc(steps, 1)
                dve.wait_ge(steps, 3 * i + 2)
                dve.tensor_tensor(h, h, shift[:, :], ALU.add).then_inc(steps, 1)

            def back(i, b, u):
                dve.wait_ge(positive, i + 1)
                dve.tensor_tensor(tile_of(x, i), tmp[:, u, :], tile_of(x, i), ALU.add).then_inc(done, 1)
            pipeline(dve, [(front, 0), (back, 1)], NT, UT)
            dve.wait_ge(done, NT)

        @block.scalar
        def _(act):
            def body(i, b, u):
                act.wait_ge(steps, 3 * (i + 1))
                act.activation(tmp[:, u, :], tmp[:, u, :], ACT.Relu).then_inc(positive, 1)
            each(act, body, NT, UT)


def load_nodes(nc, t, x):
    with Phase(nc, "load") as ph:
        here = ph.sem("here")
        block = ph.block()

        @block.sync
        def _(sp):
            sp.dma_start(x[:, :, :], t["x"].rearrange("(t p) d -> p t d", p=P)).then_inc(here, 16)
            sp.wait_ge(here, 16)


def store_nodes(nc, x, out):
    with Phase(nc, "store") as ph:
        stored = ph.sem("stored")
        block = ph.block()
        whole = N // P

        @block.sync
        def _(sp):
            sp.dma_start(out[0:whole * P, :].rearrange("(t p) d -> p t d", p=P), x[:, 0:whole, :]
                         ).then_inc(stored, 16)
            sp.dma_start(out[whole * P:N, :], x[0:N - whole * P, whole, :]).then_inc(stored, 16)
            sp.wait_ge(stored, 32)


def program(nc, t, out, stop=9):
    USED.clear()
    edges = {n: nc.dram_tensor(f"edges_{n}", (EP,), I32 if n != "weight" else F32, kind="Internal").ap()
             for n in ("src", "dst", "weight")}
    tile_row = nc.dram_tensor("tile_row", (NI,), I32, kind="Internal").ap()
    table = nc.dram_tensor("table", (NP, D), F32, kind="Internal").ap()
    wide_table = nc.dram_tensor("wide_table", (NP, T3), F32, kind="Internal").ap()
    narrow_table = nc.dram_tensor("narrow_table", (NP, T2), F32, kind="Internal").ap()
    slot_rows, y_rows = (nc.dram_tensor(n, (ST * P, D), F32, kind="Internal").ap()
                         for n in ("slot_rows", "y_rows"))
    weight_row = nc.dram_tensor("weight_row", (NP,), F32, kind="Internal").ap()
    with Phase(nc, "all") as top:
        k = constants(nc, top)
        x = top.sb("x", [P, NT, D])
        acc = top.sb("acc", [P, NT, D])
        g = {n: top.sb(n, [P, NI]) for n in ("item_dst", "item_w")}
        g["item_src"] = top.sb("item_src", [P, NI], I32)
        g["item_at"] = {n: top.sb(f"item_at{n}", [1, NI], I32) for n in (D, T3, NS)}
        g["norm_in"] = top.sb("norm_in", [P, NT])
        g["norm_out"] = top.sb("norm_out", [P, NT])
        g["stats"] = top.sb("stats", [P, NT, 2])
        load_nodes(nc, t, x)
        order_edges(nc, t, k, edges)
        degrees_and_items(nc, t, k, edges, g, tile_row)
        with Phase(nc, "gnn0") as ph:
            mix = ph.sb("mix", [P, L + 1, KC, 2 * D])
            bias = ph.sb("bias", [P, L, D])
            channel_bias = ph.sb("channel_bias", [P, L, D])
            mlp_bias = ph.sb("mlp_bias", [P, D])
            first_gnn_weights(nc, t, k, mix, bias, channel_bias, mlp_bias)
            layer_stats(nc, "st0", k, x, g["stats"])
            for l in range(L + 1):
                first_gnn_nodes(nc, l, k, g, x, acc, mix, bias, channel_bias, mlp_bias, table)
                if l < L:
                    aggregate(nc, f"agg{l}", k, g, table, D, acc, g["item_w"])
        clear_semaphores(nc)
        if stop >= 2:
            with Phase(nc, "ffn0") as ph:
                logits = ph.sb("logits", [P, NT, NE])
                share = ph.sb("share", [P, NT, 2])
                slot = ph.sb("slot", [P, NT, 2], I32)
                places = ph.sb("places", [1, ST * 3], I32)
                w = {"w1": ph.sb("w1", [P, NE, KC, H]), "w2": ph.sb("w2", [P, NE, HM, D]),
                     "b1": ph.sb("b1", [P, NE * H]), "b2": ph.sb("b2", [P, NE * D]),
                     "here": ph.sem("here"), "cleared": ph.sem("cleared"), "slot_rows": slot_rows}
                layer_stats(nc, "st1", k, x, g["stats"])
                apply_norm(nc, "an1", x, g["stats"], acc)
                layer_stats(nc, "st2", k, acc, g["stats"])
                expert_rows(nc, k, t, acc, g["stats"], logits, w)
                route_two(nc, k, logits, share, slot, places)
                scatter_rows(nc, acc, slot, slot_rows)
                routed_experts(nc, k, w, places, y_rows)
                gather_experts(nc, x, share, slot, y_rows)
        clear_semaphores(nc)
        if stop >= 3:
            with Phase(nc, "gnn1") as ph:
                kron_sum = ph.sb("kron_sum", [P, NT, D])
                edge_w = ph.sb("edge_w", [P, NI])
                factor = ph.sb("factor", [P, NI])
                layer_stats(nc, "st3", k, x, g["stats"])
                with Phase(nc, "items1") as at_items:
                    pre = at_items.sb("pre", [P, NT, PRE - D])
                    narrow = at_items.sb("narrow", [P, NT, NS])
                    below_max = at_items.sb("below_max", [P, NI])
                    item_max = at_items.sb("item_max", [P, NI])
                    second_gnn_nodes(nc, k, t, x, g["stats"], pre, wide_table)
                    project_nodes(nc, k, t, pre, narrow, narrow_table)
                    kronecker_items(nc, k, t, g, narrow, narrow_table, kron_sum, below_max, item_max)
                    attention_weights(nc, k, tile_row, below_max, item_max, edge_w, factor)
                att = ph.sb("att", [P, NT, T3])
                aggregate(nc, "agga", k, g, wide_table, T3, att, edge_w, factor)
                gated_update(nc, k, t, x, g["stats"], att, acc)
                layer_stats(nc, "st4", k, acc, g["stats"])
                combine(nc, k, t, acc, g["stats"], kron_sum, att)
                layer_stats(nc, "st5", k, att, g["stats"])
                add_normalised(nc, t, att, g["stats"], x)
        clear_semaphores(nc)
        if stop >= 4:
            with Phase(nc, "ffn1") as ph:
                xT = ph.sb("xT", [P, KC, NP])
                weight = ph.sb("weight", [P, NT, 1])
                coef = ph.sb("coef", [P, 1, NT])
                layer_stats(nc, "st6", k, x, g["stats"])
                normalised_columns(nc, "nc2", k, x, g["stats"], xT, weight, t["wr"], t["ffn_br"], add_back=True)
                choose_half(nc, k, weight_row, weight, coef, max(1, N // 2) - 1)
                experts(nc, "dense", k, xT, x, coef, lambda e, n: coef[:, 0, n:n + 1],
                        lambda e: t["w1"][:, bass.ds(e * H, H)].rearrange("(c p) n -> p c n", p=P),
                        lambda e: t["ffn_b1"][bass.ds(e * H, H)].rearrange("(m p) -> p m", p=P),
                        lambda e: t["w2"][bass.ds(e * H, H), :].rearrange("(m p) n -> p m n", p=P),
                        lambda e: bcast(t["ffn_b2"][e], P), 2, ACT.Gelu_apprx_tanh)
        store_nodes(nc, x, out)


def padded_kronecker(weight, bias):
    rows = np.zeros((4 * KCH, D), np.float32)
    products = rows[:ND * ND].reshape(ND, ND, D)
    products[:KD, :KD] = weight.reshape(KD, KD, D)
    products[KD, KD] = bias
    return rows


def laid_out(**a):
    src, dst = (np.concatenate([np.asarray(a[n]), np.full(EP - E, NP - 1, np.int32)]) for n in ("src", "dst"))
    return {
        "x": np.concatenate([np.asarray(a["x"]), np.zeros((NP - N, D), np.float32)]),
        "src": src, "dst": dst,
        "weight": np.concatenate([np.asarray(a["edge_weight"]), np.zeros(EP - E, np.float32)]),
        "fc_w": np.asarray(a["L0_gnn_fc_w"]), "fc_b": np.asarray(a["L0_gnn_fc_b"]),
        "ch_w": np.asarray(a["L0_gnn_ch_w"]), "ch_b": np.asarray(a["L0_gnn_ch_b"]),
        "mlp_wT": np.ascontiguousarray(np.asarray(a["L0_gnn_mlp_w"]).T), "mlp_b": np.asarray(a["L0_gnn_mlp_b"]),
        **{n: np.asarray(a["L0_ffn_" + n]) for n in ("gamma", "beta", "Wr", "br", "W1", "b1", "W2", "b2")},
        **{n: np.asarray(a["L1_gnn_" + n]) for n in (
            "Wp", "bp", "gp", "betap", "gk", "betak", "We", "be", "Wn", "bn", "b_ih", "b_hh",
            "g_ln", "beta_ln", "Wc", "bc", "gc", "betac")},
        "Wk": padded_kronecker(np.asarray(a["L1_gnn_Wk"]), np.asarray(a["L1_gnn_bk"])),
        "W_ihT": np.ascontiguousarray(np.asarray(a["L1_gnn_W_ih"]).T),
        "W_hhT": np.ascontiguousarray(np.asarray(a["L1_gnn_W_hh"]).T),
        "wr": np.asarray(a["L1_ffn_wr"]), "ffn_br": np.asarray(a["L1_ffn_br"]),
        "w1": np.asarray(a["L1_ffn_w1"]), "ffn_b1": np.asarray(a["L1_ffn_b1"]),
        "w2": np.asarray(a["L1_ffn_w2"]),
        "ffn_b2": np.stack([np.asarray(a["L1_ffn_b2"]), np.zeros(D, np.float32)]),
    }


def kernel(**inputs):
    from concourse import bacc
    from concourse.bass_utils import run_bass_kernel_spmd

    nc = bacc.Bacc("TRN2", target_bir_lowering=False, num_devices=1)
    arrays = laid_out(**inputs)
    t = {n: nc.dram_tensor(n, a.shape, mybir.dt.from_np(a.dtype), kind="ExternalInput").ap()
         for n, a in arrays.items()}
    out = nc.dram_tensor("out", (N, D), F32, kind="ExternalOutput").ap()
    program(nc, t, out)
    return run_bass_kernel_spmd(nc, [arrays], core_ids=[0]).results[0]["out"]
```
